# Optimizing a Trainium2 kernel written in Bass

```python
import numpy as np
import jax
import jax.numpy as jnp

def _softmax(x, axis=-1):
    return jax.nn.softmax(x, axis=axis)
def _gelu(x):
    return jax.nn.gelu(x, approximate=True)
def _silu(x):
    return jax.nn.silu(x)
def _sigmoid(x):
    return jax.nn.sigmoid(x)
def _layernorm(x, axis=-1, eps=1e-5):
    m = jnp.mean(x, axis=axis, keepdims=True)
    v = jnp.var(x, axis=axis, keepdims=True)
    return (x - m) / jnp.sqrt(v + eps)
def _scatter_add(tgt, idx, src, axis=0):
    return tgt.at[idx].add(src)
def _segment_sum(src, seg, n):
    return jax.ops.segment_sum(src, seg, n)

kernel_name = 'mk_adj_resnorm_d4_adj_256_762a5c'

def setup_inputs(seed: int = 0):
    np.random.seed(seed)
    _w = jnp.asarray
    def _rec_inputs():
        import jax
        import jax.numpy as jnp
        _gk = jax.random.key(seed)
        x = -0.000929 + 1 * jax.random.normal(jax.random.fold_in(_gk, 1), (2708, 256), jnp.float32)
        _w = (1.0 + jnp.arange(2708, dtype=jnp.float32)) ** -0.5
        _w = _w / _w.mean()
        _pij = jnp.clip(0.00590842 * _w[:, None] * _w[None, :], 0.0, 1.0)
        _a = jax.random.uniform(jax.random.fold_in(_gk, 2), (2708, 2708)) < _pij
        _a = jnp.logical_or(_a, jnp.eye(2708, dtype=bool))
        _af = _a.astype(jnp.float32)
        _af = _af * jax.random.uniform(jax.random.fold_in(_gk, 3), (2708, 2708), jnp.float32, 0.05, 1)
        adj = _af
        return x, adj
    x, adj = _rec_inputs()
    def _L0_gnn_setup():
        import jax, jax.numpy as jnp
        import numpy as np
        N, H, HEADS = (4096, 256, 3)
        ALPHA = 0.2
        NEG_INF = -9000000000000000.0

        def _sign_adj(key, n, density):
            k1, k2 = jax.random.split(key)
            mask = jax.random.uniform(k1, (n, n)) < density
            sign = jnp.where(jax.random.uniform(k2, (n, n)) < 0.5, -1.0, 1.0)
            adj = jnp.where(mask, sign, 0.0).astype(jnp.float32)
            idx = jnp.arange(n)
            return adj.at[idx, idx].set(1.0)

        def _gru_cell(x, hstate, Wih, Whh, bih, bhh):
            gi = x @ Wih.T + bih
            gh = hstate @ Whh.T + bhh
            ir, iz, inn = jnp.split(gi, 3, axis=1)
            hr, hz, hn = jnp.split(gh, 3, axis=1)
            r = jax.nn.sigmoid(ir + hr)
            z = jax.nn.sigmoid(iz + hz)
            n = jnp.tanh(inn + r * hn)
            return (1.0 - z) * n + z * hstate

        def _gat_head(h, node_adj, edge_adj, W, a):
            hW = h @ W
            hp = (node_adj > 0).astype(hW.dtype) @ hW
            hm = (node_adj < 0).astype(hW.dtype) @ hW
            e_plus = jax.nn.leaky_relu(jnp.concatenate([hp, hm], axis=1) @ a, ALPHA)[:, 0]
            e_minus = jax.nn.leaky_relu(jnp.concatenate([hm, hp], axis=1) @ a, ALPHA)[:, 0]
            att = jnp.where(edge_adj > 0, e_plus[None, :], NEG_INF)
            att = jnp.where(edge_adj < 0, e_minus[None, :], att)
            att = jax.nn.softmax(att, axis=1)
            return att * edge_adj @ hW
        key = jax.random.key(seed)
        ks = jax.random.split(key, 16)
        std = 0.01
        gain = 1.414
        return {'h': jax.random.normal(ks[0], (N, H), jnp.float32), 'node_adj': _sign_adj(ks[1], N, 0.005), 'edge_adj': _sign_adj(ks[2], N, 0.005), 'gat_W': jax.random.normal(ks[3], (HEADS, H, H), jnp.float32) * (gain / np.sqrt(H, dtype=np.float32)), 'gat_a': jax.random.normal(ks[4], (HEADS, 2 * H, 1), jnp.float32) * 0.1, 'edge_Wih': jax.random.normal(ks[5], (3 * H, H), jnp.float32) * std, 'edge_Whh': jax.random.normal(ks[6], (3 * H, H), jnp.float32) * std, 'edge_bih': jnp.zeros((3 * H,), jnp.float32), 'edge_bhh': jnp.zeros((3 * H,), jnp.float32), 'node_Wih': jax.random.normal(ks[7], (3 * H, H), jnp.float32) * std, 'node_Whh': jax.random.normal(ks[8], (3 * H, H), jnp.float32) * std, 'node_bih': jnp.zeros((3 * H,), jnp.float32), 'node_bhh': jnp.zeros((3 * H,), jnp.float32)}
    _L0_gnn_all = _L0_gnn_setup()
    _L0_gnn_in = {k: v for k, v in _L0_gnn_all.items() if k in ('gat_W', 'gat_a', 'edge_Wih', 'edge_Whh', 'edge_bih', 'edge_bhh', 'node_Wih', 'node_Whh', 'node_bih', 'node_bhh', )}
    del _L0_gnn_all

    def _L1_gnn_setup():
        import jax, jax.numpy as jnp
        import numpy as np
        N = 8192
        F_IN = 256
        F_OUT = 256
        key = jax.random.key(seed)
        k1, k2, k3, k4 = jax.random.split(key, 4)
        x = jax.random.normal(k1, (N, F_IN), dtype=jnp.float32)
        adj = jax.random.uniform(k2, (N, N), dtype=jnp.float32)
        bound = 1.0 / np.sqrt(F_IN)
        W = jax.random.uniform(k3, (F_OUT, F_IN), minval=-bound, maxval=bound, dtype=jnp.float32)
        b = jax.random.uniform(k4, (F_OUT,), minval=-bound, maxval=bound, dtype=jnp.float32)
        return {'x': x, 'adj': adj, 'W': W, 'b': b}
    _L1_gnn_all = _L1_gnn_setup()
    _L1_gnn_in = {k: v for k, v in _L1_gnn_all.items() if k in ('W', 'b', )}
    del _L1_gnn_all

    def _L2_gnn_setup():
        import jax, jax.numpy as jnp
        import numpy as np
        N = 4096
        IN_F = 256
        OUT_F = 128
        H = 2
        ALPHA = 0.2
        NEG_INF = -9000000000000000.0
        key = jax.random.key(seed)
        k_x, k_adj, k_w, k_a = jax.random.split(key, 4)
        x = jax.random.normal(k_x, (N, IN_F), dtype=jnp.float32)
        adj = (jax.random.uniform(k_adj, (N, N)) < 0.005).astype(jnp.float32)
        gain = 1.414
        bound_w = gain * np.sqrt(6.0 / (IN_F + OUT_F))
        W = jax.random.uniform(k_w, (H, IN_F, OUT_F), minval=-bound_w, maxval=bound_w, dtype=jnp.float32)
        bound_a = gain * np.sqrt(6.0 / (2 * OUT_F + 1))
        a = jax.random.uniform(k_a, (H, 2 * OUT_F, 1), minval=-bound_a, maxval=bound_a, dtype=jnp.float32)
        return {'x': x, 'adj': adj, 'W': W, 'a': a}
    _L2_gnn_all = _L2_gnn_setup()
    _L2_gnn_in = {k: v for k, v in _L2_gnn_all.items() if k in ('W', 'a', )}
    del _L2_gnn_all

    def _L3_gnn_setup():
        import jax, jax.numpy as jnp
        import numpy as np
        N = 4096
        D_IN = 256
        HEADS = 4
        C = 64
        NEG_SLOPE = 0.2
        MASK_VAL = -1000000000.0
        key = jax.random.key(seed)
        ks = jax.random.split(key, 6)
        x = jax.random.normal(ks[0], (N, D_IN), dtype=jnp.float32)
        adj = jax.random.uniform(ks[1], (N, N), dtype=jnp.float32)
        W = jax.random.normal(ks[2], (D_IN, HEADS * C), dtype=jnp.float32) * 0.05
        a_src = jax.random.normal(ks[3], (HEADS, C), dtype=jnp.float32) * 0.05
        a_dst = jax.random.normal(ks[4], (HEADS, C), dtype=jnp.float32) * 0.05
        bias = jnp.zeros((HEADS * C,), dtype=jnp.float32)
        return {'x': x, 'adj': adj, 'W': W, 'a_src': a_src, 'a_dst': a_dst, 'bias': bias}
    _L3_gnn_all = _L3_gnn_setup()
    _L3_gnn_in = {k: v for k, v in _L3_gnn_all.items() if k in ('W', 'a_src', 'a_dst', 'bias', )}
    del _L3_gnn_all

    return {
        "x": x,
        "adj": adj,
        "L0_gnn_gat_W": _L0_gnn_in["gat_W"],
        "L0_gnn_gat_a": _L0_gnn_in["gat_a"],
        "L0_gnn_edge_Wih": _L0_gnn_in["edge_Wih"],
        "L0_gnn_edge_Whh": _L0_gnn_in["edge_Whh"],
        "L0_gnn_edge_bih": _L0_gnn_in["edge_bih"],
        "L0_gnn_edge_bhh": _L0_gnn_in["edge_bhh"],
        "L0_gnn_node_Wih": _L0_gnn_in["node_Wih"],
        "L0_gnn_node_Whh": _L0_gnn_in["node_Whh"],
        "L0_gnn_node_bih": _L0_gnn_in["node_bih"],
        "L0_gnn_node_bhh": _L0_gnn_in["node_bhh"],
        "L1_gnn_W": _L1_gnn_in["W"],
        "L1_gnn_b": _L1_gnn_in["b"],
        "L2_gnn_W": _L2_gnn_in["W"],
        "L2_gnn_a": _L2_gnn_in["a"],
        "L3_gnn_W": _L3_gnn_in["W"],
        "L3_gnn_a_src": _L3_gnn_in["a_src"],
        "L3_gnn_a_dst": _L3_gnn_in["a_dst"],
        "L3_gnn_bias": _L3_gnn_in["bias"],
    }

def reference(x, adj, L0_gnn_gat_W, L0_gnn_gat_a, L0_gnn_edge_Wih, L0_gnn_edge_Whh, L0_gnn_edge_bih, L0_gnn_edge_bhh, L0_gnn_node_Wih, L0_gnn_node_Whh, L0_gnn_node_bih, L0_gnn_node_bhh, L1_gnn_W, L1_gnn_b, L2_gnn_W, L2_gnn_a, L3_gnn_W, L3_gnn_a_src, L3_gnn_a_dst, L3_gnn_bias):
    import jax
    import jax.numpy as jnp
    def _L0_gnn_ref(h, node_adj, edge_adj, gat_W, gat_a, edge_Wih, edge_Whh, edge_bih, edge_bhh, node_Wih, node_Whh, node_bih, node_bhh):
        import jax, jax.numpy as jnp
        import numpy as np
        N, H, HEADS = (4096, 256, 3)
        ALPHA = 0.2
        NEG_INF = -9000000000000000.0

        def _sign_adj(key, n, density):
            k1, k2 = jax.random.split(key)
            mask = jax.random.uniform(k1, (n, n)) < density
            sign = jnp.where(jax.random.uniform(k2, (n, n)) < 0.5, -1.0, 1.0)
            adj = jnp.where(mask, sign, 0.0).astype(jnp.float32)
            idx = jnp.arange(n)
            return adj.at[idx, idx].set(1.0)

        def _gru_cell(x, hstate, Wih, Whh, bih, bhh):
            gi = x @ Wih.T + bih
            gh = hstate @ Whh.T + bhh
            ir, iz, inn = jnp.split(gi, 3, axis=1)
            hr, hz, hn = jnp.split(gh, 3, axis=1)
            r = jax.nn.sigmoid(ir + hr)
            z = jax.nn.sigmoid(iz + hz)
            n = jnp.tanh(inn + r * hn)
            return (1.0 - z) * n + z * hstate

        def _gat_head(h, node_adj, edge_adj, W, a):
            hW = h @ W
            hp = (node_adj > 0).astype(hW.dtype) @ hW
            hm = (node_adj < 0).astype(hW.dtype) @ hW
            e_plus = jax.nn.leaky_relu(jnp.concatenate([hp, hm], axis=1) @ a, ALPHA)[:, 0]
            e_minus = jax.nn.leaky_relu(jnp.concatenate([hm, hp], axis=1) @ a, ALPHA)[:, 0]
            att = jnp.where(edge_adj > 0, e_plus[None, :], NEG_INF)
            att = jnp.where(edge_adj < 0, e_minus[None, :], att)
            att = jax.nn.softmax(att, axis=1)
            return att * edge_adj @ hW
        dn = jnp.diag(node_adj)
        de = jnp.diag(edge_adj)
        idx = jnp.arange(node_adj.shape[0])
        node_adj_norm = node_adj.at[idx, idx].add(-dn)
        edge_adj_norm = edge_adj.at[idx, idx].add(-de)
        node_support = node_adj_norm @ h
        edge_output = _gru_cell(node_support, h, edge_Wih, edge_Whh, edge_bih, edge_bhh)
        edge_support = _gat_head(h, node_adj_norm, edge_adj_norm, gat_W[0], gat_a[0])
        for i in range(1, HEADS):
            edge_support = edge_support + _gat_head(h, node_adj_norm, edge_adj_norm, gat_W[i], gat_a[i])
        edge_support = edge_support / HEADS
        node_output = _gru_cell(edge_support, h, node_Wih, node_Whh, node_bih, node_bhh)
        return de[:, None] * edge_output + dn[:, None] * node_output

    def _L1_gnn_ref(x, adj, W, b):
        import jax, jax.numpy as jnp
        import numpy as np
        N = 8192
        F_IN = 256
        F_OUT = 256
        rowsum = adj.sum(axis=1)
        d_inv_sqrt = jnp.power(rowsum, -0.5)
        d_inv_sqrt = jnp.where(jnp.isinf(d_inv_sqrt), 0.0, d_inv_sqrt)
        adj_norm = d_inv_sqrt[:, None] * adj * d_inv_sqrt[None, :]
        h = adj_norm @ x
        return h @ W.T + b

    def _L2_gnn_ref(x, adj, W, a):
        import jax, jax.numpy as jnp
        import numpy as np
        N = 4096
        IN_F = 256
        OUT_F = 128
        H = 2
        ALPHA = 0.2
        NEG_INF = -9000000000000000.0
        n = x.shape[0]
        h, _, f_out = W.shape
        adj = adj + jnp.eye(n, dtype=adj.dtype)
        xt = jnp.einsum('nf,hfo->hno', x, W)
        a1 = a[:, :f_out, 0]
        a2 = a[:, f_out:, 0]
        e1 = jnp.einsum('hno,ho->hn', xt, a1)
        e2 = jnp.einsum('hno,ho->hn', xt, a2)
        scores = jax.nn.leaky_relu(e1[:, :, None] + e2[:, None, :], negative_slope=ALPHA)
        scores = jnp.where(adj > 0, scores, jnp.asarray(NEG_INF, scores.dtype))
        attn = jax.nn.softmax(scores, axis=-1)
        h_prime = jnp.einsum('hij,hjo->hio', attn, xt)
        return jax.nn.elu(h_prime.reshape(n, h * f_out))

    def _L3_gnn_ref(x, adj, W, a_src, a_dst, bias):
        import jax, jax.numpy as jnp
        import numpy as np
        N = 4096
        D_IN = 256
        HEADS = 4
        C = 64
        NEG_SLOPE = 0.2
        MASK_VAL = -1000000000.0
        n = x.shape[0]
        h = (x @ W).reshape(n, HEADS, C)
        s_src = jnp.einsum('nhc,hc->nh', h, a_src)
        s_dst = jnp.einsum('nhc,hc->nh', h, a_dst)
        e = jax.nn.leaky_relu(s_src[:, None, :] + s_dst[None, :, :], NEG_SLOPE)
        e = jnp.where((adj > 0.5)[:, :, None], e, MASK_VAL)
        alpha = jax.nn.softmax(e, axis=0)
        out = jnp.einsum('ijh,ihc->jhc', alpha, h).reshape(n, HEADS * C) + bias
        return out

    x = _layernorm(x + _L0_gnn_ref(x, adj, adj, L0_gnn_gat_W, L0_gnn_gat_a, L0_gnn_edge_Wih, L0_gnn_edge_Whh, L0_gnn_edge_bih, L0_gnn_edge_bhh, L0_gnn_node_Wih, L0_gnn_node_Whh, L0_gnn_node_bih, L0_gnn_node_bhh), axis=-1)
    x = _layernorm(x + _L1_gnn_ref(x, adj, L1_gnn_W, L1_gnn_b), axis=-1)
    x = _layernorm(x + _L2_gnn_ref(x, adj, L2_gnn_W, L2_gnn_a), axis=-1)
    x = _layernorm(x + _L3_gnn_ref(x, adj, L3_gnn_W, L3_gnn_a_src, L3_gnn_a_dst, L3_gnn_bias), axis=-1)
    return x


_drawn_inputs = setup_inputs


def setup_inputs(seed=0):
    import zlib

    import numpy as np

    out = dict(_drawn_inputs(seed))
    spreads = {'L0_gnn_edge_bih': (0.0, 0.1),
     'L0_gnn_edge_bhh': (0.0, 0.438),
     'L0_gnn_node_bih': (0.0, 0.291),
     'L0_gnn_node_bhh': (0.0, 0.414),
     'L3_gnn_bias': (0.0, 0.1)}
    factors = {'L0_gnn_gat_W': 3.381,
     'L0_gnn_gat_a': 3.684,
     'L0_gnn_node_Wih': 3.345,
     'L3_gnn_a_dst': 2.825,
     'L0_gnn_node_Whh': 2.717}
    for name, (base, spread) in spreads.items():
        noise = np.random.default_rng([zlib.crc32(name.encode()), seed]).standard_normal(out[name].shape)
        drawn = base * np.exp(spread * noise) if base else spread * noise
        out[name] = jnp.asarray(drawn.astype(out[name].dtype))
    for name, factor in factors.items():
        out[name] = (out[name] * factor).astype(out[name].dtype)
    return out
```

```python
from contextlib import ExitStack, contextmanager

import numpy as np

import concourse.bass as bass
from concourse import mybir

F32 = mybir.dt.float32
BF16 = mybir.dt.bfloat16
ALU = mybir.AluOpType
ACT = mybir.ActivationFunctionType
AX_X = mybir.AxisListType.X
RMAX = bass.bass_isa.ReduceOp.max

P = 128
N = 2708
D = 256
KD = D // P
T = -(-N // P)
TAIL = N - (T - 1) * P
RPC = 4
W = RPC * P
CH = -(-T // RPC)
WL = N - (CH - 1) * W
QUADS = T // 4
H0, H2, H3 = 3, 2, 4
C2, C3 = D // H2, D // H3
NEG = -1e30
EPS = 1e-5
SLOPE = 0.2


class Unit:

    def __init__(self, c, last, n, tile, slot, k, diag, end):
        self.c, self.last, self.n, self.tile, self.slot, self.k, self.diag, self.end = c, last, n, tile, slot, k, diag, end
        self.q = slot % 2
        self.kp = TAIL if (isinstance(tile, int) and tile == T - 1) else P
        self.w = WL if last else W
        self.rows = [P] * RPC if not last else [P, TAIL]
        uses = 6 if slot < 2 else 5
        per = 32 if last else 16
        self.loaded = 16 * uses * c + per * (k + 1)
        self.loaded1 = 16 * (uses * c + k + 1)
        self.first = last or (isinstance(k, int) and k == 0)

    def slot_free(self):
        return self.n + 3 if (self.first and self.slot < 2) else self.n + 1


def sweep_chunks(eng, body):
    with eng.Fori(0, CH - 1) as c:
        body(c, False)
    body(CH - 1, True)


def sweep_units(eng, c, last, step):
    base = c * T
    if not last:
        for u in range(4):
            step(Unit(c, last, base + u, c * 4 + u, u, 0, u, False))
        with eng.Fori(1, QUADS) as k:
            for u in range(4):
                step(Unit(c, last, base + k * 4 + u, ((c + k) % QUADS) * 4 + u, u, k, None, False))
    else:
        with eng.Fori(0, QUADS) as k:
            for u in range(4):
                step(Unit(c, last, base + k * 4 + u, k * 4 + u, u, k, None, False))
    for u in range(2):
        step(Unit(c, last, base + 4 * QUADS + u, 4 * QUADS + u, u, QUADS, u if last else None, u == 1))


def sweep_ahead(eng, c, last, front, step):
    def run(units):
        front(units[0])
        for i, u in enumerate(units):
            if i + 1 < len(units):
                front(units[i + 1])
            step(u)

    base = c * T
    if not last:
        run([Unit(c, last, base + v, c * 4 + v, v, 0, v, False) for v in range(4)])
        with eng.Fori(1, QUADS) as k:
            run([Unit(c, last, base + k * 4 + v, ((c + k) % QUADS) * 4 + v, v, k, None, False) for v in range(4)])
    else:
        with eng.Fori(0, QUADS) as k:
            run([Unit(c, last, base + k * 4 + v, k * 4 + v, v, k, None, False) for v in range(4)])
    run([Unit(c, last, base + 4 * QUADS + v, 4 * QUADS + v, v, QUADS, v if last else None, v == 1) for v in range(2)])


def tile_pairs(eng, step, links=None, chain=None):
    with eng.Fori(0, T // 2 - 1) as g:
        with (chain.loop(g, T // 2 - 1, 2 * links) if chain else ExitStack()):
            for q in range(2):
                step(g * 2 + q, q, P)
    for q in range(2):
        ins = step(T - 2 + q, q, P if q == 0 else TAIL)
    return ins


class Chain:

    def __init__(self, eng, sem):
        self.eng, self.sem, self.base, self.local = eng, sem, 0, 0

    def __call__(self, ins):
        ins.then_inc(self.sem, 1)
        self.local += 1
        self.eng.wait_ge(self.sem, self.base + self.local)

    @contextmanager
    def loop(self, turn, turns, links):
        before = self.base + self.local
        self.base, self.local = before + turn * links, 0
        yield
        assert self.local == links, (self.local, links)
        self.base, self.local = before + turns * links, 0


FULL = ((P, slice(0, T - 1)), (TAIL, slice(T - 1, T)))


def build(nc, x, adj, gat_W, gat_a, e_Wih, e_Whh, e_bih, e_bhh, n_Wih, n_Whh, n_bih, n_bhh,
          W1, b1, W2, a2, W3, a_src, a_dst, b3, out):
    V, S, G, PE = nc.vector, nc.scalar, nc.gpsimd, nc.tensor
    e_rows = nc.dram_tensor("e_rows", (H0, T * P), F32).ap()
    m_rows = nc.dram_tensor("m_rows", (H0, T * P), F32).ap()
    r2_rows = nc.dram_tensor("r2_rows", (H2, T * P), F32).ap()
    r3_rows = nc.dram_tensor("r3_rows", (H3, T * P), F32).ap()

    heads2 = nc.dram_tensor("heads2", (H2 * N, C2), F32).ap()

    with ExitStack() as ctx:
        ARENA = 53000
        arena = ctx.enter_context(nc.sbuf_tensor("arena", [P, ARENA], F32))
        psum = ctx.enter_context(nc.psum_tensor("banks", [P, 8, 512], F32))
        top = [0]

        def sb(*shape, dt=F32):
            n = int(np.prod(shape))
            words = n if dt == F32 else (n + 1) // 2
            a = arena[:, top[0]:top[0] + words]
            top[0] += words + words % 2
            assert top[0] <= ARENA, top[0]
            if dt != F32:
                a = a.bitcast(dt)
            if len(shape) > 1:
                names = "abcd"[:len(shape)]
                a = a.rearrange(f"p ({' '.join(names)}) -> p {' '.join(names)}", **dict(zip(names, shape)))
            return a

        def sem(name):
            return ctx.enter_context(nc.semaphore(name))

        ident = sb(P)
        noteye = sb(P)
        ones = sb(P)
        zrow = sb(W, dt=BF16)
        xnat = sb(T, D)
        dn = sb(T)
        rowsum = sb(T)
        mv = sb(T, 2)
        rstd = sb(T)
        bnst = sb(T, 6)
        mrow = sb(2)
        wcat0 = sb(KD, H0 * D + 2 * H0)
        wcat2 = sb(KD, D + 2 * H2)
        wcat3 = sb(KD, D + 2 * H3)
        w1T = sb(KD, D)
        b1_bc = sb(D)
        b3_bc = sb(D)
        xs = sb(2, D)
        xT = sb(2, KD, P)
        rows_s = sb(P)
        smalls = sb(8, T * H3)
        sum_bc = sb(D)
        part = sb(D)
        cpart = sb(H3)
        cmax = sb(H3)
        stage_base = top[0]

        a0_bc = sb(H0, 2, D)
        a2_bc = sb(H2, 2, C2)
        a3_bc = sb(2, H3, C3)
        prod = sb(D * H0)
        w1n = sb(KD, D)
        top[0] = stage_base
        hW = sb(T, H0 * D + 2 * H0)
        ns = sb(T, D)
        ub = sb(T, 3, 3 * H0, dt=BF16)
        E18 = sb(T, 3, 2 * H0)
        e6 = sb(2 * H0, T)
        negm = sb(H0, T)
        den = sb(H0, T)
        ur = sb(T, 2 * H0)
        l0_base = top[0]
        blk = sb(4, RPC, P)
        AT = sb(2, W)
        Mp = sb(2, W, dt=BF16)
        Mm = sb(2, W, dt=BF16)
        top[0] = l0_base
        e_bc = sb(H0, N)
        arow = sb(2, N)
        mbias = sb(N, dt=BF16)
        srow = xnat.rearrange("p t d -> p (t d)")[:, 0:2 * N].rearrange("p (s n) -> p s n", s=2)
        top[0] = l0_base
        sb(4, RPC, P)
        m_bc = sb(H0, W)
        E = sb(2, H0, W)
        PA = sb(2, H0, W)
        es = sb(T, D)
        top[0] = stage_base
        g_wT = sb(4, KD, 3 * D)
        g_bias = sb(4, 3 * D)
        g_wn = sb(4, 6, D)
        assert top[0] <= stage_base + T * (H0 * D + 2 * H0)
        top[0] = stage_base + T * (H0 * D + 2 * H0)
        sb(T, D)
        top[0] = l0_base
        g_brz = sb(2, 2 * D)
        g_bnh = sb(2, 2 * D)
        st = sb(2, 3, D)
        sT = sb(2, 3, KD, P)
        g_rz = sb(2 * D)
        g_nh = sb(2 * D)
        g_th = sb(2 * D)
        g_q = sb(D)
        g_t = sb(D)
        g_n = sb(D)
        g_d = sb(D)
        g_e = sb(D)
        g_out = sb(2, D)
        assert top[0] <= l0_base + 4 * RPC * P + H0 * W + 4 * H0 * W, top[0]
        top[0] = stage_base
        xd = sb(T, D)
        raw1 = sb(T, D)
        proj = sb(T, D + 2 * H3)
        blk2 = sb(4, RPC, P)
        msk = sb(2, W, dt=BF16)
        stage_w = sb(2, H3 * (C3 + 1))
        S2 = sb(H2, W)
        den2 = sb(T, H2)
        free_from = top[0]
        r_bc = sb(H3, N)
        Y = sb(2, H3, W)
        PM = sb(2, H3, W)
        end_of_3 = top[0]
        top[0] = stage_base
        rawT2 = sb(H2, N)
        top[0] = stage_base
        rawT3 = sb(H3, N)
        assert top[0] <= stage_base + 2 * T * D
        top[0] = free_from
        AT2 = sb(2, W)
        top[0] = free_from
        tmp = sb(T, D)
        tmp2 = sb(T, D)
        assert top[0] <= end_of_3

        def bank(i, n=1):
            return psum[:, i:i + n, :].rearrange("p b n -> p (b n)")

        psT = [bank(6), bank(7)]

        waits_seen = sem("waits_seen")
        loaded, x_again = sem("loaded"), sem("x_again")
        const_ok = sem("const_ok")
        stage_done = sem("stage_done")
        dve_link, act_link, pool_link = sem("dve_link"), sem("act_link"), sem("pool_link")
        w1T_ok = sem("w1T_ok")
        projs = [[sem(f"l{l}_{s}") for s in ("staged", "xt_ps", "xt_ok", "proj_ps", "proj_ok")] for l in (0, 2, 3)]
        rows = {k: [None] + [sem(f"{k}_{s}") for s in ("ps", "sb", "dram", "bc")] for k in ("e", "m", "r2", "r3")}
        steps = dict(A="transposed diag_ok at_ok mask_ok", C="transposed diag_ok y_ok p_ok", L1="transposed at_ok",
                     L2="transposed diag_ok mask_ok y_ok p_ok", L3="mask_ok y_ok p_ok")
        sw = {k: dict(blk_in=[sem(f"{k}_blk_in{i}") for i in range(4)],
                      **{s: sem(f"{k}_{s}") for s in (names + " mm_done acc_free").split()})
              for k, names in steps.items()}
        b_in = [sem(f"b_in{i}") for i in range(2)]
        b_diag, b_rowfree, b_s, b_negm, b_exp = (sem(f"b_{s}") for s in ("diag", "rowfree", "s", "negm", "exp"))
        b_sum = sem("b_sum")
        mbc_in, c_arg = sem("mbc_in"), sem("c_arg")
        g_in, g_wps, g_wok = sem("g_in"), sem("g_wps"), sem("g_wok")
        g_staged, g_tps, g_tok, g_ready, g_pre, g_thok, g_tok2, g_nok = (
            sem(f"g_{s}") for s in ("staged", "tps", "tok", "ready", "pre", "thok", "tok2", "nok"))
        ln_var = [sem(f"ln_var{i}") for i in range(4)]
        ln_std = [sem(f"ln_std{i}") for i in range(4)]
        deg_in, deg_out = sem("deg_in"), sem("deg_out")
        h1_st, h1_ps, h1_ok, h1_mm, h1_done = (sem(f"h1_{s}") for s in ("st", "ps", "ok", "mm", "done"))
        cm_in = [sem(f"cm_in{i}") for i in range(2)]
        cm_ok = [sem(f"cm_ok{i}") for i in range(2)]
        fg_in = [sem(f"fg_in{i}") for i in range(2)]
        fg_ok = [sem(f"fg_ok{i}") for i in range(2)]
        neg_ok, den_zero = sem("neg_ok"), sem("den_zero")
        elu_in, elu_ok = sem("elu_in"), sem("elu_ok")
        sx_in = [sem(f"sx_in{i}") for i in range(2)]
        sx_ok = [sem(f"sx_ok{i}") for i in range(2)]
        stored = sem("stored")
        den_dve, den_pool, den_out, den_ps = (sem(f"den_{s}") for s in ("dve", "pool", "out", "ps"))
        back_ps = [sem(f"back_ps{i}") for i in range(2)]
        back_ok = [sem(f"back_ok{i}") for i in range(2)]
        h2_made, h2_out, h2_back = sem("h2_made"), sem("h2_out"), sem("h2_back")

        barriers = {}

        def stage_end(eng, name):
            barriers[name] = barriers.get(name, 0) + 1
            eng.drain().then_inc(stage_done, 1)
            eng.wait_ge(stage_done, 5 * barriers[name])

        def settle(eng):
            eng.sem_inc(waits_seen, 1)

        def load(eng, dst, src, s):
            eng.dma_start(dst, src).then_inc(s, 16)

        def load_nodes(eng, dst, src, s):
            load(eng, dst[:, 0:T - 1, :], src[0:(T - 1) * P, :].rearrange("(t p) d -> p t d", p=P), s)
            load(eng, dst[0:TAIL, T - 1, :], src[(T - 1) * P:N, :], s)

        def tl(a, t, nr):
            if isinstance(t, int):
                return a[0:nr, t, :]
            return a[0:nr, bass.ds(t, 1), :].rearrange("p a d -> p (a d)")

        def col(a, h, t, nr):
            return a[0:nr, h, bass.ds(t, 1)]

        degs = rowsum

        def empty(c, last, acc, width, dst):
            if not last:
                return V.tensor_copy(dst[:, bass.ds(c * RPC, RPC), :], acc[:, 0:RPC * width].rearrange(
                    "p (r d) -> p r d", r=RPC))
            V.tensor_copy(dst[:, c * RPC, :], acc[:, 0:width])
            return V.tensor_copy(dst[0:TAIL, c * RPC + 1, :], acc[0:TAIL, width:2 * width])

        def sp_blocks(sp, k):
            s = sw[k]

            def chunk(c, last):
                def step(u):
                    sp.wait_ge(s["transposed"], u.slot_free())
                    col = bass.ds(u.tile * P, u.kp)
                    if not last:
                        load(sp, blk_of(k)[:, u.slot, :, 0:u.kp],
                             adj[bass.ds(c * W, W), col].rearrange("(r p) n -> p r n", p=P), s["blk_in"][u.slot])
                    else:
                        for r, nr in enumerate(u.rows):
                            load(sp, blk_of(k)[0:nr, u.slot, r, 0:u.kp], adj[c * W + r * P:c * W + r * P + nr, col],
                                 s["blk_in"][u.slot])
                sweep_units(sp, c, last, step)
            sweep_chunks(sp, chunk)

        def blk_of(k):
            return blk if k in ("A", "C") else blk2

        def sp_rows(sp, k, dram, heads, bc):
            sp.wait_ge(rows[k][2], 1)
            load(sp, dram.rearrange("h (t p) -> (h t) p", p=P), rows_s[0:heads * T, :], rows[k][3])
            sp.wait_ge(rows[k][3], 16)
            if bc is not None:
                for h in range(heads):
                    load(sp, bc[:, h, :], dram[h:h + 1, 0:N].partition_broadcast(P).rearrange("p a n -> p (a n)"),
                         rows[k][4])

        block = ctx.enter_context(nc.Block())

        @block.sync
        def _(sp):
            load_nodes(sp, xnat, x, loaded)
            for kk in range(KD):
                f = slice(kk * P, (kk + 1) * P)
                load(sp, wcat0[:, kk, 0:H0 * D].rearrange("p (h f) -> p h f", h=H0),
                     gat_W[:, f, :].rearrange("h k f -> k h f"), loaded)
                load(sp, wcat2[:, kk, 0:D].rearrange("p (h f) -> p h f", h=H2), W2[:, f, :].rearrange("h k f -> k h f"),
                     loaded)
                load(sp, wcat3[:, kk, 0:D], W3[f, :], loaded)
                load(sp, w1n[:, kk, :], W1[f, :], loaded)
            flat = lambda a: a.partition_broadcast(P)
            load(sp, a0_bc.rearrange("p h s f -> p (h s f)"), flat(gat_a.rearrange("h f o -> (h f o)")), loaded)
            load(sp, a2_bc.rearrange("p h s f -> p (h s f)"), flat(a2.rearrange("h f o -> (h f o)")), loaded)
            load(sp, a3_bc[:, 0].rearrange("p h f -> p (h f)"), flat(a_src.rearrange("h f -> (h f)")), loaded)
            load(sp, a3_bc[:, 1].rearrange("p h f -> p (h f)"), flat(a_dst.rearrange("h f -> (h f)")), loaded)
            load(sp, b1_bc, flat(b1), loaded)
            load(sp, b3_bc, flat(b3), loaded)
            diag = bass.AP(adj.tensor, 0, [[N + 1, P], [P * (N + 1), T - 1], [1, 1]])
            sp.dma_start(dn[:, 0:T - 1].unsqueeze(2), diag, allow_slow_non_contiguous=True).then_inc(loaded, 16)
            diag_tail = bass.AP(adj.tensor, (T - 1) * P * (N + 1), [[N + 1, TAIL], [1, 1]])
            sp.dma_start(dn[0:TAIL, T - 1:T], diag_tail, allow_slow_non_contiguous=True).then_inc(loaded, 16)
            stage_end(sp, "sp")
            stage_end(sp, "sp")
            sp_blocks(sp, "A")
            stage_end(sp, "sp")
            sp_rows(sp, "e", e_rows, H0, e_bc)

            def row_tile(t, q, nr):
                sp.wait_ge(b_rowfree, t + 1)
                load(sp, arow[0:nr, q, :], adj[bass.ds(t * P, nr), :], b_in[q])
            tile_pairs(sp, row_tile)
            sp_rows(sp, "m", m_rows, H0, None)
            stage_end(sp, "sp")
            load_nodes(sp, xnat, x, x_again)
            s = sw["C"]

            def chunk(c, last):
                w = WL if last else W
                sp.wait_ge(c_arg, c * T + 1)
                for h in range(H0):
                    load(sp, m_bc[:, h, 0:w],
                         m_rows[h:h + 1, bass.ds(c * W, w)].partition_broadcast(P).rearrange("p a n -> p (a n)"), mbc_in)

                def step(u):
                    sp.wait_ge(s["transposed"], u.slot_free())
                    col = bass.ds(u.tile * P, u.kp)
                    if not last:
                        load(sp, blk[:, u.slot, :, 0:u.kp],
                             adj[bass.ds(c * W, W), col].rearrange("(r p) n -> p r n", p=P), s["blk_in"][u.slot])
                    else:
                        for r, nr in enumerate(u.rows):
                            load(sp, blk[0:nr, u.slot, r, 0:u.kp], adj[c * W + r * P:c * W + r * P + nr, col],
                                 s["blk_in"][u.slot])
                sweep_units(sp, c, last, step)
            sweep_chunks(sp, chunk)
            sp.wait_ge(x_again, 32)
            stage_end(sp, "sp")
            for i, (w, b) in enumerate(((e_Wih, e_bih), (e_Whh, e_bhh), (n_Wih, n_bih), (n_Whh, n_bhh))):
                load(sp, g_wn[:, i], w.rearrange("(g p) k -> p g k", p=P), g_in)
                load(sp, g_bias[:, i], b.partition_broadcast(P), g_in)
            stage_end(sp, "sp")
            stage_end(sp, "sp")
            sp_blocks(sp, "L1")
            stage_end(sp, "sp")
            stage_end(sp, "sp")
            stage_end(sp, "sp")
            sp_rows(sp, "r2", r2_rows, H2, r_bc[:, 0:H2])
            sp_blocks(sp, "L2")
            stage_end(sp, "sp")
            sp.wait_ge(h2_made, 1)
            for h in range(H2):
                f = slice(h * C2, (h + 1) * C2)
                load(sp, heads2[h * N:h * N + (T - 1) * P, :].rearrange("(t p) c -> p t c", p=P), tmp[:, 0:T - 1, f], h2_out)
                load(sp, heads2[h * N + (T - 1) * P:(h + 1) * N, :], tmp[0:TAIL, T - 1, f], h2_out)
            sp.wait_ge(h2_out, 16 * 2 * H2)
            load_nodes(sp, tmp, heads2.rearrange("(n g) c -> n (g c)", g=H2), h2_back)
            stage_end(sp, "sp")
            stage_end(sp, "sp")
            sp_rows(sp, "r3", r3_rows, H3, r_bc)
            s = sw["L3"]

            def chunk3(c, last):
                w = WL if last else W

                def step(u):
                    sp.wait_ge(s["mask_ok"], u.slot_free())
                    load(sp, blk2[0:u.kp, u.slot].rearrange("p r n -> p (r n)")[:, 0:w],
                         adj[bass.ds(u.tile * P, u.kp), bass.ds(c * W, w)], s["blk_in"][u.slot])
                sweep_units(sp, c, last, step)
            sweep_chunks(sp, chunk3)
            stage_end(sp, "sp")
            stage_end(sp, "sp")
            sp.dma_start(out[0:(T - 1) * P, :].rearrange("(t p) d -> p t d", p=P), xnat[:, 0:T - 1, :]).then_inc(stored, 16)
            sp.dma_start(out[(T - 1) * P:N, :], xnat[0:TAIL, T - 1, :]).then_inc(stored, 16)
            sp.wait_ge(stored, 32)

        def pool_diag(pool, k, what):
            s = sw[k]

            def chunk(c, last):
                nd = 4 if not last else 2

                def step(u):
                    if u.diag is None:
                        return
                    pool.wait_ge(s["blk_in"][u.slot], u.loaded)
                    r, nr = u.diag, u.rows[u.diag]
                    b = blk_of(k)[0:nr, u.slot, r, 0:nr]
                    mat = (noteye if what == ALU.mult else ident)[0:nr, 0:nr]
                    G.tensor_tensor(b, b, mat, what).then_inc(s["diag_ok"], 1)
                if not last:
                    for u in range(4):
                        step(Unit(c, last, c * T + u, c * 4 + u, u, 0, u, False))
                else:
                    for u in range(2):
                        step(Unit(c, last, c * T + 20 + u, 20 + u, u, QUADS, u, False))
            sweep_chunks(pool, chunk)

        @block.gpsimd
        def _(pool):
            link = Chain(pool, pool_link)
            G.memset(ones, 1.0)
            G.memset(zrow, 0.0)
            G.memset(ident, 0.0)
            link(G.memset(noteye, 1.0))
            G.affine_select(out=ident, in_=ident, compare_op=ALU.not_equal, fill=1.0, base=0, pattern=[[-1, P]],
                            channel_multiplier=1)
            G.affine_select(out=noteye, in_=noteye, compare_op=ALU.not_equal, fill=0.0, base=0, pattern=[[-1, P]],
                            channel_multiplier=1).then_inc(const_ok, 1)
            stage_end(pool, "pool")
            G.memset(e6, 0.0)
            G.memset(negm, 0.0)
            stage_end(pool, "pool")
            pool_diag(pool, "A", ALU.mult)
            stage_end(pool, "pool")

            def row_tile(t, q, nr):
                pool.wait_ge(b_in[q], 8 * (t - q) + 16)
                b = arow[0:nr, q, bass.ds(t * P, nr)]
                G.tensor_tensor(b, b, noteye[0:nr, 0:nr], ALU.mult).then_inc(b_diag, 1)
            tile_pairs(pool, row_tile)
            stage_end(pool, "pool")
            pool_diag(pool, "C", ALU.mult)
            stage_end(pool, "pool")

            def gate_tile(t, q, nr):
                pool.wait_ge(g_tps, t + 1)
                G.tensor_copy(st[0:nr, q, 0], tl(ns, t, nr))
                G.tensor_copy(st[0:nr, q, 1], tl(es, t, nr))
                G.tensor_copy(st[0:nr, q, 2], tl(xnat, t, nr)).then_inc(g_staged, 1)
            tile_pairs(pool, gate_tile)
            stage_end(pool, "pool")
            stage_end(pool, "pool")
            stage_end(pool, "pool")
            stage_end(pool, "pool")

            def maxima(i, heads):
                pool.wait_ge(cm_in[i], 1)
                G.partition_all_reduce(cmax[:, 0:heads], cpart[:, 0:heads], P, RMAX).then_inc(cm_ok[i], 1)
            G.memset(smalls.rearrange("p a b -> p (a b)"), 0.0)
            stage_end(pool, "pool")
            maxima(0, H2)
            s = sw["L2"]
            pool.sem_inc(den_pool, 2)

            def chunk2(c, last):
                def diagonal(u):
                    pool.wait_ge(s["blk_in"][u.slot], u.loaded)
                    nr = u.rows[u.diag]
                    b = blk2[0:nr, u.slot, u.diag, 0:nr]
                    G.tensor_tensor(b, b, ident[0:nr, 0:nr], ALU.add).then_inc(s["diag_ok"], 1)

                def step(u):
                    if last and u.diag is not None:
                        diagonal(u)
                    pool.wait_ge(den_pool, u.n + 2)
                    pool.wait_ge(s["p_ok"], 2 * H2 + u.n * H2 + 1)
                    G.tensor_tensor(S2[0:u.kp, 0, 0:u.w], S2[0:u.kp, 0, 0:u.w], PM[0:u.kp, u.q, 0, 0:u.w], ALU.add
                                    ).then_inc(den_pool, 1)
                if not last:
                    for v in range(4):
                        diagonal(Unit(c, last, c * T + v, c * 4 + v, v, 0, v, False))
                pool.wait_ge(den_ps, c + 1)
                settle(pool)
                G.memset(S2[:, 0, :], 0.0).then_inc(pool_link, 1)
                pool.wait_ge(pool_link, c + 2)
                settle(pool)
                sweep_units(pool, c, last, step)
            sweep_chunks(pool, chunk2)
            stage_end(pool, "pool")
            stage_end(pool, "pool")
            stage_end(pool, "pool")
            maxima(1, H3)
            s = sw["L3"]
            pool.sem_inc(s["mask_ok"], 4)

            def chunk3(c, last):
                w = WL if last else W

                def step(u):
                    pool.wait_ge(s["blk_in"][u.slot], u.loaded1)
                    pool.wait_ge(s["p_ok"], u.n * H3 + H3)
                    settle(pool)
                    G.tensor_scalar(msk[0:u.kp, u.q, 0:w], blk2[0:u.kp, u.slot].rearrange("p r n -> p (r n)")[:, 0:w],
                                    0.5, None, ALU.is_gt).then_inc(s["mask_ok"], 1)
                sweep_units(pool, c, last, step)
            sweep_chunks(pool, chunk3)
            stage_end(pool, "pool")
            stage_end(pool, "pool")

        def pe_project(pe, i, wcat, cols):
            staged, xt_ps, xt_ok, proj_ps, proj_ok = projs[i]
            pe.sem_inc(xt_ps, 2)

            def tile(t, q, nr):
                pe.wait_ge(staged, t + 1)
                for kk in range(KD):
                    last = PE.transpose(psT[q][:, kk * P:kk * P + nr], xs[0:nr, q, kk * P:(kk + 1) * P], ident[0:nr, 0:nr])
                last.then_inc(xt_ps, 1)
                pe.wait_ge(xt_ok, t + 1)
                pe.wait_ge(proj_ok, t + 1)
                for kk in range(KD):
                    for b, (lo, hi) in enumerate(splits(cols)):
                        last = PE.matmul(bank(2 * q + b)[0:nr, 0:hi - lo], xT[:, q, kk, 0:nr], wcat[:, kk, lo:hi],
                                         start=kk == 0, stop=kk == KD - 1)
                last.then_inc(proj_ps, 1)
            tile_pairs(pe, tile)

        def pe_back(pe, i, src, heads, m):
            for t in range(T):
                nr = P if t < T - 1 else TAIL
                if t >= 4:
                    pe.wait_ge(back_ok[i], t - 3)
                for h in range(heads):
                    ins = PE.transpose(bank(t % 4)[0:nr, h * m:(h + 1) * m], src[0:m, h, t * P:t * P + nr],
                                       ident[0:m, 0:m])
                ins.then_inc(back_ps[i], 1)

        def pe_sums(pe, i):
            pe.wait_ge(sx_in[i], 1)
            PE.matmul(bank(4)[:, 0:D], ones, part, start=True, stop=True).then_inc(sx_ok[i], 1)

        def splits(cols):
            return [(0, cols)] if cols <= 512 else [(0, 512), (512, cols)]

        def pe_rows(k, src, heads):
            PE.transpose(bank(5)[0:heads * T, 0:P], src, ident[:, :]).then_inc(rows[k][1], 1)

        def transposes(pe, k, u, c, last):
            s = sw[k]
            if u.diag is None or k == "L1":
                pe.wait_ge(s["blk_in"][u.slot], u.loaded)
            else:
                pe.wait_ge(s["diag_ok"], (c * 4 + u.diag + 1))
            for r, nr in enumerate(u.rows):
                ins = PE.transpose(psT[u.q][0:u.kp, r * P:r * P + nr], blk_of(k)[0:nr, u.slot, r, 0:u.kp],
                                   ident[0:nr, 0:nr])
            ins.then_inc(s["transposed"], 1)

        def pe_sweep(pe, k, nbanks, psT_free, products, tr=True):
            s = sw[k]
            if tr:
                pe.sem_inc(s["transposed"], 4)
            pe.sem_inc(s["mm_done"], 2)

            def chunk(c, last):
                pe.wait_ge(s["acc_free"], c + 1)
                for b in range(nbanks):
                    PE.matmul(bank(b), zrow[0:1, 0:P], zrow[0:1, :], start=True, stop=False)

                def front(u):
                    if tr:
                        psT_free(u)
                        transposes(pe, k, u, c, last)

                def step(u):
                    products(u)

                sweep_ahead(pe, c, last, front, step)
            sweep_chunks(pe, chunk)

        def accumulate(u, mms):
            for i, (o, b, l, r) in enumerate(mms):
                ins = PE.matmul(o, l, r, start=False, stop=False, skip_group_check=True)
            return ins

        def unit_done(u, ins, s, nbanks):
            if u.end:
                for b in range(nbanks):
                    ins = PE.matmul(bank(b), zrow[0:1, 0:P], zrow[0:1, :], start=False, stop=True)
            ins.then_inc(s["mm_done"], 1)

        @block.tensor
        def _(pe):
            pe.wait_ge(const_ok, 1)
            pe.wait_ge(loaded, 16 * (2 + 4 * KD + 8))
            for fo in range(KD):
                for kk in range(KD):
                    ins = PE.transpose(bank(4)[:, (kk * KD + fo) * P:(kk * KD + fo + 1) * P],
                                       w1n[:, fo, kk * P:(kk + 1) * P], ident)
            ins.then_inc(w1T_ok, 1)
            stage_end(pe, "pe")
            pe_project(pe, 0, wcat0, H0 * D + 2 * H0)
            stage_end(pe, "pe")
            s = sw["A"]

            def free_A(u):
                pe.wait_ge(s["at_ok"], u.n + 1)

            def products_A(u):
                rhs_x = xnat[0:u.kp, u.tile, :] if isinstance(u.tile, int) else \
                    xnat[0:u.kp, bass.ds(u.tile, 1), :].rearrange("p a d -> p (a d)")
                pe.wait_ge(s["at_ok"], u.n + 3)
                accumulate(u, [(bank(0, 2)[0:nr, r * D:(r + 1) * D], r // 2, AT[0:u.kp, u.q, r * P:r * P + nr], rhs_x)
                               for r, nr in enumerate(u.rows)])
                pe.wait_ge(s["mask_ok"], u.n + 1)
                mms = []
                for m, lo in ((Mp, 0), (Mm, H0)):
                    rhs_u = ub[0:u.kp, bass.ds(u.tile, 1), :, lo:lo + 2 * H0].rearrange("p a s h -> p (a s) h")
                    mms += [(bank(2)[0:nr, r * 18:(r + 1) * 18].rearrange("p (s h) -> p s h", s=3), 2,
                             m[0:u.kp, u.q, r * P:r * P + nr], rhs_u) for r, nr in enumerate(u.rows)]
                unit_done(u, accumulate(u, mms), s, 3)
            pe_sweep(pe, "A", 3, free_A, products_A)
            stage_end(pe, "pe")
            pe_rows("e", e6[:, 0:H0, :].rearrange("p h t -> p (h t)"), H0)
            pe.wait_ge(b_negm, T * H0)
            pe_rows("m", negm.rearrange("p h t -> p (h t)"), H0)
            stage_end(pe, "pe")
            s = sw["C"]

            def free_C(u):
                pe.wait_ge(s["p_ok"], u.n * H0 + H0)

            def products_C(u):
                for h in range(H0):
                    pe.wait_ge(s["p_ok"], 2 * H0 + u.n * H0 + h + 1)
                    rhs_h = hW[0:u.kp, bass.ds(u.tile, 1), h * D:(h + 1) * D].rearrange("p a d -> p (a d)")
                    mms = [(bank(0, 6)[0:nr, (r * H0 + h) * D:(r * H0 + h + 1) * D], (r * H0 + h) // 2,
                            PA[0:u.kp, u.q, h, r * P:r * P + nr], rhs_h) for r, nr in enumerate(u.rows)]
                    for o, b, l, rr in mms:
                        ins = PE.matmul(o, l, rr, start=False, stop=False, skip_group_check=True)
                unit_done(u, ins, s, 6)
            pe_sweep(pe, "C", 6, free_C, products_C)
            stage_end(pe, "pe")
            pe.wait_ge(g_in, 128)
            n = 0
            for i in range(4):
                for kk in range(KD):
                    for g0 in (0, 3):
                        if n >= 4:
                            pe.wait_ge(g_wok, n - 3)
                        for g in range(g0, g0 + 3):
                            ins = PE.transpose(bank(n % 4)[:, (g - g0) * P:(g - g0 + 1) * P],
                                               g_wn[:, i, g, kk * P:(kk + 1) * P], ident)
                        ins.then_inc(g_wps, 1)
                        n += 1
            pe.wait_ge(g_wok, n)
            pe.sem_inc(g_tps, 2)

            def gate_tile(t, q, nr):
                pe.wait_ge(g_staged, t + 1)
                pe.wait_ge(g_tok, t + 1)
                for j in range(3):
                    for kk in range(KD):
                        i = j * KD + kk
                        ins = PE.transpose(bank(4, 2)[:, i * P:i * P + nr], st[0:nr, q, j, kk * P:(kk + 1) * P],
                                           ident[0:nr, 0:nr])
                ins.then_inc(g_tps, 1)
                pe.wait_ge(g_tok, t + 2)
                for g in range(2):
                    pe.wait_ge(g_pre, 2 * t + g + 1)
                    wi, wh = g_wT[:, 2 * g], g_wT[:, 2 * g + 1]
                    rz, nh = bank(2 * g)[0:nr], bank(2 * g + 1)[0:nr]
                    for kk in range(KD):
                        X, Hh = sT[:, q, g, kk, 0:nr], sT[:, q, 2, kk, 0:nr]
                        PE.matmul(rz, X, wi[:, kk, 0:2 * D], start=kk == 0, stop=False)
                        PE.matmul(rz, Hh, wh[:, kk, 0:2 * D], start=False, stop=kk == 1)
                        PE.matmul(nh[:, 0:D], X, wi[:, kk, 2 * D:3 * D], start=kk == 0, stop=False, skip_group_check=True)
                        ins = PE.matmul(nh[:, D:2 * D], Hh, wh[:, kk, 2 * D:3 * D], start=False, stop=kk == 1,
                                        skip_group_check=True)
                    ins.then_inc(g_ready, 1)
            tile_pairs(pe, gate_tile)
            stage_end(pe, "pe")
            stage_end(pe, "pe")
            s = sw["L1"]

            def free_1(u):
                pe.wait_ge(s["at_ok"], u.n + 1)

            def products_1(u):
                pe.wait_ge(s["at_ok"], u.n + 3)
                r1 = xd[0:u.kp, bass.ds(u.tile, 1), :].rearrange("p a d -> p (a d)")
                unit_done(u, accumulate(u, [(bank(0, 2)[0:nr, r * D:(r + 1) * D], r // 2,
                                             AT2[0:u.kp, u.q, r * P:r * P + nr], r1)
                                            for r, nr in enumerate(u.rows)]), s, 2)
            pe_sweep(pe, "L1", 2, free_1, products_1)
            stage_end(pe, "pe")
            pe.sem_inc(h1_ps, 2)

            def tile1(t, q, nr):
                pe.wait_ge(h1_st, t + 1)
                for kk in range(KD):
                    ins = PE.transpose(psT[q][:, kk * P:kk * P + nr], xs[0:nr, q, kk * P:(kk + 1) * P], ident[0:nr, 0:nr])
                ins.then_inc(h1_ps, 1)
                pe.wait_ge(h1_ok, t + 1)
                pe.wait_ge(h1_done, t + 1)
                for kk in range(KD):
                    ins = PE.matmul(bank(q)[0:nr, 0:D], xT[:, q, kk, 0:nr], w1T[:, kk, :], start=kk == 0, stop=kk == KD - 1)
                ins.then_inc(h1_mm, 1)
            tile_pairs(pe, tile1)
            stage_end(pe, "pe")
            pe_project(pe, 1, wcat2, D + 2 * H2)
            pe_sums(pe, 0)
            stage_end(pe, "pe")
            pe.wait_ge(fg_ok[0], 1)
            pe_rows("r2", smalls[:, 6, 0:H2 * T], H2)
            s2 = sw["L2"]

            def free_2(u):
                pe.wait_ge(s2["mask_ok"], u.n + 1)

            def products_2(u):
                for h in range(H2):
                    pe.wait_ge(s2["p_ok"], 2 * H2 + u.n * H2 + h + 1)
                    ins = PE.matmul(bank(h)[:, 0:u.w], stage_w[0:u.kp, u.q, h * C2:(h + 1) * C2],
                                    PM[0:u.kp, u.q, h, 0:u.w], start=False, stop=False)
                unit_done(u, ins, s2, H2)
                if u.end:
                    pe.wait_ge(den_dve, (u.c + 1) * T + 1)
                    pe.wait_ge(den_pool, (u.c + 1) * T + 2)
                    pe.wait_ge(den_out, u.c + 1)
                    for h in range(H2):
                        for r, nr in enumerate(u.rows):
                            i = r * H2 + h
                            ins = PE.matmul(bank(4)[0:nr, i:i + 1], S2[:, h, r * P:r * P + nr], ones[:, 0:1], start=True,
                                            stop=True)
                    ins.then_inc(den_ps, 1)
            pe_sweep(pe, "L2", H2, free_2, products_2)
            stage_end(pe, "pe")
            pe_back(pe, 0, rawT2, H2, C2)
            stage_end(pe, "pe")
            pe_project(pe, 2, wcat3, D + 2 * H3)
            pe_sums(pe, 1)
            stage_end(pe, "pe")
            pe.wait_ge(fg_ok[1], 1)
            pe_rows("r3", smalls[:, 6, 0:H3 * T], H3)
            s3 = sw["L3"]

            def products_3(u):
                for h in range(H3):
                    pe.wait_ge(s3["p_ok"], 2 * H3 + u.n * H3 + h + 1)
                    ins = PE.matmul(bank(h)[0:C3 + 1, 0:u.w], stage_w[0:u.kp, u.q, h * (C3 + 1):(h + 1) * (C3 + 1)],
                                    PM[0:u.kp, u.q, h, 0:u.w], start=False, stop=False)
                unit_done(u, ins, s3, H3)
            pe_sweep(pe, "L3", H3, None, products_3, tr=False)
            stage_end(pe, "pe")
            pe_back(pe, 1, rawT3, H3, C3 + 1)
            stage_end(pe, "pe")

        def act_project(act, i):
            staged, xt_ps, xt_ok, proj_ps, proj_ok = projs[i]

            def tile(t, q, nr):
                act.wait_ge(xt_ps, t + 1)
                settle(act)
                S.copy(xs[0:nr, q, :], tl(xnat, t, nr)).then_inc(staged, 1)
                act.wait_ge(xt_ps, t + 3)
                act.wait_ge(proj_ps, t + 1)
                S.copy(xT[:, q, :, 0:nr], psT[q][:, 0:D].rearrange("p (k n) -> p k n", k=KD)[:, :, 0:nr]).then_inc(xt_ok, 1)
            act.sem_inc(proj_ps, 2)
            tile_pairs(act, tile)

        def act_rows(act, k, heads):
            act.wait_ge(rows[k][1], 1)
            S.copy(rows_s[0:heads * T, :], bank(5)[0:heads * T, 0:P]).then_inc(rows[k][2], 1)

        def act_std(act, i):
            act.wait_ge(ln_var[i], 1)
            S.activation(rstd, rstd, ACT.Sqrt).then_inc(ln_std[i], 1)

        def act_copy_sweep(act, k, dst):
            s = sw[k]
            act.sem_inc(s["at_ok"], 2)

            def chunk(c, last):
                def step(u):
                    act.wait_ge(s["transposed"], u.n + 5)
                    act.wait_ge(s["mm_done"], u.n + 1)
                    S.copy(dst[0:u.kp, u.q, 0:u.w], psT[u.q][0:u.kp, 0:u.w]).then_inc(s["at_ok"], 1)
                sweep_units(act, c, last, step)
            sweep_chunks(act, chunk)

        def act_ratio_sweep(act, k, heads, sm):
            s = sw[k]
            act.wait_ge(rows["r2" if k == "L2" else "r3"][4], 16 * heads)
            act.wait_ge(neg_ok, 1 if k == "L2" else 2)

            def chunk(c, last):
                def step(u):
                    for h in range(heads):
                        act.wait_ge(s["p_ok"], u.n * heads + h + 1)
                        settle(act)
                        S.activation(Y[0:u.kp, u.q, h, 0:u.w], r_bc[0:u.kp, h, bass.ds(c * W, u.w)], ACT.Relu,
                                     bias=sm[0:u.kp, 3, bass.ds(u.tile + h * T, 1)],
                                     scale=sm[0:u.kp, 5, bass.ds(u.tile + h * T, 1)]
                                     ).then_inc(s["y_ok"], 1)
                sweep_units(act, c, last, step)
            sweep_chunks(act, chunk)

        @block.scalar
        def _(act):
            act.wait_ge(w1T_ok, 1)
            S.copy(w1T.rearrange("p k f -> p (k f)"), bank(4)[:, 0:KD * D])
            stage_end(act, "act")
            act_project(act, 0)
            stage_end(act, "act")
            act_copy_sweep(act, "A", AT)
            stage_end(act, "act")
            act_rows(act, "e", H0)

            def row_sum(t, q, nr):
                act.wait_ge(b_diag, t + 1)
                settle(act)
                S.activation(arow[0:nr, q, :], arow[0:nr, q, :], ACT.Copy, accum_out=rowsum[0:nr, bass.ds(t, 1)]
                             ).then_inc(b_sum, 1)
            row_sum(0, 0, P)

            def row_tile(t, q, nr):
                if not (isinstance(t, int) and t == T - 1):
                    row_sum(t + 1, 1 - q, P if not isinstance(t, int) else TAIL)
                for h in range(H0):
                    sl = (q * H0 + h) % 2
                    act.wait_ge(b_negm, H0 * t + h + 1)
                    settle(act)
                    S.activation(srow[0:nr, sl, :], srow[0:nr, sl, :], ACT.Exp, bias=col(negm, h, t, nr),
                                 accum_out=col(den, h, t, nr)).then_inc(b_exp, 1)
            tile_pairs(act, row_tile)
            act_rows(act, "m", H0)
            stage_end(act, "act")
            s = sw["C"]

            def chunk(c, last):
                def step(u):
                    act.wait_ge(c_arg, u.n + 2)
                    S.activation(E[0:u.kp, u.q, :, 0:u.w], E[0:u.kp, u.q, :, 0:u.w], ACT.Exp).then_inc(s["y_ok"], 1)
                sweep_units(act, c, last, step)
            sweep_chunks(act, chunk)
            stage_end(act, "act")
            n = 0
            for i in range(4):
                for kk in range(KD):
                    for g0 in (0, 3):
                        act.wait_ge(g_wps, n + 1)
                        S.copy(g_wT[:, i, kk, g0 * P:(g0 + 3) * P], bank(n % 4)[:, 0:3 * P]).then_inc(g_wok, 1)
                        n += 1
            act.sem_inc(g_tok, 1)

            def gate_tile(t, q, nr):
                act.wait_ge(g_tps, t + 3)
                act.wait_ge(g_ready, 2 * t + 1)
                S.copy(sT[:, q].rearrange("p j k n -> p (j k) n")[:, :, 0:nr],
                       bank(4, 2)[:, 0:3 * D].rearrange("p (i n) -> p i n", n=P)[:, :, 0:nr]).then_inc(g_tok, 1)
                for g in range(2):
                    act.wait_ge(g_pre, 2 * t + g + 3)
                    S.activation(g_th[0:nr], g_rz[0:nr], ACT.Tanh, scale=0.5).then_inc(g_thok, 1)
                    act.wait_ge(g_tok2, 2 * t + g + 1)
                    S.activation(g_n[0:nr], g_t[0:nr], ACT.Tanh).then_inc(g_nok, 1)
            act.sem_inc(g_ready, 3)
            tile_pairs(act, gate_tile)
            stage_end(act, "act")
            act_std(act, 0)
            act.wait_ge(deg_in, 1)
            S.activation(degs, degs, ACT.Sqrt).then_inc(deg_out, 1)
            stage_end(act, "act")
            act_copy_sweep(act, "L1", AT2)
            stage_end(act, "act")

            def tile1(t, q, nr):
                act.wait_ge(h1_ps, t + 1)
                settle(act)
                S.copy(xs[0:nr, q, :], tl(raw1, t, nr)).then_inc(h1_st, 1)
                act.wait_ge(h1_ps, t + 3)
                act.wait_ge(h1_mm, t + 1)
                S.copy(xT[:, q, :, 0:nr], psT[q][:, 0:D].rearrange("p (k n) -> p k n", k=KD)[:, :, 0:nr]).then_inc(h1_ok, 1)
            act.sem_inc(h1_mm, 2)
            tile_pairs(act, tile1)
            act_std(act, 1)
            stage_end(act, "act")
            act_project(act, 1)
            stage_end(act, "act")

            def factors(i, heads):
                act.wait_ge(fg_in[i], 1)
                S.activation(smalls[:, 4:7, 0:heads * T], smalls[:, 0:3, 0:heads * T], ACT.Exp).then_inc(fg_ok[i], 1)
            factors(0, H2)
            act_rows(act, "r2", H2)
            act_ratio_sweep(act, "L2", H2, smalls)
            stage_end(act, "act")
            act.wait_ge(elu_in, 1)
            for nr, ts in FULL:
                ins = S.activation(tmp[0:nr, ts], tmp[0:nr, ts], ACT.Exp)
            ins.then_inc(elu_ok, 1)
            act_std(act, 2)
            stage_end(act, "act")
            act_project(act, 2)
            stage_end(act, "act")
            factors(1, H3)
            act_rows(act, "r3", H3)
            act_ratio_sweep(act, "L3", H3, smalls)
            stage_end(act, "act")
            act_std(act, 3)
            stage_end(act, "act")

        def dve_project(dve, i, dst, cols):
            staged, xt_ps, xt_ok, proj_ps, proj_ok = projs[i]
            dve.sem_inc(proj_ok, 2)

            def tile(t, q, nr):
                dve.wait_ge(proj_ps, t + 3)
                for b, (lo, hi) in enumerate(splits(cols)):
                    ins = V.tensor_copy(dst[0:nr, bass.ds(t, 1), lo:hi].rearrange("p a d -> p (a d)"),
                                        bank(2 * q + b)[0:nr, 0:hi - lo])
                ins.then_inc(proj_ok, 1)
            tile_pairs(dve, tile)
            dve.wait_ge(proj_ok, T + 2)

        def dve_norm(dve, link, i):
            def stats(t, q, nr):
                return V.bn_stats(bnst[0:nr, bass.ds(t, 1), :].rearrange("p a m -> p (a m)"), tl(xnat, t, nr))
            link(tile_pairs(dve, stats))
            for t in range(T):
                nr = P if t < T - 1 else TAIL
                ins = V.bn_aggr(mv[0:nr, t, :], bnst[0:nr, t, :])
            link(ins)
            V.tensor_scalar(rstd[:, 0:T - 1], mv[:, 0:T - 1, 1], EPS, None, ALU.add)
            V.tensor_scalar(rstd[0:TAIL, T - 1:T], mv[0:TAIL, T - 1:T, 1], EPS, None, ALU.add).then_inc(ln_var[i], 1)
            dve.wait_ge(ln_std[i], 1)
            link(V.reciprocal(rstd, rstd))

            def scale(t, q, nr):
                return V.tensor_scalar(tl(xnat, t, nr), tl(xnat, t, nr), mv[0:nr, bass.ds(t, 1), 0], rstd[0:nr, bass.ds(t, 1)],
                                ALU.subtract, ALU.mult)
            link(tile_pairs(dve, scale))

        def head_vector(link, wv, av, dst):
            _, hh, ff = wv.shape
            pv = prod[:, 0:hh * ff].rearrange("p (h f) -> p h f", h=hh)
            link(V.tensor_tensor(pv, wv, av, ALU.mult))
            link(V.tensor_reduce(dst, pv, AX_X, ALU.add))

        def node_sum(dve, link, i):
            link(V.tensor_reduce(part, proj[:, 0:T - 1, 0:D].rearrange("p t d -> p d t"), AX_X, ALU.add))
            V.tensor_tensor(part[0:TAIL], part[0:TAIL], proj[0:TAIL, T - 1, 0:D], ALU.add).then_inc(sx_in[i], 1)
            dve.wait_ge(sx_ok[i], 1)
            V.tensor_copy(sum_bc, bank(4)[:, 0:D])

        @block.vector
        def _(dve):
            link = Chain(dve, dve_link)
            V.memset(rstd, 1.0)
            V.memset(rowsum, 1.0)
            dve.wait_ge(const_ok, 1)
            dve.wait_ge(loaded, 16 * (2 + 4 * KD + 8))
            for kk in range(KD):
                w0 = wcat0[:, kk, 0:H0 * D].rearrange("p (h f) -> p h f", h=H0)
                w2 = wcat2[:, kk, 0:D].rearrange("p (h f) -> p h f", h=H2)
                w3 = wcat3[:, kk, 0:D].rearrange("p (h f) -> p h f", h=H3)
                for j in range(2):
                    head_vector(link, w0, a0_bc[:, :, j, :], wcat0[:, kk, H0 * D + j * H0:H0 * D + (j + 1) * H0])
                    head_vector(link, w2, a2_bc[:, :, j, :], wcat2[:, kk, D + j * H2:D + (j + 1) * H2])
                    head_vector(link, w3, a3_bc[:, j], wcat3[:, kk, D + j * H3:D + (j + 1) * H3])
            stage_end(dve, "dve")
            dve_project(dve, 0, hW, H0 * D + 2 * H0)
            for nr, ts in FULL:
                ins = V.tensor_copy(ur[0:nr, ts], hW[0:nr, ts, H0 * D:])
            link(ins)
            for part in range(3):
                for nr, ts in FULL:
                    ins = V.tensor_copy(ub[0:nr, ts, part, 0:2 * H0], ur[0:nr, ts])
                link(ins)
                for nr, ts in FULL:
                    V.tensor_copy(ub[0:nr, ts, part, 2 * H0:3 * H0], ub[0:nr, ts, part, 0:H0])
                    ins = V.tensor_tensor(ur[0:nr, ts], ur[0:nr, ts], ub[0:nr, ts, part, 0:2 * H0], ALU.subtract)
                link(ins)
            stage_end(dve, "dve")
            s = sw["A"]
            dve.sem_inc(s["acc_free"], 1)

            def chunkA(c, last):
                def step(u):
                    dve.wait_ge(s["at_ok"], u.n + 3)
                    dve.wait_ge(s["mm_done"], u.n + 1)
                    V.tensor_scalar(Mp[0:u.kp, u.q, 0:u.w], AT[0:u.kp, u.q, 0:u.w], 0.0, None, ALU.is_gt)
                    V.tensor_scalar(Mm[0:u.kp, u.q, 0:u.w], AT[0:u.kp, u.q, 0:u.w], 0.0, None, ALU.is_lt
                                    ).then_inc(s["mask_ok"], 1)
                sweep_units(dve, c, last, step)
                dve.wait_ge(s["mm_done"], (c + 1) * T + 2)
                empty(c, last, bank(0, 2), D, ns)
                empty(c, last, bank(2), 18, E18.rearrange("p t s h -> p t (s h)")).then_inc(s["acc_free"], 1)
            sweep_chunks(dve, chunkA)
            dve.wait_ge(s["acc_free"], CH + 1)
            for nr, ts in FULL:
                ev = e6[0:nr, :, ts].rearrange("p h t -> p t h")
                link(V.tensor_tensor(ur[0:nr, ts], E18[0:nr, ts, 2], E18[0:nr, ts, 1], ALU.add))
                link(V.tensor_tensor(ur[0:nr, ts], ur[0:nr, ts], E18[0:nr, ts, 0], ALU.add))
                link(V.scalar_tensor_tensor(ev, ur[0:nr, ts], SLOPE, ur[0:nr, ts], ALU.mult, ALU.max))
            stage_end(dve, "dve")
            V.memset(den.rearrange("p h t -> p (h t)"), 1.0)
            dve.wait_ge(rows["e"][4], 16 * H0)
            dve.sem_inc(b_rowfree, 2)
            dve.sem_inc(b_exp, 2)

            def row_tile(t, q, nr):
                dve.wait_ge(b_diag, t + 1)
                dve.wait_ge(b_sum, t + 1)
                link(V.tensor_scalar(mbias[0:nr, :], arow[0:nr, q, :], 0.0, NEG, ALU.is_le, ALU.mult))
                dve.sem_inc(b_rowfree, 1)
                for h in range(H0):
                    sl = (q * H0 + h) % 2
                    dve.wait_ge(b_exp, H0 * t + h + 1)
                    settle(dve)
                    link(V.tensor_tensor_reduce(out=srow[0:nr, sl, :], in0=mbias[0:nr, :], in1=e_bc[0:nr, h, :], scale=1.0,
                                                scalar=3 * NEG, op0=ALU.add, op1=ALU.max, accum_out=mrow[0:nr, sl:sl + 1]))
                    V.tensor_scalar(col(negm, h, t, nr), mrow[0:nr, sl:sl + 1], -1.0, None, ALU.mult).then_inc(b_negm, 1)
            tile_pairs(dve, row_tile, 1 + H0, link)
            dve.wait_ge(b_exp, T * H0 + 2)
            link(V.reciprocal(den.rearrange("p h t -> p (h t)"), den.rearrange("p h t -> p (h t)")))
            link(V.tensor_scalar(den.rearrange("p h t -> p (h t)"), den.rearrange("p h t -> p (h t)"), 1.0 / H0, None,
                                 ALU.mult))
            stage_end(dve, "dve")
            s = sw["C"]
            dve.sem_inc(s["acc_free"], 1)
            dve.sem_inc(s["p_ok"], 2 * H0)

            dve.sem_inc(c_arg, 1)

            def chunkC(c, last):
                dve.wait_ge(mbc_in, 16 * H0 * (c + 1))

                def exponents(u):
                    dve.wait_ge(s["p_ok"], u.n * H0 + H0)
                    for h in range(H0):
                        ins = V.tensor_scalar(E[0:u.kp, u.q, h, 0:u.w], m_bc[0:u.kp, h, 0:u.w],
                                              e6[0:u.kp, h, bass.ds(u.tile, 1)], 0.0, ALU.add, ALU.min)
                    ins.then_inc(c_arg, 1)

                def step(u):
                    dve.wait_ge(s["transposed"], u.n + 5)
                    dve.wait_ge(s["mm_done"], u.n + 1)
                    dve.wait_ge(s["y_ok"], u.n + 1)
                    for h in range(H0):
                        V.tensor_tensor(PA[0:u.kp, u.q, h, 0:u.w], E[0:u.kp, u.q, h, 0:u.w],
                                        psT[u.q][0:u.kp, 0:u.w], ALU.mult).then_inc(s["p_ok"], 1)
                sweep_ahead(dve, c, last, exponents, step)
                dve.wait_ge(s["mm_done"], (c + 1) * T + 2)
                sizes = [P] * RPC if not last else [P, TAIL]
                for h in range(H0):
                    for r, nr in enumerate(sizes):
                        t = c * RPC + r
                        acc = bank(0, 6)[0:nr, (r * H0 + h) * D:(r * H0 + h + 1) * D]
                        if h == 0:
                            ins = V.tensor_scalar(tl(es, t, nr), acc, col(den, h, t, nr), None, ALU.mult)
                        else:
                            ins = V.scalar_tensor_tensor(tl(es, t, nr), acc, col(den, h, t, nr), tl(es, t, nr), ALU.mult,
                                                         ALU.add)
                    if h < H0 - 1:
                        link(ins)
                ins.then_inc(s["acc_free"], 1)
            with dve.Fori(0, CH - 1) as c:
                with link.loop(c, CH - 1, H0 - 1):
                    chunkC(c, False)
            chunkC(CH - 1, True)
            stage_end(dve, "dve")
            dve.sem_inc(g_pre, 2)
            dve.wait_ge(g_in, 128)
            for g in range(2):
                V.tensor_tensor(g_brz[:, g], g_bias[:, 2 * g, 0:2 * D], g_bias[:, 2 * g + 1, 0:2 * D], ALU.add)
                V.tensor_copy(g_bnh[:, g, 0:D], g_bias[:, 2 * g, 2 * D:])
                ins = V.tensor_copy(g_bnh[:, g, D:], g_bias[:, 2 * g + 1, 2 * D:])
            link(ins)

            def gate_tile(t, q, nr):
                X = tl(xnat, t, nr)
                for g in range(2):
                    dve.wait_ge(g_ready, 2 * t + g + 4)
                    V.tensor_tensor(g_rz[0:nr], bank(2 * g)[0:nr], g_brz[0:nr, g], ALU.add)
                    V.tensor_tensor(g_nh[0:nr], bank(2 * g + 1)[0:nr], g_bnh[0:nr, g], ALU.add).then_inc(g_pre, 1)
                    dve.wait_ge(g_pre, 2 * t + g + 3)
                    dve.wait_ge(g_thok, 2 * t + g + 1)
                    link(V.scalar_tensor_tensor(g_q[0:nr], g_th[0:nr, 0:D], 1.0, g_nh[0:nr, D:2 * D], ALU.add, ALU.mult))
                    V.scalar_tensor_tensor(g_t[0:nr], g_q[0:nr], 0.5, g_nh[0:nr, 0:D], ALU.mult, ALU.add
                                           ).then_inc(g_tok2, 1)
                    dve.wait_ge(g_nok, 2 * t + g + 1)
                    link(V.tensor_tensor(g_d[0:nr], X, g_n[0:nr], ALU.subtract))
                    link(V.scalar_tensor_tensor(g_e[0:nr], g_th[0:nr, D:2 * D], 1.0, g_d[0:nr], ALU.add, ALU.mult))
                    link(V.scalar_tensor_tensor(g_out[0:nr, g], g_e[0:nr], 0.5, g_n[0:nr], ALU.mult, ALU.add))
                link(V.tensor_tensor(g_d[0:nr], g_out[0:nr, 0], g_out[0:nr, 1], ALU.add))
                dve.wait_ge(g_staged, t + 1)
                link(V.scalar_tensor_tensor(X, g_d[0:nr], dn[0:nr, bass.ds(t, 1)], X, ALU.mult, ALU.add))
            tile_pairs(dve, gate_tile, 10, link)
            stage_end(dve, "dve")
            dve_norm(dve, link, 0)
            zero = smalls[:, 7, 0:T]
            for nr, ts in FULL:
                ins = V.tensor_tensor(rowsum[0:nr, ts], rowsum[0:nr, ts], dn[0:nr, ts], ALU.add)
            link(ins)
            link(V.tensor_scalar(zero, rowsum, 0.0, None, ALU.is_equal))
            dve.sem_inc(deg_in, 1)
            dve.wait_ge(deg_out, 1)
            link(V.tensor_tensor(rowsum, rowsum, zero, ALU.add))
            link(V.reciprocal(rowsum, rowsum))
            link(V.tensor_scalar(zero, zero, -1.0, 1.0, ALU.mult, ALU.add))
            link(V.tensor_tensor(rowsum, rowsum, zero, ALU.mult))
            r1v = xd

            def by_degree(t, q, nr):
                V.tensor_scalar(tl(r1v, t, nr), tl(xnat, t, nr), rowsum[0:nr, bass.ds(t, 1)], None, ALU.mult)
            tile_pairs(dve, by_degree)
            stage_end(dve, "dve")
            s1 = sw["L1"]
            dve.sem_inc(s1["acc_free"], 1)

            def chunk1(c, last):
                dve.wait_ge(s1["mm_done"], (c + 1) * T + 2)
                empty(c, last, bank(0, 2), D, raw1).then_inc(s1["acc_free"], 1)
            sweep_chunks(dve, chunk1)
            stage_end(dve, "dve")
            dve.sem_inc(h1_done, 2)
            for nr, ts in FULL:
                ins = V.tensor_tensor(xnat[0:nr, ts], xnat[0:nr, ts], b1_bc[0:nr].unsqueeze(1).to_broadcast(
                    [nr, ts.stop - ts.start, D]), ALU.add)
            link(ins)

            def tile1(t, q, nr):
                dve.wait_ge(h1_mm, t + 3)
                link(V.scalar_tensor_tensor(tl(xnat, t, nr), bank(q)[0:nr, 0:D], rowsum[0:nr, bass.ds(t, 1)],
                                            tl(xnat, t, nr), ALU.mult, ALU.add))
                dve.sem_inc(h1_done, 1)
            tile_pairs(dve, tile1, 1, link)
            dve_norm(dve, link, 1)
            stage_end(dve, "dve")
            for i, (heads, cf) in enumerate(((H2, C2), (H3, C3))):
                k = "L2" if i == 0 else "L3"
                s = sw[k]
                dve_project(dve, i + 1, proj, D + 2 * heads)
                node_sum(dve, link, i)
                stage_end(dve, "dve")
                own, oth = (0, heads) if i == 0 else (heads, 0)
                sm = lambda j: smalls[:, j, 0:heads * T].rearrange("p (h t) -> p h t", h=heads)
                for nr, ts in FULL:
                    V.tensor_copy(sm(0)[0:nr, :, ts], proj[0:nr, ts, D + oth:D + oth + heads].rearrange("p t h -> p h t"))
                    ins = V.tensor_copy(sm(2)[0:nr, :, ts],
                                        proj[0:nr, ts, D + own:D + own + heads].rearrange("p t h -> p h t"))
                link(ins)
                link(V.tensor_reduce(cpart[:, 0:heads], sm(0)[:, :, 0:T - 1], AX_X, ALU.max))
                V.tensor_tensor(cpart[0:TAIL, 0:heads], cpart[0:TAIL, 0:heads], sm(0)[0:TAIL, :, T - 1], ALU.max
                                ).then_inc(cm_in[i], 1)
                dve.wait_ge(cm_ok[i], 1)
                cb = cmax[:, 0:heads].unsqueeze(2).to_broadcast([P, heads, T])
                link(V.tensor_tensor(sm(0), sm(0), cb, ALU.subtract))
                V.tensor_scalar(sm(1), sm(0), SLOPE, None, ALU.mult)
                link(V.tensor_tensor(sm(2), sm(2), cb, ALU.add))
                V.tensor_scalar(sm(2), sm(2), -(1.0 - SLOPE), None, ALU.mult).then_inc(fg_in[i], 1)
                dve.wait_ge(fg_ok[i], 1)
                V.tensor_scalar(sm(3), sm(4), -1.0, None, ALU.mult).then_inc(neg_ok, 1)
                dve.wait_ge(neg_ok, i + 1)
                V.memset(stage_w.rearrange("p q m -> p (q m)"), 1.0)
                if i == 0:
                    dve.sem_inc(s["mask_ok"], 2)
                    dve.sem_inc(den_out, 1)
                    dve.sem_inc(den_ps, 1)
                    dve.sem_inc(den_dve, 1)
                link(V.memset(cpart, 0.0))
                dve.sem_inc(s["acc_free"], 1)
                dve.sem_inc(s["p_ok"], 2 * heads)
                width = cf if i == 0 else cf + 1
                rawT = rawT2 if i == 0 else rawT3
                sv = stage_w.rearrange("p q (h m) -> p q h m", h=H3) if i == 1 else \
                    stage_w[:, :, 0:D].rearrange("p q (h m) -> p q h m", h=H2)

                def chunk(c, last):
                    def step(u):
                        if i == 0:
                            dve.wait_ge(s["transposed"], u.n + 5)
                            V.tensor_scalar(msk[0:u.kp, u.q, 0:u.w], psT[u.q][0:u.kp, 0:u.w], 0.0, None, ALU.is_gt
                                            ).then_inc(s["mask_ok"], 1)
                            dve.wait_ge(s["mask_ok"], u.n + 3)
                        else:
                            dve.wait_ge(s["mask_ok"], u.n + 5)
                        dve.wait_ge(s["mm_done"], u.n + 1)
                        if i == 0:
                            dve.wait_ge(den_pool, u.n + 1)
                        V.tensor_copy(sv[0:u.kp, u.q, :, 0:cf], proj[0:u.kp, bass.ds(u.tile, 1), 0:D].rearrange(
                            "p a (h c) -> p (a h) c", h=heads))
                        for h in range(heads):
                            dve.wait_ge(s["y_ok"], u.n * heads + h + 1)
                            V.scalar_tensor_tensor(PM[0:u.kp, u.q, h, 0:u.w], Y[0:u.kp, u.q, h, 0:u.w],
                                                   smalls[0:u.kp, 4, bass.ds(u.tile + h * T, 1)],
                                                   msk[0:u.kp, u.q, 0:u.w], ALU.add, ALU.mult).then_inc(s["p_ok"], 1)
                        if i == 0:
                            dve.wait_ge(den_dve, u.n + 1)
                            dve.wait_ge(s["p_ok"], 2 * H2 + u.n * H2 + H2)
                            V.tensor_tensor(S2[0:u.kp, 1, 0:u.w], S2[0:u.kp, 1, 0:u.w], PM[0:u.kp, u.q, 1, 0:u.w],
                                            ALU.add).then_inc(den_dve, 1)
                    if i == 0:
                        dve.wait_ge(den_ps, c + 1)
                        V.memset(S2[:, 1, :], 0.0).then_inc(den_zero, 1)
                        dve.wait_ge(den_zero, c + 1)
                        settle(dve)
                    sweep_units(dve, c, last, step)
                    dve.wait_ge(s["mm_done"], (c + 1) * T + 2)
                    w = WL if last else W
                    for h in range(heads):
                        ins = V.tensor_copy(rawT[0:width, h, bass.ds(c * W, w)], bank(h)[0:width, 0:w])
                    ins.then_inc(s["acc_free"], 1)
                    if i == 0:
                        dve.wait_ge(den_ps, c + 2)
                        empty(c, last, bank(4), H2, den2).then_inc(den_out, 1)
                sweep_chunks(dve, chunk)
                stage_end(dve, "dve")
                zz = smalls[:, 7, 0:heads * T].rearrange("p (t h) -> p t h", h=heads)
                dd = smalls[:, 3, 0:heads * T].rearrange("p (t h) -> p t h", h=heads)
                t4 = tmp.rearrange("p t (h c) -> p t h c", h=heads)
                u4 = tmp2.rearrange("p t (h c) -> p t h c", h=heads)
                if i == 0:
                    link(V.tensor_copy(dd, den2))
                for t in range(T):
                    nr = P if t < T - 1 else TAIL
                    b4 = bank(t % 4)[0:nr, 0:heads * width].rearrange("p (h c) -> p h c", h=heads)
                    dve.wait_ge(back_ps[i], t + 1)
                    if i == 1:
                        V.tensor_copy(dd[0:nr, t, :].unsqueeze(2), b4[:, :, cf:cf + 1])
                    ins = V.tensor_copy(t4[0:nr, t], b4[:, :, 0:cf])
                    ins.then_inc(back_ok[i], 1)
                dve.wait_ge(back_ok[i], T)
                for nr, ts in FULL:
                    nt = ts.stop - ts.start
                    link(V.tensor_scalar(zz[0:nr, ts], dd[0:nr, ts], 0.0, None, ALU.is_equal))
                    link(V.scalar_tensor_tensor(dd[0:nr, ts], zz[0:nr, ts], float(N), dd[0:nr, ts], ALU.mult, ALU.add))
                    link(V.reciprocal(dd[0:nr, ts], dd[0:nr, ts]))
                    for h in range(heads):
                        mb = sum_bc[0:nr, h * cf:(h + 1) * cf].unsqueeze(1).to_broadcast([nr, nt, cf])
                        ins = V.tensor_tensor(u4[0:nr, ts, h], zz[0:nr, ts, h].unsqueeze(2).to_broadcast([nr, nt, cf]),
                                              mb, ALU.mult)
                    link(ins)
                    link(V.tensor_tensor(tmp[0:nr, ts], tmp[0:nr, ts], tmp2[0:nr, ts], ALU.add))
                    for h in range(heads):
                        ins = V.tensor_tensor(t4[0:nr, ts, h], t4[0:nr, ts, h],
                                              dd[0:nr, ts, h].unsqueeze(2).to_broadcast([nr, nt, cf]), ALU.mult)
                    link(ins)
                if i == 0:
                    dve.sem_inc(h2_made, 1)
                    dve.wait_ge(h2_back, 32)
                    for nr, ts in FULL:
                        a, b = tmp[0:nr, ts], tmp2[0:nr, ts]
                        link(V.tensor_scalar(b, a, 0.0, -1.0, ALU.max, ALU.add))
                        link(V.tensor_tensor(xnat[0:nr, ts], xnat[0:nr, ts], b, ALU.add))
                    for nr, ts in FULL:
                        ins = V.tensor_scalar(tmp[0:nr, ts], tmp[0:nr, ts], 0.0, None, ALU.min)
                    ins.then_inc(elu_in, 1)
                    dve.wait_ge(elu_ok, 1)
                for nr, ts in FULL:
                    ins = V.tensor_tensor(xnat[0:nr, ts], xnat[0:nr, ts], tmp[0:nr, ts], ALU.add)
                link(ins)
                if i == 1:
                    for nr, ts in FULL:
                        ins = V.tensor_tensor(xnat[0:nr, ts], xnat[0:nr, ts], b3_bc[0:nr].unsqueeze(1).to_broadcast(
                            [nr, ts.stop - ts.start, D]), ALU.add)
                    link(ins)
                dve_norm(dve, link, 2 + i)
                stage_end(dve, "dve")


_OUT = (N, D)
_NAMES = ["x", "adj", "L0_gnn_gat_W", "L0_gnn_gat_a", "L0_gnn_edge_Wih", "L0_gnn_edge_Whh", "L0_gnn_edge_bih",
          "L0_gnn_edge_bhh", "L0_gnn_node_Wih", "L0_gnn_node_Whh", "L0_gnn_node_bih", "L0_gnn_node_bhh", "L1_gnn_W",
          "L1_gnn_b", "L2_gnn_W", "L2_gnn_a", "L3_gnn_W", "L3_gnn_a_src", "L3_gnn_a_dst", "L3_gnn_bias"]


def kernel(**inputs):
    import concourse.bacc as bacc
    from concourse.bass_utils import run_bass_kernel_spmd

    nc = bacc.Bacc("TRN2", target_bir_lowering=False, num_devices=1)
    arrays, args = {}, []
    for name in _NAMES:
        a = np.ascontiguousarray(inputs[name])
        arrays[f"in_{name}"] = a
        args.append(nc.dram_tensor(f"in_{name}", a.shape, mybir.dt.from_np(a.dtype), kind="ExternalInput").ap())
    args.append(nc.dram_tensor("out_x", _OUT, F32, kind="ExternalOutput").ap())
    build(nc, *args)
    r = run_bass_kernel_spmd(nc, [arrays], core_ids=[0])
    return r.results[0]["out_x"]
```

```python
from contextlib import ExitStack, contextmanager

import numpy as np

import concourse.bass as bass
from concourse import mybir

F32 = mybir.dt.float32
BF16 = mybir.dt.bfloat16
I32 = mybir.dt.int32
ALU = mybir.AluOpType
ACT = mybir.ActivationFunctionType
AX_X = mybir.AxisListType.X
RMAX = bass.bass_isa.ReduceOp.max

P = 128
N = 2708
D = 256
KD = D // P
T = -(-N // P)
TAIL = N - (T - 1) * P
RPC = 4
W = RPC * P
CH = -(-T // RPC)
WL = N - (CH - 1) * W
QUADS = T // 4
H0, H2, H3 = 3, 2, 4
C2, C3 = D // H2, D // H3
NEG = -1e30
EPS = 1e-5
SLOPE = 0.2


class Unit:

    def __init__(self, c, last, n, tile, slot, k, diag, end):
        self.c, self.last, self.n, self.tile, self.slot, self.k, self.diag, self.end = c, last, n, tile, slot, k, diag, end
        self.q = slot % 2
        self.kp = TAIL if (isinstance(tile, int) and tile == T - 1) else P
        self.w = WL if last else W
        self.rows = [P] * RPC if not last else [P, TAIL]
        uses = 6 if slot < 2 else 5
        per = 32 if last else 16
        self.loaded = 16 * uses * c + per * (k + 1)
        self.loaded1 = 16 * (uses * c + k + 1)
        self.first = last or (isinstance(k, int) and k == 0)

    def slot_free(self):
        return self.n + 3 if (self.first and self.slot < 2) else self.n + 1


def sweep_chunks(eng, body):
    with eng.Fori(0, CH - 1) as c:
        body(c, False)
    body(CH - 1, True)


def sweep_units(eng, c, last, step):
    base = c * T
    if not last:
        for u in range(4):
            step(Unit(c, last, base + u, c * 4 + u, u, 0, u, False))
        with eng.Fori(1, QUADS) as k:
            for u in range(4):
                step(Unit(c, last, base + k * 4 + u, ((c + k) % QUADS) * 4 + u, u, k, None, False))
    else:
        with eng.Fori(0, QUADS) as k:
            for u in range(4):
                step(Unit(c, last, base + k * 4 + u, k * 4 + u, u, k, None, False))
    for u in range(2):
        step(Unit(c, last, base + 4 * QUADS + u, 4 * QUADS + u, u, QUADS, u if last else None, u == 1))


def sweep_ahead(eng, c, last, front, step, tail=None):
    def run(units):
        front(units[0])
        for i, u in enumerate(units):
            if tail:
                step(u)
            if i + 1 < len(units):
                front(units[i + 1])
            (tail or step)(u)

    base = c * T
    if not last:
        run([Unit(c, last, base + v, c * 4 + v, v, 0, v, False) for v in range(4)])
        with eng.Fori(1, QUADS) as k:
            run([Unit(c, last, base + k * 4 + v, ((c + k) % QUADS) * 4 + v, v, k, None, False) for v in range(4)])
    else:
        with eng.Fori(0, QUADS) as k:
            run([Unit(c, last, base + k * 4 + v, k * 4 + v, v, k, None, False) for v in range(4)])
    run([Unit(c, last, base + 4 * QUADS + v, 4 * QUADS + v, v, QUADS, v if last else None, v == 1) for v in range(2)])


def tile_pairs(eng, step, *chains):
    with eng.Fori(0, T // 2 - 1) as g:
        with ExitStack() as counts:
            for chain, links in chains:
                counts.enter_context(chain.loop(g, T // 2 - 1, 2 * links))
            for q in range(2):
                step(g * 2 + q, q, P)
    for q in range(2):
        ins = step(T - 2 + q, q, P if q == 0 else TAIL)
    return ins


class Chain:

    def __init__(self, eng, sem):
        self.eng, self.sem, self.base, self.local = eng, sem, 0, 0

    def __call__(self, ins):
        ins.then_inc(self.sem, 1)
        self.local += 1
        self.eng.wait_ge(self.sem, self.base + self.local)

    @contextmanager
    def loop(self, turn, turns, links):
        before = self.base + self.local
        self.base, self.local = before + turn * links, 0
        yield
        assert self.local == links, (self.local, links)
        self.base, self.local = before + turns * links, 0

    @contextmanager
    def either(self):
        before = self.base, self.local
        yield
        self.base, self.local = before


FULL = ((P, slice(0, T - 1)), (TAIL, slice(T - 1, T)))


def build(nc, x, adj, gat_W, gat_a, e_Wih, e_Whh, e_bih, e_bhh, n_Wih, n_Whh, n_bih, n_bhh,
          W1, b1, W2, a2, W3, a_src, a_dst, b3, out):
    V, S, G, PE = nc.vector, nc.scalar, nc.gpsimd, nc.tensor
    e_rows = nc.dram_tensor("e_rows", (H0, T * P), F32).ap()
    d_rows = nc.dram_tensor("d_rows", (H0, T * P), F32).ap()
    m_rows = nc.dram_tensor("m_rows", (H0, T * P), F32).ap()
    r2_rows = nc.dram_tensor("r2_rows", (H2, T * P), F32).ap()
    r3_rows = nc.dram_tensor("r3_rows", (H3, T * P), F32).ap()

    adj_T = nc.dram_tensor("adj_T", (N, N), F32).ap()

    heads2 = nc.dram_tensor("heads2", (H2 * N, C2), F32).ap()

    with ExitStack() as ctx:
        ARENA = 53000
        arena = ctx.enter_context(nc.sbuf_tensor("arena", [P, ARENA], F32))
        psum = ctx.enter_context(nc.psum_tensor("banks", [P, 8, 512], F32))
        top = [0]

        def sb(*shape, dt=F32):
            n = int(np.prod(shape))
            words = n if dt == F32 else (n + 1) // 2
            a = arena[:, top[0]:top[0] + words]
            top[0] += words + words % 2
            assert top[0] <= ARENA, top[0]
            if dt != F32:
                a = a.bitcast(dt)
            if len(shape) > 1:
                names = "abcd"[:len(shape)]
                a = a.rearrange(f"p ({' '.join(names)}) -> p {' '.join(names)}", **dict(zip(names, shape)))
            return a

        def sem(name):
            return ctx.enter_context(nc.semaphore(name))

        ident = sb(P)
        noteye = sb(P)
        ones = sb(P)
        zrow = sb(W, dt=BF16)
        xnat = sb(T, D)
        dn = sb(T)
        rowsum = sb(T)
        mv = sb(T, 2)
        rstd = sb(T)
        bnst = sb(T, 6)
        mrow = sb(2)
        wcat0 = sb(KD, H0 * D + 2 * H0)
        wcat2 = sb(KD, D + 2 * H2)
        wcat3 = sb(KD, D + 2 * H3)
        w1T = sb(KD, D)
        b1_bc = sb(D)
        b3_bc = sb(D)
        xs = sb(2, D)
        xT = sb(2, KD, P)
        rows_s = sb(P)
        smalls = sb(8, T * H3)
        sum_bc = sb(D)
        part = sb(D)
        cpart = sb(H3)
        dflag = sb(T)
        cmax = sb(H3)
        has_neg = sb(1)
        has_neg_int = has_neg.bitcast(I32)
        stage_base = top[0]

        a0_bc = sb(H0, 2, D)
        a2_bc = sb(H2, 2, C2)
        a3_bc = sb(2, H3, C3)
        prod = sb(D * H0)
        w1n = sb(KD, D)
        top[0] = stage_base
        hW = sb(T, H0 * D + 2 * H0)
        ns = sb(T, D)
        ub = sb(T, 3, 3 * H0 + 1, dt=BF16)
        E21 = sb(T, 3, 2 * H0 + 1)
        e6 = sb(2 * H0, T)
        e_step = sb(H0, T)
        d_s = sb(P)
        negm = sb(H0, T)
        den = sb(H0, T)
        ur = sb(T, 2 * H0)
        l0_base = top[0]
        print("L0BASE", l0_base)
        blk = sb(4, RPC, P)
        AT = sb(4, W)
        Mp = sb(2, W, dt=BF16)
        Mm = sb(2, W, dt=BF16)
        top[0] = l0_base
        d_bc = wcat0.rearrange("p k n -> p (k n)")[:, 0:N // 2]
        e_bc = sb(H0, N)
        arow = sb(2, N)
        mbias = sb(N, dt=BF16)
        srow = xnat.rearrange("p t d -> p (t d)")[:, 0:2 * N].rearrange("p (s n) -> p s n", s=2)
        top[0] = l0_base
        sb(4, RPC, P)
        m_bc = sb(H0, W)
        E = sb(2, H0, W)
        PA = sb(2, H0, W)
        es = sb(T, D)
        top[0] = stage_base
        g_wT = sb(4, KD, 3 * D)
        g_bias = sb(4, 3 * D)
        g_wn = sb(4, 6, D)
        assert top[0] <= stage_base + T * (H0 * D + 2 * H0)
        top[0] = stage_base + T * (H0 * D + 2 * H0)
        sb(T, D)
        top[0] = l0_base
        g_brz = sb(2, 2 * D)
        g_bnh = sb(2, 2 * D)
        st = sb(2, 3, D)
        sT = sb(2, 3, KD, P)
        g_rz = sb(2 * D)
        g_nh = sb(2 * D)
        g_th = sb(2 * D)
        g_q = sb(D)
        g_t = sb(D)
        g_n = sb(D)
        g_d = sb(D)
        g_e = sb(D)
        g_out = sb(2, D)
        assert top[0] <= l0_base + 4 * RPC * P + H0 * W + 4 * H0 * W, top[0]
        top[0] = stage_base
        xd = sb(T, D)
        raw1 = sb(T, D)
        proj = sb(T, D + 2 * H3)
        blk2 = sb(4, RPC, P)
        msk = sb(2, W, dt=BF16)
        stage_w = sb(2, H3 * (C3 + 1))
        S2 = sb(H2, W)
        den2 = sb(T, H2)
        free_from = top[0]
        r_bc = sb(H3, N)
        Y = sb(2, H3, W)
        PM = sb(2, H3, W)
        end_of_3 = top[0]
        top[0] = stage_base
        rawT2 = sb(H2, N)
        top[0] = stage_base
        rawT3 = sb(H3, N)
        assert top[0] <= stage_base + 2 * T * D
        top[0] = free_from
        tmp = sb(T, D)
        tmp2 = sb(T, D)
        assert top[0] <= end_of_3

        def bank(i, n=1):
            return psum[:, i:i + n, :].rearrange("p b n -> p (b n)")

        psT = [bank(6), bank(7)]

        waits_seen = sem("waits_seen")
        loaded, x_again = sem("loaded"), sem("x_again")
        const_ok = sem("const_ok")
        stage_done = sem("stage_done")
        dve_link, act_link, pool_link = sem("dve_link"), sem("act_link"), sem("pool_link")
        w1T_ok = sem("w1T_ok")
        projs = [[sem(f"l{l}_{s}") for s in ("staged", "xt_ps", "xt_ok", "proj_ps", "proj_ok")] for l in (0, 2, 3)]
        rows = {k: [None] + [sem(f"{k}_{s}") for s in ("ps", "sb", "dram", "bc")] for k in ("e", "d", "m", "r2", "r3")}
        steps = dict(A="transposed diag_ok at_ok mask_ok", C="y_ok p_ok", L1="",
                     L2="diag_ok mask_ok y_ok p_ok", L3="mask_ok y_ok p_ok")
        sw = {k: dict(blk_in=[sem(f"{k}_blk_in{i}") for i in range(4)],
                      **{s: sem(f"{k}_{s}") for s in (names + " mm_done acc_free").split()})
              for k, names in steps.items()}
        at_out = [sem(f"at_out{i}") for i in range(4)]
        st_ok = sem("st_ok")
        b_in = [sem(f"b_in{i}") for i in range(2)]
        b_diag, b_rowfree, b_s, b_negm, b_exp = (sem(f"b_{s}") for s in ("diag", "rowfree", "s", "negm", "exp"))
        b_sum = sem("b_sum")
        gen_arg, neg_in, neg_all, gen_in, gen_free, gen_link = (sem(s) for s in ("gen_arg", "neg_in", "neg_all", "gen_in", "gen_free", "gen_link"))
        mbc_in, c_arg = sem("mbc_in"), sem("c_arg")
        g_in, g_wps, g_wok = sem("g_in"), sem("g_wps"), sem("g_wok")
        g_staged, g_tps, g_tok, g_ready, g_pre, g_thok, g_tok2, g_nok = (
            sem(f"g_{s}") for s in ("staged", "tps", "tok", "ready", "pre", "thok", "tok2", "nok"))
        ln_var = sem("ln_var")
        ln_std = sem("ln_std")
        deg_in, deg_out = sem("deg_in"), sem("deg_out")
        h1_st, h1_ps, h1_ok, h1_mm, h1_done = (sem(f"h1_{s}") for s in ("st", "ps", "ok", "mm", "done"))
        cm_in = sem("cm_in")
        cm_ok = sem("cm_ok")
        fg_in = sem("fg_in")
        fg_ok = sem("fg_ok")
        neg_ok, den_zero = sem("neg_ok"), sem("den_zero")
        elu_in, elu_ok = sem("elu_in"), sem("elu_ok")
        sx_in = sem("sx_in")
        sx_ok = sem("sx_ok")
        stored = sem("stored")
        den_dve, den_pool, den_out, den_ps = (sem(f"den_{s}") for s in ("dve", "pool", "out", "ps"))
        back_ps = [sem(f"back_ps{i}") for i in range(2)]
        back_ok = [sem(f"back_ok{i}") for i in range(2)]
        h2_made, h2_out, h2_back = sem("h2_made"), sem("h2_out"), sem("h2_back")

        barriers = {}

        def stage_end(eng, name):
            barriers[name] = barriers.get(name, 0) + 1
            eng.drain().then_inc(stage_done, 1)
            eng.wait_ge(stage_done, 5 * barriers[name])

        def settle(eng):
            eng.sem_inc(waits_seen, 1)

        def load(eng, dst, src, s):
            eng.dma_start(dst, src).then_inc(s, 16)

        def load_nodes(eng, dst, src, s):
            load(eng, dst[:, 0:T - 1, :], src[0:(T - 1) * P, :].rearrange("(t p) d -> p t d", p=P), s)
            load(eng, dst[0:TAIL, T - 1, :], src[(T - 1) * P:N, :], s)

        def tl(a, t, nr):
            if isinstance(t, int):
                return a[0:nr, t, :]
            return a[0:nr, bass.ds(t, 1), :].rearrange("p a d -> p (a d)")

        def col(a, h, t, nr):
            return a[0:nr, h, bass.ds(t, 1)]

        degs = rowsum

        def empty(c, last, acc, width, dst):
            if not last:
                return V.tensor_copy(dst[:, bass.ds(c * RPC, RPC), :], acc[:, 0:RPC * width].rearrange(
                    "p (r d) -> p r d", r=RPC))
            V.tensor_copy(dst[:, c * RPC, :], acc[:, 0:width])
            return V.tensor_copy(dst[0:TAIL, c * RPC + 1, :], acc[0:TAIL, width:2 * width])

        def sp_blocks(sp, k):
            s = sw[k]

            def chunk(c, last):
                def step(u):
                    sp.wait_ge(s["transposed"], u.slot_free())
                    col = bass.ds(u.tile * P, u.kp)
                    if not last:
                        load(sp, blk[:, u.slot, :, 0:u.kp],
                             adj[bass.ds(c * W, W), col].rearrange("(r p) n -> p r n", p=P), s["blk_in"][u.slot])
                    else:
                        for r, nr in enumerate(u.rows):
                            load(sp, blk[0:nr, u.slot, r, 0:u.kp], adj[c * W + r * P:c * W + r * P + nr, col],
                                 s["blk_in"][u.slot])
                sweep_units(sp, c, last, step)
            sweep_chunks(sp, chunk)

        def sp_strips(sp, k, matrix, used, per=1):
            s, dst = sw[k], blk2

            def chunk(c, last):
                def step(u):
                    sp.wait_ge(used, per * u.slot_free())
                    load(sp, dst[0:u.kp, u.slot].rearrange("p r n -> p (r n)")[:, 0:u.w],
                         matrix[bass.ds(u.tile * P, u.kp), bass.ds(c * W, u.w)], s["blk_in"][u.slot])
                sweep_units(sp, c, last, step)
            sweep_chunks(sp, chunk)

        def sp_rows(sp, k, dram, heads, bc):
            sp.wait_ge(rows[k][2], 1)
            load(sp, dram.rearrange("h (t p) -> (h t) p", p=P), (d_s if k == "d" else rows_s)[0:heads * T, :], rows[k][3])
            sp.wait_ge(rows[k][3], 16)
            if bc is not None:
                for h in range(heads):
                    load(sp, bc[:, h, :], dram[h:h + 1, 0:N].partition_broadcast(P).rearrange("p a n -> p (a n)"),
                         rows[k][4])

        block = ctx.enter_context(nc.Block())

        @block.sync
        def _(sp):
            load_nodes(sp, xnat, x, loaded)
            for kk in range(KD):
                f = slice(kk * P, (kk + 1) * P)
                load(sp, wcat0[:, kk, 0:H0 * D].rearrange("p (h f) -> p h f", h=H0),
                     gat_W[:, f, :].rearrange("h k f -> k h f"), loaded)
                load(sp, wcat2[:, kk, 0:D].rearrange("p (h f) -> p h f", h=H2), W2[:, f, :].rearrange("h k f -> k h f"),
                     loaded)
                load(sp, wcat3[:, kk, 0:D], W3[f, :], loaded)
                load(sp, w1n[:, kk, :], W1[f, :], loaded)
            flat = lambda a: a.partition_broadcast(P)
            load(sp, a0_bc.rearrange("p h s f -> p (h s f)"), flat(gat_a.rearrange("h f o -> (h f o)")), loaded)
            load(sp, a2_bc.rearrange("p h s f -> p (h s f)"), flat(a2.rearrange("h f o -> (h f o)")), loaded)
            load(sp, a3_bc[:, 0].rearrange("p h f -> p (h f)"), flat(a_src.rearrange("h f -> (h f)")), loaded)
            load(sp, a3_bc[:, 1].rearrange("p h f -> p (h f)"), flat(a_dst.rearrange("h f -> (h f)")), loaded)
            load(sp, b1_bc, flat(b1), loaded)
            load(sp, b3_bc, flat(b3), loaded)
            diag = bass.AP(adj.tensor, 0, [[N + 1, P], [P * (N + 1), T - 1], [1, 1]])
            sp.dma_start(dn[:, 0:T - 1].unsqueeze(2), diag, allow_slow_non_contiguous=True).then_inc(loaded, 16)
            diag_tail = bass.AP(adj.tensor, (T - 1) * P * (N + 1), [[N + 1, TAIL], [1, 1]])
            sp.dma_start(dn[0:TAIL, T - 1:T], diag_tail, allow_slow_non_contiguous=True).then_inc(loaded, 16)
            stage_end(sp, "sp")
            stage_end(sp, "sp")
            sp_blocks(sp, "A")
            stage_end(sp, "sp")
            sp_rows(sp, "e", e_rows, H0, e_bc)
            sp_rows(sp, "d", d_rows, H0, None)
            negative = sp.value_load(has_neg_int[0:1, 0:1])

            def row_tile(t, q, nr):
                sp.wait_ge(b_rowfree, t + 1)
                load(sp, arow[0:nr, q, :], adj[bass.ds(t * P, nr), :], b_in[q])

            def row_tile_general(t, q, nr):
                if not isinstance(t, int) or t < T - 1:
                    row_tile(t + 1, 1 - q, TAIL if isinstance(t, int) else P)
                for i in range(2 * H0):
                    h, half = i // 2, i % 2
                    sp.wait_ge(gen_free, t * 2 * H0 + i + 1)
                    load(sp, d_bc, d_rows[h:h + 1, half * (N // 2):(half + 1) * (N // 2)].partition_broadcast(P).rearrange(
                        "p a n -> p (a n)"), gen_in)
            with sp.If(negative != 0):
                row_tile(0, 0, P)
                tile_pairs(sp, row_tile_general)
            with sp.Else():
                tile_pairs(sp, row_tile)
            sp_rows(sp, "m", m_rows, H0, None)
            stage_end(sp, "sp")
            load_nodes(sp, xnat, x, x_again)
            s = sw["C"]

            def chunk(c, last):
                w = WL if last else W
                sp.wait_ge(c_arg, c * T + 1)
                for h in range(H0):
                    load(sp, m_bc[:, h, 0:w],
                         m_rows[h:h + 1, bass.ds(c * W, w)].partition_broadcast(P).rearrange("p a n -> p (a n)"), mbc_in)

                def step(u):
                    sp.wait_ge(s["p_ok"], H0 * u.slot_free())
                    load(sp, blk[0:u.kp, u.slot].rearrange("p r n -> p (r n)")[:, 0:w],
                         adj_T[bass.ds(u.tile * P, u.kp), bass.ds(c * W, w)], s["blk_in"][u.slot])
                sweep_units(sp, c, last, step)
            sweep_chunks(sp, chunk)
            sp.wait_ge(x_again, 32)
            stage_end(sp, "sp")
            for i, (w, b) in enumerate(((e_Wih, e_bih), (e_Whh, e_bhh), (n_Wih, n_bih), (n_Whh, n_bhh))):
                load(sp, g_wn[:, i], w.rearrange("(g p) k -> p g k", p=P), g_in)
                load(sp, g_bias[:, i], b.partition_broadcast(P), g_in)
            stage_end(sp, "sp")
            stage_end(sp, "sp")
            sp_strips(sp, "L1", adj_T, sw["L1"]["mm_done"])
            stage_end(sp, "sp")
            stage_end(sp, "sp")
            stage_end(sp, "sp")
            sp_rows(sp, "r2", r2_rows, H2, r_bc[:, 0:H2])
            sp_strips(sp, "L2", adj_T, sw["L2"]["mask_ok"])
            stage_end(sp, "sp")
            sp.wait_ge(h2_made, 1)
            for h in range(H2):
                f = slice(h * C2, (h + 1) * C2)
                load(sp, heads2[h * N:h * N + (T - 1) * P, :].rearrange("(t p) c -> p t c", p=P), tmp[:, 0:T - 1, f], h2_out)
                load(sp, heads2[h * N + (T - 1) * P:(h + 1) * N, :], tmp[0:TAIL, T - 1, f], h2_out)
            sp.wait_ge(h2_out, 16 * 2 * H2)
            load_nodes(sp, tmp, heads2.rearrange("(n g) c -> n (g c)", g=H2), h2_back)
            stage_end(sp, "sp")
            stage_end(sp, "sp")
            sp_rows(sp, "r3", r3_rows, H3, r_bc)
            sp_strips(sp, "L3", adj, sw["L3"]["mask_ok"])
            stage_end(sp, "sp")
            stage_end(sp, "sp")
            sp.dma_start(out[0:(T - 1) * P, :].rearrange("(t p) d -> p t d", p=P), xnat[:, 0:T - 1, :]).then_inc(stored, 16)
            sp.dma_start(out[(T - 1) * P:N, :], xnat[0:TAIL, T - 1, :]).then_inc(stored, 16)
            sp.wait_ge(stored, 32)

        def pool_diag(pool):
            s = sw["A"]

            def chunk(c, last):
                nd = 4 if not last else 2

                def step(u):
                    if u.diag is None:
                        return
                    pool.wait_ge(s["blk_in"][u.slot], u.loaded)
                    r, nr = u.diag, u.rows[u.diag]
                    b = blk[0:nr, u.slot, r, 0:nr]
                    G.tensor_tensor(b, b, noteye[0:nr, 0:nr], ALU.mult).then_inc(s["diag_ok"], 1)
                if not last:
                    for u in range(4):
                        step(Unit(c, last, c * T + u, c * 4 + u, u, 0, u, False))
                else:
                    for u in range(2):
                        step(Unit(c, last, c * T + 20 + u, 20 + u, u, QUADS, u, False))
            sweep_chunks(pool, chunk)

        @block.gpsimd
        def _(pool):
            link = Chain(pool, pool_link)
            G.memset(ones, 1.0)
            G.memset(zrow, 0.0)
            G.memset(ident, 0.0)
            link(G.memset(noteye, 1.0))
            G.affine_select(out=ident, in_=ident, compare_op=ALU.not_equal, fill=1.0, base=0, pattern=[[-1, P]],
                            channel_multiplier=1)
            G.affine_select(out=noteye, in_=noteye, compare_op=ALU.not_equal, fill=0.0, base=0, pattern=[[-1, P]],
                            channel_multiplier=1).then_inc(const_ok, 1)
            stage_end(pool, "pool")
            G.memset(e6, 0.0)
            G.memset(negm, 0.0)
            stage_end(pool, "pool")
            pool_diag(pool)
            pool.wait_ge(neg_in, 1)
            G.partition_all_reduce(cmax[:, 0:1], cpart[:, 0:1], P, RMAX).then_inc(neg_all, 1)
            stage_end(pool, "pool")

            def row_tile(t, q, nr):
                pool.wait_ge(b_in[q], 8 * (t - q) + 16)
                b = arow[0:nr, q, bass.ds(t * P, nr)]
                G.tensor_tensor(b, b, noteye[0:nr, 0:nr], ALU.mult).then_inc(b_diag, 1)
            tile_pairs(pool, row_tile)
            stage_end(pool, "pool")
            stage_end(pool, "pool")

            def gate_tile(t, q, nr):
                pool.wait_ge(g_tps, t + 1)
                G.tensor_copy(st[0:nr, q, 0], tl(ns, t, nr))
                G.tensor_copy(st[0:nr, q, 1], tl(es, t, nr))
                G.tensor_copy(st[0:nr, q, 2], tl(xnat, t, nr)).then_inc(g_staged, 1)
            tile_pairs(pool, gate_tile)
            stage_end(pool, "pool")
            stage_end(pool, "pool")
            stage_end(pool, "pool")
            stage_end(pool, "pool")

            def maxima(i, heads):
                pool.wait_ge(cm_in, i + 1)
                G.partition_all_reduce(cmax[:, 0:heads], cpart[:, 0:heads], P, RMAX).then_inc(cm_ok, 1)
            G.memset(smalls.rearrange("p a b -> p (a b)"), 0.0)
            stage_end(pool, "pool")
            maxima(0, H2)
            s = sw["L2"]
            pool.sem_inc(den_pool, 2)

            def chunk2(c, last):
                def step(u):
                    pool.wait_ge(den_pool, u.n + 2)
                    pool.wait_ge(s["p_ok"], 2 * H2 + u.n * H2 + 1)
                    G.tensor_tensor(S2[0:u.kp, 0, 0:u.w], S2[0:u.kp, 0, 0:u.w], PM[0:u.kp, u.q, 0, 0:u.w], ALU.add
                                    ).then_inc(den_pool, 1)
                pool.wait_ge(den_ps, c + 1)
                settle(pool)
                G.memset(S2[:, 0, :], 0.0).then_inc(pool_link, 1)
                pool.wait_ge(pool_link, c + 2)
                settle(pool)
                sweep_units(pool, c, last, step)
            sweep_chunks(pool, chunk2)
            stage_end(pool, "pool")
            stage_end(pool, "pool")
            stage_end(pool, "pool")
            maxima(1, H3)
            s = sw["L3"]
            pool.sem_inc(s["mask_ok"], 4)

            def chunk3(c, last):
                w = WL if last else W

                def step(u):
                    pool.wait_ge(s["blk_in"][u.slot], u.loaded1)
                    pool.wait_ge(s["p_ok"], u.n * H3 + H3)
                    settle(pool)
                    G.tensor_scalar(msk[0:u.kp, u.q, 0:w], blk2[0:u.kp, u.slot].rearrange("p r n -> p (r n)")[:, 0:w],
                                    0.5, None, ALU.is_gt).then_inc(s["mask_ok"], 1)
                sweep_units(pool, c, last, step)
            sweep_chunks(pool, chunk3)
            stage_end(pool, "pool")
            stage_end(pool, "pool")

        def pe_project(pe, i, wcat, cols):
            staged, xt_ps, xt_ok, proj_ps, proj_ok = projs[i]
            pe.sem_inc(xt_ps, 2)

            def tile(t, q, nr):
                pe.wait_ge(staged, t + 1)
                for kk in range(KD):
                    last = PE.transpose(psT[q][:, kk * P:kk * P + nr], xs[0:nr, q, kk * P:(kk + 1) * P], ident[0:nr, 0:nr])
                last.then_inc(xt_ps, 1)
                pe.wait_ge(xt_ok, t + 1)
                pe.wait_ge(proj_ok, t + 1)
                for kk in range(KD):
                    for b, (lo, hi) in enumerate(splits(cols)):
                        last = PE.matmul(bank(2 * q + b)[0:nr, 0:hi - lo], xT[:, q, kk, 0:nr], wcat[:, kk, lo:hi],
                                         start=kk == 0, stop=kk == KD - 1)
                last.then_inc(proj_ps, 1)
            tile_pairs(pe, tile)

        def pe_back(pe, i, src, heads, m):
            for t in range(T):
                nr = P if t < T - 1 else TAIL
                if t >= 4:
                    pe.wait_ge(back_ok[i], t - 3)
                for h in range(heads):
                    ins = PE.transpose(bank(t % 4)[0:nr, h * m:(h + 1) * m], src[0:m, h, t * P:t * P + nr],
                                       ident[0:m, 0:m])
                ins.then_inc(back_ps[i], 1)

        def pe_sums(pe, i):
            pe.wait_ge(sx_in, i + 1)
            PE.matmul(bank(4)[:, 0:D], ones, part, start=True, stop=True).then_inc(sx_ok, 1)

        def splits(cols):
            return [(0, cols)] if cols <= 512 else [(0, 512), (512, cols)]

        def pe_rows(k, src, heads, b=5):
            PE.transpose(bank(b)[0:heads * T, 0:P], src, ident[:, :]).then_inc(rows[k][1], 1)

        def pe_sweep(pe, k, nbanks, products, front=None, ahead=2):
            s = sw[k]
            pe.sem_inc(s["mm_done"], ahead)

            def chunk(c, last):
                pe.wait_ge(s["acc_free"], c + 1)
                for b in range(nbanks):
                    PE.matmul(bank(b), zrow[0:1, 0:P], zrow[0:1, :], start=True, stop=False)
                sweep_ahead(pe, c, last, front or (lambda u: None), products)
            sweep_chunks(pe, chunk)

        def accumulate(u, mms):
            for i, (o, b, l, r) in enumerate(mms):
                ins = PE.matmul(o, l, r, start=False, stop=False, skip_group_check=True)
            return ins

        def unit_done(u, ins, s, nbanks):
            if u.end:
                for b in range(nbanks):
                    ins = PE.matmul(bank(b), zrow[0:1, 0:P], zrow[0:1, :], start=False, stop=True)
            ins.then_inc(s["mm_done"], 1)

        @block.tensor
        def _(pe):
            pe.wait_ge(const_ok, 1)
            pe.wait_ge(loaded, 16 * (2 + 4 * KD + 8))
            for fo in range(KD):
                for kk in range(KD):
                    ins = PE.transpose(bank(4)[:, (kk * KD + fo) * P:(kk * KD + fo + 1) * P],
                                       w1n[:, fo, kk * P:(kk + 1) * P], ident)
            ins.then_inc(w1T_ok, 1)
            stage_end(pe, "pe")
            pe_project(pe, 0, wcat0, H0 * D + 2 * H0)
            stage_end(pe, "pe")
            s = sw["A"]

            def transposes_A(u):
                pe.wait_ge(s["at_ok"], u.n + 1)
                if u.diag is None:
                    pe.wait_ge(s["blk_in"][u.slot], u.loaded)
                else:
                    pe.wait_ge(s["diag_ok"], u.c * 4 + u.diag + 1)
                for r, nr in enumerate(u.rows):
                    ins = PE.transpose(psT[u.q][0:u.kp, r * P:r * P + nr], blk[0:nr, u.slot, r, 0:u.kp], ident[0:nr, 0:nr])
                ins.then_inc(s["transposed"], 1)

            def products_A(u):
                rhs_x = xnat[0:u.kp, u.tile, :] if isinstance(u.tile, int) else \
                    xnat[0:u.kp, bass.ds(u.tile, 1), :].rearrange("p a d -> p (a d)")
                pe.wait_ge(s["at_ok"], u.n + 3)
                accumulate(u, [(bank(0, 2)[0:nr, r * D:(r + 1) * D], r // 2, AT[0:u.kp, u.slot, r * P:r * P + nr], rhs_x)
                               for r, nr in enumerate(u.rows)])
                pe.wait_ge(s["mask_ok"], u.n + 1)
                mms = []
                for m, lo, wide in ((Mp, 0, 2 * H0), (Mm, H0, 2 * H0 + 1)):
                    rhs_u = ub[0:u.kp, bass.ds(u.tile, 1), :, lo:lo + wide].rearrange("p a s h -> p (a s) h")
                    mms += [(bank(2)[0:nr, r * 21:(r + 1) * 21].rearrange("p (s h) -> p s h", s=3)[:, :, 0:wide], 2,
                             m[0:u.kp, u.q, r * P:r * P + nr], rhs_u) for r, nr in enumerate(u.rows)]
                unit_done(u, accumulate(u, mms), s, 3)
            pe.sem_inc(s["transposed"], 4)
            pe_sweep(pe, "A", 3, products_A, transposes_A)
            stage_end(pe, "pe")
            pe_rows("e", e6[:, 0:H0, :].rearrange("p h t -> p (h t)"), H0)
            pe_rows("d", e_step.rearrange("p h t -> p (h t)"), H0, 4)
            pe.wait_ge(b_negm, T * H0)
            pe_rows("m", negm.rearrange("p h t -> p (h t)"), H0)
            stage_end(pe, "pe")
            s = sw["C"]

            def products_C(u):
                for h in range(H0):
                    pe.wait_ge(s["p_ok"], 4 * H0 + u.n * H0 + h + 1)
                    rhs_h = hW[0:u.kp, bass.ds(u.tile, 1), h * D:(h + 1) * D].rearrange("p a d -> p (a d)")
                    mms = [(bank(0, 6)[0:nr, (r * H0 + h) * D:(r * H0 + h + 1) * D], (r * H0 + h) // 2,
                            PA[0:u.kp, u.q, h, r * P:r * P + nr], rhs_h) for r, nr in enumerate(u.rows)]
                    for o, b, l, rr in mms:
                        ins = PE.matmul(o, l, rr, start=False, stop=False, skip_group_check=True)
                unit_done(u, ins, s, 6)
            pe_sweep(pe, "C", 6, products_C)
            stage_end(pe, "pe")
            pe.wait_ge(g_in, 128)
            n = 0
            for i in range(4):
                for kk in range(KD):
                    for g0 in (0, 3):
                        if n >= 4:
                            pe.wait_ge(g_wok, n - 3)
                        for g in range(g0, g0 + 3):
                            ins = PE.transpose(bank(n % 4)[:, (g - g0) * P:(g - g0 + 1) * P],
                                               g_wn[:, i, g, kk * P:(kk + 1) * P], ident)
                        ins.then_inc(g_wps, 1)
                        n += 1
            pe.wait_ge(g_wok, n)
            pe.sem_inc(g_tps, 2)

            def gate_tile(t, q, nr):
                pe.wait_ge(g_staged, t + 1)
                pe.wait_ge(g_tok, t + 1)
                for j in range(3):
                    for kk in range(KD):
                        i = j * KD + kk
                        ins = PE.transpose(bank(4, 2)[:, i * P:i * P + nr], st[0:nr, q, j, kk * P:(kk + 1) * P],
                                           ident[0:nr, 0:nr])
                ins.then_inc(g_tps, 1)
                pe.wait_ge(g_tok, t + 2)
                for g in range(2):
                    pe.wait_ge(g_pre, 2 * t + g + 1)
                    wi, wh = g_wT[:, 2 * g], g_wT[:, 2 * g + 1]
                    rz, nh = bank(2 * g)[0:nr], bank(2 * g + 1)[0:nr]
                    for kk in range(KD):
                        X, Hh = sT[:, q, g, kk, 0:nr], sT[:, q, 2, kk, 0:nr]
                        PE.matmul(rz, X, wi[:, kk, 0:2 * D], start=kk == 0, stop=False)
                        PE.matmul(rz, Hh, wh[:, kk, 0:2 * D], start=False, stop=kk == 1)
                        PE.matmul(nh[:, 0:D], X, wi[:, kk, 2 * D:3 * D], start=kk == 0, stop=False, skip_group_check=True)
                        ins = PE.matmul(nh[:, D:2 * D], Hh, wh[:, kk, 2 * D:3 * D], start=False, stop=kk == 1,
                                        skip_group_check=True)
                    ins.then_inc(g_ready, 1)
            tile_pairs(pe, gate_tile)
            stage_end(pe, "pe")
            stage_end(pe, "pe")
            s = sw["L1"]

            def products_1(u):
                pe.wait_ge(s["blk_in"][u.slot], u.loaded1)
                r1 = xd[0:u.kp, bass.ds(u.tile, 1), :].rearrange("p a d -> p (a d)")
                unit_done(u, accumulate(u, [(bank(0, 2)[0:nr, r * D:(r + 1) * D], r // 2,
                                             blk2[0:u.kp, u.slot, r, 0:nr], r1) for r, nr in enumerate(u.rows)]), s, 2)
            pe_sweep(pe, "L1", 2, products_1, ahead=4)
            stage_end(pe, "pe")
            pe.sem_inc(h1_ps, 2)

            def tile1(t, q, nr):
                pe.wait_ge(h1_st, t + 1)
                for kk in range(KD):
                    ins = PE.transpose(psT[q][:, kk * P:kk * P + nr], xs[0:nr, q, kk * P:(kk + 1) * P], ident[0:nr, 0:nr])
                ins.then_inc(h1_ps, 1)
                pe.wait_ge(h1_ok, t + 1)
                pe.wait_ge(h1_done, t + 1)
                for kk in range(KD):
                    ins = PE.matmul(bank(q)[0:nr, 0:D], xT[:, q, kk, 0:nr], w1T[:, kk, :], start=kk == 0, stop=kk == KD - 1)
                ins.then_inc(h1_mm, 1)
            tile_pairs(pe, tile1)
            stage_end(pe, "pe")
            pe_project(pe, 1, wcat2, D + 2 * H2)
            pe_sums(pe, 0)
            stage_end(pe, "pe")
            pe.wait_ge(fg_ok, 1)
            pe_rows("r2", smalls[:, 6, 0:H2 * T], H2)
            s2 = sw["L2"]

            def products_2(u):
                pe.wait_ge(st_ok, u.n + 1)
                for h in range(H2):
                    pe.wait_ge(s2["p_ok"], 2 * H2 + u.n * H2 + h + 1)
                    ins = PE.matmul(bank(h)[:, 0:u.w], stage_w[0:u.kp, u.q, h * C2:(h + 1) * C2],
                                    PM[0:u.kp, u.q, h, 0:u.w], start=False, stop=False)
                unit_done(u, ins, s2, H2)
                if u.end:
                    pe.wait_ge(den_dve, (u.c + 1) * T + 1)
                    pe.wait_ge(den_pool, (u.c + 1) * T + 2)
                    pe.wait_ge(den_out, u.c + 1)
                    for h in range(H2):
                        for r, nr in enumerate(u.rows):
                            i = r * H2 + h
                            ins = PE.matmul(bank(4)[0:nr, i:i + 1], S2[:, h, r * P:r * P + nr], ones[:, 0:1], start=True,
                                            stop=True)
                    ins.then_inc(den_ps, 1)
            pe_sweep(pe, "L2", H2, products_2)
            stage_end(pe, "pe")
            pe_back(pe, 0, rawT2, H2, C2)
            stage_end(pe, "pe")
            pe_project(pe, 2, wcat3, D + 2 * H3)
            pe_sums(pe, 1)
            stage_end(pe, "pe")
            pe.wait_ge(fg_ok, 2)
            pe_rows("r3", smalls[:, 6, 0:H3 * T], H3)
            s3 = sw["L3"]

            def products_3(u):
                for h in range(H3):
                    pe.wait_ge(s3["p_ok"], 2 * H3 + u.n * H3 + h + 1)
                    ins = PE.matmul(bank(h)[0:C3 + 1, 0:u.w], stage_w[0:u.kp, u.q, h * (C3 + 1):(h + 1) * (C3 + 1)],
                                    PM[0:u.kp, u.q, h, 0:u.w], start=False, stop=False)
                unit_done(u, ins, s3, H3)
            pe_sweep(pe, "L3", H3, products_3)
            stage_end(pe, "pe")
            pe_back(pe, 1, rawT3, H3, C3 + 1)
            stage_end(pe, "pe")

        def act_project(act, i):
            staged, xt_ps, xt_ok, proj_ps, proj_ok = projs[i]

            def tile(t, q, nr):
                act.wait_ge(xt_ps, t + 1)
                settle(act)
                S.copy(xs[0:nr, q, :], tl(xnat, t, nr)).then_inc(staged, 1)
                act.wait_ge(xt_ps, t + 3)
                act.wait_ge(proj_ps, t + 1)
                S.copy(xT[:, q, :, 0:nr], psT[q][:, 0:D].rearrange("p (k n) -> p k n", k=KD)[:, :, 0:nr]).then_inc(xt_ok, 1)
            act.sem_inc(proj_ps, 2)
            tile_pairs(act, tile)

        def act_rows(act, k, heads):
            act.wait_ge(rows[k][1], 1)
            dst, b = (d_s, 4) if k == "d" else (rows_s, 5)
            S.copy(dst[0:heads * T, :], bank(b)[0:heads * T, 0:P]).then_inc(rows[k][2], 1)

        def act_std(act, i):
            act.wait_ge(ln_var, i + 1)
            S.activation(rstd, rstd, ACT.Sqrt).then_inc(ln_std, 1)

        def act_copy_sweep(act):
            s = sw["A"]
            act.sem_inc(s["at_ok"], 2)
            for i in range(4):
                act.sem_inc(at_out[i], 16)

            def chunk(c, last):
                def step(u):
                    act.wait_ge(s["transposed"], u.n + 5)
                    act.wait_ge(s["mm_done"], u.n + 1)
                    act.wait_ge(at_out[u.slot], u.loaded1)
                    S.copy(AT[0:u.kp, u.slot, 0:u.w], psT[u.q][0:u.kp, 0:u.w]).then_inc(s["at_ok"], 1)
                    act.wait_ge(s["at_ok"], u.n + 3)
                    act.dma_start(adj_T[bass.ds(u.tile * P, u.kp), bass.ds(c * W, u.w)], AT[0:u.kp, u.slot, 0:u.w]
                                  ).then_inc(at_out[u.slot], 16)
                sweep_units(act, c, last, step)
            sweep_chunks(act, chunk)
            for i in range(4):
                act.wait_ge(at_out[i], 16 * (1 + (6 if i < 2 else 5) * CH))

        def act_ratio_sweep(act, k, heads, sm):
            s = sw[k]
            act.wait_ge(rows["r2" if k == "L2" else "r3"][4], 16 * heads)
            act.wait_ge(neg_ok, 1 if k == "L2" else 2)

            def chunk(c, last):
                def step(u):
                    if k == "L2":
                        act.wait_ge(s["mm_done"], u.n + 1)
                        settle(act)
                        S.copy(stage_w[0:u.kp, u.q, 0:D], proj[0:u.kp, bass.ds(u.tile, 1), 0:D].rearrange(
                            "p a d -> p (a d)")).then_inc(st_ok, 1)
                    for h in range(heads):
                        act.wait_ge(s["p_ok"], u.n * heads + h + 1)
                        settle(act)
                        S.activation(Y[0:u.kp, u.q, h, 0:u.w], r_bc[0:u.kp, h, bass.ds(c * W, u.w)], ACT.Relu,
                                     bias=sm[0:u.kp, 3, bass.ds(u.tile + h * T, 1)],
                                     scale=sm[0:u.kp, 5, bass.ds(u.tile + h * T, 1)]
                                     ).then_inc(s["y_ok"], 1)
                sweep_units(act, c, last, step)
            sweep_chunks(act, chunk)

        @block.scalar
        def _(act):
            act.wait_ge(w1T_ok, 1)
            S.copy(w1T.rearrange("p k f -> p (k f)"), bank(4)[:, 0:KD * D])
            stage_end(act, "act")
            act_project(act, 0)
            stage_end(act, "act")
            act_copy_sweep(act)
            stage_end(act, "act")
            act_rows(act, "e", H0)
            act_rows(act, "d", H0)

            def row_sum(t, q, nr):
                act.wait_ge(b_diag, t + 1)
                settle(act)
                S.activation(arow[0:nr, q, :], arow[0:nr, q, :], ACT.Copy, accum_out=rowsum[0:nr, bass.ds(t, 1)]
                             ).then_inc(b_sum, 1)
            row_sum(0, 0, P)

            def row_tile(t, q, nr):
                if not (isinstance(t, int) and t == T - 1):
                    row_sum(t + 1, 1 - q, P if not isinstance(t, int) else TAIL)
                for h in range(H0):
                    sl = (q * H0 + h) % 2
                    act.wait_ge(b_negm, H0 * t + h + 1)
                    settle(act)
                    S.activation(srow[0:nr, sl, :], srow[0:nr, sl, :], ACT.Exp, bias=col(negm, h, t, nr),
                                 accum_out=col(den, h, t, nr)).then_inc(b_exp, 1)
            tile_pairs(act, row_tile)
            act_rows(act, "m", H0)
            stage_end(act, "act")
            s = sw["C"]

            def chunk(c, last):
                def step(u):
                    act.wait_ge(c_arg, u.n + 2)
                    S.activation(E[0:u.kp, u.q, :, 0:u.w], E[0:u.kp, u.q, :, 0:u.w], ACT.Exp).then_inc(s["y_ok"], 1)
                sweep_units(act, c, last, step)
            sweep_chunks(act, chunk)
            stage_end(act, "act")
            n = 0
            for i in range(4):
                for kk in range(KD):
                    for g0 in (0, 3):
                        act.wait_ge(g_wps, n + 1)
                        S.copy(g_wT[:, i, kk, g0 * P:(g0 + 3) * P], bank(n % 4)[:, 0:3 * P]).then_inc(g_wok, 1)
                        n += 1
            act.sem_inc(g_tok, 1)

            def gate_tile(t, q, nr):
                act.wait_ge(g_tps, t + 3)
                act.wait_ge(g_ready, 2 * t + 1)
                S.copy(sT[:, q].rearrange("p j k n -> p (j k) n")[:, :, 0:nr],
                       bank(4, 2)[:, 0:3 * D].rearrange("p (i n) -> p i n", n=P)[:, :, 0:nr]).then_inc(g_tok, 1)
                for g in range(2):
                    act.wait_ge(g_pre, 2 * t + g + 3)
                    S.activation(g_th[0:nr], g_rz[0:nr], ACT.Tanh, scale=0.5).then_inc(g_thok, 1)
                    act.wait_ge(g_tok2, 2 * t + g + 1)
                    S.activation(g_n[0:nr], g_t[0:nr], ACT.Tanh).then_inc(g_nok, 1)
            act.sem_inc(g_ready, 3)
            tile_pairs(act, gate_tile)
            stage_end(act, "act")
            act_std(act, 0)
            act.wait_ge(deg_in, 1)
            S.activation(degs, degs, ACT.Sqrt).then_inc(deg_out, 1)
            stage_end(act, "act")
            stage_end(act, "act")

            def tile1(t, q, nr):
                act.wait_ge(h1_ps, t + 1)
                settle(act)
                S.copy(xs[0:nr, q, :], tl(raw1, t, nr)).then_inc(h1_st, 1)
                act.wait_ge(h1_ps, t + 3)
                act.wait_ge(h1_mm, t + 1)
                S.copy(xT[:, q, :, 0:nr], psT[q][:, 0:D].rearrange("p (k n) -> p k n", k=KD)[:, :, 0:nr]).then_inc(h1_ok, 1)
            act.sem_inc(h1_mm, 2)
            tile_pairs(act, tile1)
            act_std(act, 1)
            stage_end(act, "act")
            act_project(act, 1)
            stage_end(act, "act")

            def factors(i, heads):
                act.wait_ge(fg_in, i + 1)
                S.activation(smalls[:, 4:7, 0:heads * T], smalls[:, 0:3, 0:heads * T], ACT.Exp).then_inc(fg_ok, 1)
            factors(0, H2)
            act_rows(act, "r2", H2)
            act_ratio_sweep(act, "L2", H2, smalls)
            stage_end(act, "act")
            act.wait_ge(elu_in, 1)
            for nr, ts in FULL:
                ins = S.activation(tmp[0:nr, ts], tmp[0:nr, ts], ACT.Exp)
            ins.then_inc(elu_ok, 1)
            act_std(act, 2)
            stage_end(act, "act")
            act_project(act, 2)
            stage_end(act, "act")
            factors(1, H3)
            act_rows(act, "r3", H3)
            act_ratio_sweep(act, "L3", H3, smalls)
            stage_end(act, "act")
            act_std(act, 3)
            stage_end(act, "act")

        def dve_project(dve, i, dst, cols):
            staged, xt_ps, xt_ok, proj_ps, proj_ok = projs[i]
            dve.sem_inc(proj_ok, 2)

            def tile(t, q, nr):
                dve.wait_ge(proj_ps, t + 3)
                for b, (lo, hi) in enumerate(splits(cols)):
                    ins = V.tensor_copy(dst[0:nr, bass.ds(t, 1), lo:hi].rearrange("p a d -> p (a d)"),
                                        bank(2 * q + b)[0:nr, 0:hi - lo])
                ins.then_inc(proj_ok, 1)
            tile_pairs(dve, tile)
            dve.wait_ge(proj_ok, T + 2)

        def dve_norm(dve, link, i):
            def stats(t, q, nr):
                return V.bn_stats(bnst[0:nr, bass.ds(t, 1), :].rearrange("p a m -> p (a m)"), tl(xnat, t, nr))
            link(tile_pairs(dve, stats))
            for t in range(T):
                nr = P if t < T - 1 else TAIL
                ins = V.bn_aggr(mv[0:nr, t, :], bnst[0:nr, t, :])
            link(ins)
            V.tensor_scalar(rstd[:, 0:T - 1], mv[:, 0:T - 1, 1], EPS, None, ALU.add)
            V.tensor_scalar(rstd[0:TAIL, T - 1:T], mv[0:TAIL, T - 1:T, 1], EPS, None, ALU.add).then_inc(ln_var, 1)
            dve.wait_ge(ln_std, i + 1)
            link(V.reciprocal(rstd, rstd))

            def scale(t, q, nr):
                return V.tensor_scalar(tl(xnat, t, nr), tl(xnat, t, nr), mv[0:nr, bass.ds(t, 1), 0], rstd[0:nr, bass.ds(t, 1)],
                                ALU.subtract, ALU.mult)
            link(tile_pairs(dve, scale))

        def head_vector(link, wv, av, dst):
            _, hh, ff = wv.shape
            pv = prod[:, 0:hh * ff].rearrange("p (h f) -> p h f", h=hh)
            link(V.tensor_tensor(pv, wv, av, ALU.mult))
            link(V.tensor_reduce(dst, pv, AX_X, ALU.add))

        def node_sum(dve, link, i):
            link(V.tensor_reduce(part, proj[:, 0:T - 1, 0:D].rearrange("p t d -> p d t"), AX_X, ALU.add))
            V.tensor_tensor(part[0:TAIL], part[0:TAIL], proj[0:TAIL, T - 1, 0:D], ALU.add).then_inc(sx_in, 1)
            dve.wait_ge(sx_ok, i + 1)
            V.tensor_copy(sum_bc, bank(4)[:, 0:D])

        @block.vector
        def _(dve):
            link = Chain(dve, dve_link)
            V.memset(rstd, 1.0)
            V.memset(rowsum, 1.0)
            dve.wait_ge(const_ok, 1)
            dve.wait_ge(loaded, 16 * (2 + 4 * KD + 8))
            for kk in range(KD):
                w0 = wcat0[:, kk, 0:H0 * D].rearrange("p (h f) -> p h f", h=H0)
                w2 = wcat2[:, kk, 0:D].rearrange("p (h f) -> p h f", h=H2)
                w3 = wcat3[:, kk, 0:D].rearrange("p (h f) -> p h f", h=H3)
                for j in range(2):
                    head_vector(link, w0, a0_bc[:, :, j, :], wcat0[:, kk, H0 * D + j * H0:H0 * D + (j + 1) * H0])
                    head_vector(link, w2, a2_bc[:, :, j, :], wcat2[:, kk, D + j * H2:D + (j + 1) * H2])
                    head_vector(link, w3, a3_bc[:, j], wcat3[:, kk, D + j * H3:D + (j + 1) * H3])
            stage_end(dve, "dve")
            dve_project(dve, 0, hW, H0 * D + 2 * H0)
            for nr, ts in FULL:
                ins = V.tensor_copy(ur[0:nr, ts], hW[0:nr, ts, H0 * D:])
            link(ins)
            for part in range(3):
                for nr, ts in FULL:
                    ins = V.tensor_copy(ub[0:nr, ts, part, 0:2 * H0], ur[0:nr, ts])
                link(ins)
                for nr, ts in FULL:
                    V.tensor_copy(ub[0:nr, ts, part, 2 * H0:3 * H0], ub[0:nr, ts, part, 0:H0])
                    V.memset(ub[0:nr, ts, part, 3 * H0:], 1.0)
                    ins = V.tensor_tensor(ur[0:nr, ts], ur[0:nr, ts], ub[0:nr, ts, part, 0:2 * H0], ALU.subtract)
                link(ins)
            stage_end(dve, "dve")
            s = sw["A"]
            dve.sem_inc(s["acc_free"], 1)

            def chunkA(c, last):
                def step(u):
                    dve.wait_ge(s["at_ok"], u.n + 3)
                    dve.wait_ge(s["mm_done"], u.n + 1)
                    V.tensor_scalar(Mp[0:u.kp, u.q, 0:u.w], AT[0:u.kp, u.slot, 0:u.w], 0.0, None, ALU.is_gt)
                    V.tensor_scalar(Mm[0:u.kp, u.q, 0:u.w], AT[0:u.kp, u.slot, 0:u.w], 0.0, None, ALU.is_lt
                                    ).then_inc(s["mask_ok"], 1)
                sweep_units(dve, c, last, step)
                dve.wait_ge(s["mm_done"], (c + 1) * T + 2)
                empty(c, last, bank(0, 2), D, ns)
                empty(c, last, bank(2), 21, E21.rearrange("p t s h -> p t (s h)")).then_inc(s["acc_free"], 1)
            sweep_chunks(dve, chunkA)
            dve.wait_ge(s["acc_free"], CH + 1)
            for nr, ts in FULL:
                ev = e6[0:nr, :, ts].rearrange("p h t -> p t h")
                link(V.tensor_tensor(ur[0:nr, ts], E21[0:nr, ts, 2, 0:2 * H0], E21[0:nr, ts, 1, 0:2 * H0], ALU.add))
                link(V.tensor_tensor(ur[0:nr, ts], ur[0:nr, ts], E21[0:nr, ts, 0, 0:2 * H0], ALU.add))
                link(V.scalar_tensor_tensor(ev, ur[0:nr, ts], SLOPE, ur[0:nr, ts], ALU.mult, ALU.max))
            V.tensor_tensor(e_step, e6[:, H0:2 * H0, :], e6[:, 0:H0, :], ALU.subtract)
            link(V.tensor_reduce(cpart[:, 0:1], E21[:, 0:T - 1, 0, 2 * H0], AX_X, ALU.max))
            V.tensor_tensor(cpart[0:TAIL, 0:1], cpart[0:TAIL, 0:1], E21[0:TAIL, T - 1, 0, 2 * H0:], ALU.max
                            ).then_inc(neg_in, 1)
            dve.wait_ge(neg_all, 1)
            link(V.tensor_scalar(cpart[:, 0:1], cmax[:, 0:1], 0.0, None, ALU.is_gt))
            V.tensor_copy(has_neg_int, cpart[:, 0:1])
            stage_end(dve, "dve")
            V.memset(den.rearrange("p h t -> p (h t)"), 1.0)
            dve.wait_ge(rows["e"][4], 16 * H0)
            dve.sem_inc(b_rowfree, 2)
            dve.sem_inc(b_exp, 2)

            negative = dve.value_load(has_neg_int[0:1, 0:1])
            glink = Chain(dve, gen_link)

            def row_tile(t, q, nr, general=False):
                dve.wait_ge(b_diag, t + 1)
                dve.wait_ge(b_sum, t + 1)
                link(V.tensor_scalar(mbias[0:nr, :], arow[0:nr, q, :], 0.0, NEG, ALU.is_equal, ALU.mult))
                if not general:
                    dve.sem_inc(b_rowfree, 1)
                for h in range(H0):
                    sl = (q * H0 + h) % 2
                    dve.wait_ge(b_exp, H0 * t + h + 1)
                    settle(dve)
                    link(V.tensor_tensor_reduce(out=srow[0:nr, sl, :], in0=mbias[0:nr, :], in1=e_bc[0:nr, h, :], scale=1.0,
                                                scalar=3 * NEG, op0=ALU.add, op1=ALU.max, accum_out=mrow[0:nr, sl:sl + 1]))
                    if general:
                        for half in range(2):
                            cols = slice(half * (N // 2), (half + 1) * (N // 2))
                            dve.wait_ge(gen_in, 16 * ((t * H0 + h) * 2 + half + 1))
                            glink(V.scalar_tensor_tensor(d_bc[0:nr], arow[0:nr, q, cols], 0.0, d_bc[0:nr], ALU.is_lt,
                                                         ALU.mult))
                            glink(V.tensor_tensor(srow[0:nr, sl, cols], srow[0:nr, sl, cols], d_bc[0:nr], ALU.add))
                            dve.sem_inc(gen_free, 1)
                        glink(V.tensor_reduce(mrow[0:nr, sl:sl + 1], srow[0:nr, sl, :], AX_X, ALU.max))
                    V.tensor_scalar(col(negm, h, t, nr), mrow[0:nr, sl:sl + 1], -1.0, None, ALU.mult).then_inc(b_negm, 1)
                if general:
                    dve.sem_inc(b_rowfree, 1)
            with link.either():
                with dve.If(negative != 0):
                    dve.sem_inc(gen_free, 1)
                    tile_pairs(dve, lambda *a: row_tile(*a, general=True), (link, 1 + H0), (glink, 5 * H0))
            with dve.Else():
                tile_pairs(dve, row_tile, (link, 1 + H0))
            dve.wait_ge(b_exp, T * H0 + 2)
            link(V.reciprocal(den.rearrange("p h t -> p (h t)"), den.rearrange("p h t -> p (h t)")))
            link(V.tensor_scalar(den.rearrange("p h t -> p (h t)"), den.rearrange("p h t -> p (h t)"), 1.0 / H0, None,
                                 ALU.mult))
            stage_end(dve, "dve")
            s = sw["C"]
            dve.sem_inc(s["acc_free"], 1)
            dve.sem_inc(s["p_ok"], 4 * H0)

            dve.sem_inc(c_arg, 1)

            def chunkC(c, last, general):
                dve.wait_ge(mbc_in, 16 * H0 * (c + 1))

                def strip(u):
                    return blk[0:u.kp, u.slot].rearrange("p r n -> p (r n)")[:, 0:u.w]

                def exponents(u):
                    dve.wait_ge(s["p_ok"], u.n * H0 + 3 * H0)
                    if general:
                        dve.wait_ge(s["blk_in"][u.slot], u.loaded1)
                        for h in range(H0):
                            ins = V.tensor_scalar(E[0:u.kp, u.q, h, 0:u.w], strip(u), 0.0,
                                                  e_step[0:u.kp, h, bass.ds(u.tile, 1)], ALU.is_lt, ALU.mult)
                        ins.then_inc(gen_arg, 1)
                        dve.wait_ge(gen_arg, 2 * u.n + 1)
                        V.tensor_tensor(E[0:u.kp, u.q, :, 0:u.w], E[0:u.kp, u.q, :, 0:u.w], m_bc[0:u.kp, :, 0:u.w], ALU.add
                                        ).then_inc(gen_arg, 1)
                        dve.wait_ge(gen_arg, 2 * u.n + 2)
                    arg = E[:, u.q] if general else m_bc
                    for h in range(H0):
                        ins = V.tensor_scalar(E[0:u.kp, u.q, h, 0:u.w], arg[0:u.kp, h, 0:u.w],
                                              e6[0:u.kp, h, bass.ds(u.tile, 1)], 0.0, ALU.add, ALU.min)
                    ins.then_inc(c_arg, 1)

                def step(u):
                    dve.wait_ge(s["blk_in"][u.slot], u.loaded1)
                    dve.wait_ge(s["mm_done"], u.n + 1)
                    dve.wait_ge(s["y_ok"], u.n + 1)
                    for h in range(H0):
                        V.tensor_tensor(PA[0:u.kp, u.q, h, 0:u.w], E[0:u.kp, u.q, h, 0:u.w], strip(u), ALU.mult
                                        ).then_inc(s["p_ok"], 1)
                sweep_ahead(dve, c, last, exponents, step)
                dve.wait_ge(s["mm_done"], (c + 1) * T + 2)
                sizes = [P] * RPC if not last else [P, TAIL]
                for h in range(H0):
                    for r, nr in enumerate(sizes):
                        t = c * RPC + r
                        acc = bank(0, 6)[0:nr, (r * H0 + h) * D:(r * H0 + h + 1) * D]
                        if h == 0:
                            ins = V.tensor_scalar(tl(es, t, nr), acc, col(den, h, t, nr), None, ALU.mult)
                        else:
                            ins = V.scalar_tensor_tensor(tl(es, t, nr), acc, col(den, h, t, nr), tl(es, t, nr), ALU.mult,
                                                         ALU.add)
                    if h < H0 - 1:
                        link(ins)
                ins.then_inc(s["acc_free"], 1)
            def all_chunks(general):
                with dve.Fori(0, CH - 1) as c:
                    with link.loop(c, CH - 1, H0 - 1):
                        chunkC(c, False, general)
                chunkC(CH - 1, True, general)
            with link.either():
                with dve.If(negative != 0):
                    all_chunks(True)
            with dve.Else():
                all_chunks(False)
            stage_end(dve, "dve")
            dve.sem_inc(g_pre, 2)
            dve.wait_ge(g_in, 128)
            for g in range(2):
                V.tensor_tensor(g_brz[:, g], g_bias[:, 2 * g, 0:2 * D], g_bias[:, 2 * g + 1, 0:2 * D], ALU.add)
                V.tensor_copy(g_bnh[:, g, 0:D], g_bias[:, 2 * g, 2 * D:])
                ins = V.tensor_copy(g_bnh[:, g, D:], g_bias[:, 2 * g + 1, 2 * D:])
            link(ins)

            def gate_tile(t, q, nr):
                X = tl(xnat, t, nr)
                for g in range(2):
                    dve.wait_ge(g_ready, 2 * t + g + 4)
                    V.tensor_tensor(g_rz[0:nr], bank(2 * g)[0:nr], g_brz[0:nr, g], ALU.add)
                    V.tensor_tensor(g_nh[0:nr], bank(2 * g + 1)[0:nr], g_bnh[0:nr, g], ALU.add).then_inc(g_pre, 1)
                    dve.wait_ge(g_pre, 2 * t + g + 3)
                    dve.wait_ge(g_thok, 2 * t + g + 1)
                    link(V.scalar_tensor_tensor(g_q[0:nr], g_th[0:nr, 0:D], 1.0, g_nh[0:nr, D:2 * D], ALU.add, ALU.mult))
                    V.scalar_tensor_tensor(g_t[0:nr], g_q[0:nr], 0.5, g_nh[0:nr, 0:D], ALU.mult, ALU.add
                                           ).then_inc(g_tok2, 1)
                    dve.wait_ge(g_nok, 2 * t + g + 1)
                    link(V.tensor_tensor(g_d[0:nr], X, g_n[0:nr], ALU.subtract))
                    link(V.scalar_tensor_tensor(g_e[0:nr], g_th[0:nr, D:2 * D], 1.0, g_d[0:nr], ALU.add, ALU.mult))
                    link(V.scalar_tensor_tensor(g_out[0:nr, g], g_e[0:nr], 0.5, g_n[0:nr], ALU.mult, ALU.add))
                link(V.tensor_tensor(g_d[0:nr], g_out[0:nr, 0], g_out[0:nr, 1], ALU.add))
                dve.wait_ge(g_staged, t + 1)
                link(V.scalar_tensor_tensor(X, g_d[0:nr], dn[0:nr, bass.ds(t, 1)], X, ALU.mult, ALU.add))
            tile_pairs(dve, gate_tile, (link, 10))
            stage_end(dve, "dve")
            dve_norm(dve, link, 0)
            zero = smalls[:, 7, 0:T]
            for nr, ts in FULL:
                ins = V.tensor_tensor(rowsum[0:nr, ts], rowsum[0:nr, ts], dn[0:nr, ts], ALU.add)
            link(ins)
            link(V.tensor_scalar(zero, rowsum, 0.0, None, ALU.is_equal))
            dve.sem_inc(deg_in, 1)
            dve.wait_ge(deg_out, 1)
            link(V.tensor_tensor(rowsum, rowsum, zero, ALU.add))
            link(V.reciprocal(rowsum, rowsum))
            link(V.tensor_scalar(zero, zero, -1.0, 1.0, ALU.mult, ALU.add))
            link(V.tensor_tensor(rowsum, rowsum, zero, ALU.mult))
            r1v = xd

            def by_degree(t, q, nr):
                V.tensor_scalar(tl(r1v, t, nr), tl(xnat, t, nr), rowsum[0:nr, bass.ds(t, 1)], None, ALU.mult)
            tile_pairs(dve, by_degree)
            stage_end(dve, "dve")
            s1 = sw["L1"]
            dve.sem_inc(s1["acc_free"], 1)

            def chunk1(c, last):
                dve.wait_ge(s1["mm_done"], (c + 1) * T + 4)
                for r, nr in enumerate([P] * RPC if not last else [P, TAIL]):
                    t = c * RPC + r
                    ins = V.scalar_tensor_tensor(tl(raw1, t, nr), tl(xd, t, nr), dn[0:nr, bass.ds(t, 1)],
                                                 bank(0, 2)[0:nr, r * D:(r + 1) * D], ALU.mult, ALU.add)
                ins.then_inc(s1["acc_free"], 1)
            sweep_chunks(dve, chunk1)
            stage_end(dve, "dve")
            dve.sem_inc(h1_done, 2)
            for nr, ts in FULL:
                ins = V.tensor_tensor(xnat[0:nr, ts], xnat[0:nr, ts], b1_bc[0:nr].unsqueeze(1).to_broadcast(
                    [nr, ts.stop - ts.start, D]), ALU.add)
            link(ins)

            def tile1(t, q, nr):
                dve.wait_ge(h1_mm, t + 3)
                link(V.scalar_tensor_tensor(tl(xnat, t, nr), bank(q)[0:nr, 0:D], rowsum[0:nr, bass.ds(t, 1)],
                                            tl(xnat, t, nr), ALU.mult, ALU.add))
                dve.sem_inc(h1_done, 1)
            tile_pairs(dve, tile1, (link, 1))
            dve_norm(dve, link, 1)
            stage_end(dve, "dve")
            for i, (heads, cf) in enumerate(((H2, C2), (H3, C3))):
                k = "L2" if i == 0 else "L3"
                s = sw[k]
                dve_project(dve, i + 1, proj, D + 2 * heads)
                node_sum(dve, link, i)
                stage_end(dve, "dve")
                own, oth = (0, heads) if i == 0 else (heads, 0)
                sm = lambda j: smalls[:, j, 0:heads * T].rearrange("p (h t) -> p h t", h=heads)
                for nr, ts in FULL:
                    V.tensor_copy(sm(0)[0:nr, :, ts], proj[0:nr, ts, D + oth:D + oth + heads].rearrange("p t h -> p h t"))
                    ins = V.tensor_copy(sm(2)[0:nr, :, ts],
                                        proj[0:nr, ts, D + own:D + own + heads].rearrange("p t h -> p h t"))
                link(ins)
                link(V.tensor_reduce(cpart[:, 0:heads], sm(0)[:, :, 0:T - 1], AX_X, ALU.max))
                V.tensor_tensor(cpart[0:TAIL, 0:heads], cpart[0:TAIL, 0:heads], sm(0)[0:TAIL, :, T - 1], ALU.max
                                ).then_inc(cm_in, 1)
                dve.wait_ge(cm_ok, i + 1)
                cb = cmax[:, 0:heads].unsqueeze(2).to_broadcast([P, heads, T])
                link(V.tensor_tensor(sm(0), sm(0), cb, ALU.subtract))
                V.tensor_scalar(sm(1), sm(0), SLOPE, None, ALU.mult)
                link(V.tensor_tensor(sm(2), sm(2), cb, ALU.add))
                V.tensor_scalar(sm(2), sm(2), -(1.0 - SLOPE), None, ALU.mult).then_inc(fg_in, 1)
                dve.wait_ge(fg_ok, i + 1)
                V.tensor_scalar(sm(3), sm(4), -1.0, None, ALU.mult).then_inc(neg_ok, 1)
                dve.wait_ge(neg_ok, i + 1)
                if i == 1:
                    V.memset(stage_w.rearrange("p q m -> p (q m)"), 1.0)
                else:
                    for nr, ts in FULL:
                        V.tensor_scalar(dflag[0:nr, ts], dn[0:nr, ts], 1.0, 0.0, ALU.add, ALU.is_gt)
                    dve.sem_inc(s["mask_ok"], 4)
                    dve.sem_inc(den_out, 1)
                    dve.sem_inc(den_ps, 1)
                    dve.sem_inc(den_dve, 1)
                link(V.memset(cpart, 0.0))
                dve.sem_inc(s["acc_free"], 1)
                dve.sem_inc(s["p_ok"], 2 * heads)
                width = cf if i == 0 else cf + 1
                rawT = rawT2 if i == 0 else rawT3
                sv = stage_w.rearrange("p q (h m) -> p q h m", h=H3) if i == 1 else \
                    stage_w[:, :, 0:D].rearrange("p q (h m) -> p q h m", h=H2)

                def chunk(c, last):
                    def front(u):
                        if i == 0:
                            dve.wait_ge(s["blk_in"][u.slot], u.loaded1)
                            m = msk[0:u.kp, u.q, 0:u.w]
                            ins = V.tensor_scalar(m, blk2[0:u.kp, u.slot].rearrange("p r n -> p (r n)")[:, 0:u.w], 0.0,
                                                  None, ALU.is_gt)
                            if u.diag is not None:
                                ins.then_inc(s["diag_ok"], 1)
                                dve.wait_ge(s["diag_ok"], c * 4 + u.diag + 1)
                                nr = u.rows[u.diag]
                                mb = m[:, u.diag * P:u.diag * P + nr]
                                ins = V.scalar_tensor_tensor(mb, ident[0:nr, 0:nr], dflag[0:nr, bass.ds(u.tile, 1)], mb,
                                                             ALU.mult, ALU.add)
                            ins.then_inc(s["mask_ok"], 1)

                    def step(u):
                        if i == 0:
                            dve.wait_ge(s["mask_ok"], u.n + 5)
                            dve.wait_ge(s["mm_done"], u.n + 1)
                            dve.wait_ge(den_pool, u.n + 1)
                        else:
                            dve.wait_ge(s["mask_ok"], u.n + 5)
                            dve.wait_ge(s["mm_done"], u.n + 1)
                            V.tensor_copy(sv[0:u.kp, u.q, :, 0:cf], proj[0:u.kp, bass.ds(u.tile, 1), 0:D].rearrange(
                                "p a (h c) -> p (a h) c", h=heads))
                        for h in range(heads):
                            dve.wait_ge(s["y_ok"], u.n * heads + h + 1)
                            V.scalar_tensor_tensor(PM[0:u.kp, u.q, h, 0:u.w], Y[0:u.kp, u.q, h, 0:u.w],
                                                   smalls[0:u.kp, 4, bass.ds(u.tile + h * T, 1)],
                                                   msk[0:u.kp, u.q, 0:u.w], ALU.add, ALU.mult).then_inc(s["p_ok"], 1)

                    def tail(u):
                        if i == 0:
                            dve.wait_ge(den_dve, u.n + 1)
                            dve.wait_ge(s["p_ok"], 2 * H2 + u.n * H2 + H2)
                            V.tensor_tensor(S2[0:u.kp, 1, 0:u.w], S2[0:u.kp, 1, 0:u.w], PM[0:u.kp, u.q, 1, 0:u.w],
                                            ALU.add).then_inc(den_dve, 1)
                    if i == 0:
                        dve.wait_ge(den_ps, c + 1)
                        V.memset(S2[:, 1, :], 0.0).then_inc(den_zero, 1)
                        dve.wait_ge(den_zero, c + 1)
                        settle(dve)
                    sweep_ahead(dve, c, last, front, step, tail)
                    dve.wait_ge(s["mm_done"], (c + 1) * T + 2)
                    w = WL if last else W
                    for h in range(heads):
                        ins = V.tensor_copy(rawT[0:width, h, bass.ds(c * W, w)], bank(h)[0:width, 0:w])
                    ins.then_inc(s["acc_free"], 1)
                    if i == 0:
                        dve.wait_ge(den_ps, c + 2)
                        empty(c, last, bank(4), H2, den2).then_inc(den_out, 1)
                sweep_chunks(dve, chunk)
                stage_end(dve, "dve")
                zz = smalls[:, 7, 0:heads * T].rearrange("p (t h) -> p t h", h=heads)
                dd = smalls[:, 3, 0:heads * T].rearrange("p (t h) -> p t h", h=heads)
                t4 = tmp.rearrange("p t (h c) -> p t h c", h=heads)
                u4 = tmp2.rearrange("p t (h c) -> p t h c", h=heads)
                if i == 0:
                    link(V.tensor_copy(dd, den2))
                for t in range(T):
                    nr = P if t < T - 1 else TAIL
                    b4 = bank(t % 4)[0:nr, 0:heads * width].rearrange("p (h c) -> p h c", h=heads)
                    dve.wait_ge(back_ps[i], t + 1)
                    if i == 1:
                        V.tensor_copy(dd[0:nr, t, :].unsqueeze(2), b4[:, :, cf:cf + 1])
                    ins = V.tensor_copy(t4[0:nr, t], b4[:, :, 0:cf])
                    ins.then_inc(back_ok[i], 1)
                dve.wait_ge(back_ok[i], T)
                for nr, ts in FULL:
                    nt = ts.stop - ts.start
                    link(V.tensor_scalar(zz[0:nr, ts], dd[0:nr, ts], 0.0, None, ALU.is_equal))
                    link(V.scalar_tensor_tensor(dd[0:nr, ts], zz[0:nr, ts], float(N), dd[0:nr, ts], ALU.mult, ALU.add))
                    link(V.reciprocal(dd[0:nr, ts], dd[0:nr, ts]))
                    for h in range(heads):
                        mb = sum_bc[0:nr, h * cf:(h + 1) * cf].unsqueeze(1).to_broadcast([nr, nt, cf])
                        ins = V.tensor_tensor(u4[0:nr, ts, h], zz[0:nr, ts, h].unsqueeze(2).to_broadcast([nr, nt, cf]),
                                              mb, ALU.mult)
                    link(ins)
                    link(V.tensor_tensor(tmp[0:nr, ts], tmp[0:nr, ts], tmp2[0:nr, ts], ALU.add))
                    for h in range(heads):
                        ins = V.tensor_tensor(t4[0:nr, ts, h], t4[0:nr, ts, h],
                                              dd[0:nr, ts, h].unsqueeze(2).to_broadcast([nr, nt, cf]), ALU.mult)
                    link(ins)
                if i == 0:
                    dve.sem_inc(h2_made, 1)
                    dve.wait_ge(h2_back, 32)
                    for nr, ts in FULL:
                        a, b = tmp[0:nr, ts], tmp2[0:nr, ts]
                        link(V.tensor_scalar(b, a, 0.0, -1.0, ALU.max, ALU.add))
                        link(V.tensor_tensor(xnat[0:nr, ts], xnat[0:nr, ts], b, ALU.add))
                    for nr, ts in FULL:
                        ins = V.tensor_scalar(tmp[0:nr, ts], tmp[0:nr, ts], 0.0, None, ALU.min)
                    ins.then_inc(elu_in, 1)
                    dve.wait_ge(elu_ok, 1)
                for nr, ts in FULL:
                    ins = V.tensor_tensor(xnat[0:nr, ts], xnat[0:nr, ts], tmp[0:nr, ts], ALU.add)
                link(ins)
                if i == 1:
                    for nr, ts in FULL:
                        ins = V.tensor_tensor(xnat[0:nr, ts], xnat[0:nr, ts], b3_bc[0:nr].unsqueeze(1).to_broadcast(
                            [nr, ts.stop - ts.start, D]), ALU.add)
                    link(ins)
                dve_norm(dve, link, 2 + i)
                stage_end(dve, "dve")


_OUT = (N, D)
_NAMES = ["x", "adj", "L0_gnn_gat_W", "L0_gnn_gat_a", "L0_gnn_edge_Wih", "L0_gnn_edge_Whh", "L0_gnn_edge_bih",
          "L0_gnn_edge_bhh", "L0_gnn_node_Wih", "L0_gnn_node_Whh", "L0_gnn_node_bih", "L0_gnn_node_bhh", "L1_gnn_W",
          "L1_gnn_b", "L2_gnn_W", "L2_gnn_a", "L3_gnn_W", "L3_gnn_a_src", "L3_gnn_a_dst", "L3_gnn_bias"]


def kernel(**inputs):
    import concourse.bacc as bacc
    from concourse.bass_utils import run_bass_kernel_spmd

    nc = bacc.Bacc("TRN2", target_bir_lowering=False, num_devices=1)
    arrays, args = {}, []
    for name in _NAMES:
        a = np.ascontiguousarray(inputs[name])
        arrays[f"in_{name}"] = a
        args.append(nc.dram_tensor(f"in_{name}", a.shape, mybir.dt.from_np(a.dtype), kind="ExternalInput").ap())
    args.append(nc.dram_tensor("out_x", _OUT, F32, kind="ExternalOutput").ap())
    build(nc, *args)
    r = run_bass_kernel_spmd(nc, [arrays], core_ids=[0])
    return r.results[0]["out_x"]
```

```python
from contextlib import ExitStack, contextmanager

import numpy as np

import concourse.bass as bass
from concourse import mybir

F32 = mybir.dt.float32
BF16 = mybir.dt.bfloat16
I32 = mybir.dt.int32
ALU = mybir.AluOpType
ACT = mybir.ActivationFunctionType
AX_X = mybir.AxisListType.X
RMAX = bass.bass_isa.ReduceOp.max

P = 128
N = 2708
D = 256
KD = D // P
T = -(-N // P)
TAIL = N - (T - 1) * P
RPC = 4
W = RPC * P
CH = -(-T // RPC)
WL = N - (CH - 1) * W
QUADS = T // 4
LOADS = (QUADS + 1) // 2
H0, H2, H3 = 3, 2, 4
C2, C3 = D // H2, D // H3
NEG = -1e30
EPS = 1e-5
SLOPE = 0.2


class Unit:

    def __init__(self, c, last, n, tile, slot, k, diag, end):
        self.c, self.last, self.n, self.tile, self.slot, self.k, self.diag, self.end = c, last, n, tile, slot, k, diag, end
        self.q = slot % 2
        self.kp = TAIL if (isinstance(tile, int) and tile == T - 1) else P
        self.w = WL if last else W
        self.rows = [P] * RPC if not last else [P, TAIL]
        uses = 6 if slot < 2 else 5
        self.loaded = 16 * (uses * c + k + 1)
        self.first = last or (isinstance(k, int) and k == 0)

    def slot_free(self):
        return self.n + 3 if (self.first and self.slot < 2) else self.n + 1


def sweep_chunks(eng, body):
    with eng.Fori(0, CH - 1) as c:
        body(c, False)
    body(CH - 1, True)


def sweep_units(eng, c, last, step):
    base = c * T
    if not last:
        for u in range(4):
            step(Unit(c, last, base + u, c * 4 + u, u, 0, u, False))
        with eng.Fori(1, QUADS) as k:
            for u in range(4):
                step(Unit(c, last, base + k * 4 + u, ((c + k) % QUADS) * 4 + u, u, k, None, False))
    else:
        with eng.Fori(0, QUADS) as k:
            for u in range(4):
                step(Unit(c, last, base + k * 4 + u, k * 4 + u, u, k, None, False))
    for u in range(2):
        step(Unit(c, last, base + 4 * QUADS + u, 4 * QUADS + u, u, QUADS, u if last else None, u == 1))


def run_ahead(units, front, step, tail=None):
    front(units[0])
    for i, u in enumerate(units):
        if tail:
            step(u)
        if i + 1 < len(units):
            front(units[i + 1])
        (tail or step)(u)


def sweep_ahead(eng, c, last, front, step, tail=None):
    def run(units):
        run_ahead(units, front, step, tail)

    base = c * T
    if not last:
        run([Unit(c, last, base + v, c * 4 + v, v, 0, v, False) for v in range(4)])
        with eng.Fori(1, QUADS) as k:
            run([Unit(c, last, base + k * 4 + v, ((c + k) % QUADS) * 4 + v, v, k, None, False) for v in range(4)])
    else:
        with eng.Fori(0, QUADS) as k:
            run([Unit(c, last, base + k * 4 + v, k * 4 + v, v, k, None, False) for v in range(4)])
    run([Unit(c, last, base + 4 * QUADS + v, 4 * QUADS + v, v, QUADS, v if last else None, v == 1) for v in range(2)])


def load_units(c, last, k, wide, turn):
    pair = isinstance(k, int) and k == QUADS
    out = []
    for v in range(2 if pair else 4):
        tile = k * 4 + v if last or pair else ((c + k) % QUADS) * 4 + v
        diag = v if (pair if last else isinstance(k, int) and k == 0) else None
        u = Unit(c, last, c * T + k * 4 + v, tile, v, k, diag, pair and v == 1)
        u.wide = wide
        u.wide_loaded = 16 * LOADS * c + (32 if last else 16) * (turn + 1)
        out.append(u)
    return out


def sweep_wide(eng, c, last, run):
    run(load_units(c, last, 0, 0, 0))
    with eng.Fori(0, LOADS - 1) as m:
        run(load_units(c, last, m * 2 + 1, 1, m) + load_units(c, last, m * 2 + 2, 0, m + 1))
    run(load_units(c, last, QUADS, 1, LOADS - 1))


def tile_pairs(eng, step, *chains):
    with eng.Fori(0, T // 2 - 1) as g:
        with ExitStack() as counts:
            for chain, links in chains:
                counts.enter_context(chain.loop(g, T // 2 - 1, 2 * links))
            for q in range(2):
                step(g * 2 + q, q, P)
    for q in range(2):
        ins = step(T - 2 + q, q, P if q == 0 else TAIL)
    return ins


def pairs_ahead(eng, first, step, *chains):
    def both(t, q, nr):
        if not isinstance(t, int) or t < T - 1:
            first(t + 1, 1 - q, TAIL if isinstance(t, int) else P)
        return step(t, q, nr)
    first(0, 0, P)
    return tile_pairs(eng, both, *chains)


class Chain:

    def __init__(self, eng, sem):
        self.eng, self.sem, self.base, self.local = eng, sem, 0, 0

    def __call__(self, ins):
        ins.then_inc(self.sem, 1)
        self.local += 1
        self.eng.wait_ge(self.sem, self.base + self.local)

    @contextmanager
    def loop(self, turn, turns, links):
        before = self.base + self.local
        self.base, self.local = before + turn * links, 0
        yield
        assert self.local == links, (self.local, links)
        self.base, self.local = before + turns * links, 0

    @contextmanager
    def either(self):
        before = self.base, self.local
        yield
        self.base, self.local = before


FULL = ((P, slice(0, T - 1)), (TAIL, slice(T - 1, T)))


def build(nc, x, adj, gat_W, gat_a, e_Wih, e_Whh, e_bih, e_bhh, n_Wih, n_Whh, n_bih, n_bhh,
          W1, b1, W2, a2, W3, a_src, a_dst, b3, out):
    V, S, G, PE = nc.vector, nc.scalar, nc.gpsimd, nc.tensor
    e_rows = nc.dram_tensor("e_rows", (H0, T * P), F32).ap()
    d_rows = nc.dram_tensor("d_rows", (H0, T * P), F32).ap()
    m_rows = nc.dram_tensor("m_rows", (H0, T * P), F32).ap()
    r2_rows = nc.dram_tensor("r2_rows", (H2, T * P), F32).ap()
    r3_rows = nc.dram_tensor("r3_rows", (H3, T * P), F32).ap()

    adj_T = nc.dram_tensor("adj_T", (N, N), F32).ap()

    support = nc.dram_tensor("support", (N, D), F32).ap()

    heads2 = nc.dram_tensor("heads2", (H2 * N, C2), F32).ap()

    with ExitStack() as ctx:
        ARENA = 53000
        arena = ctx.enter_context(nc.sbuf_tensor("arena", [P, ARENA], F32))
        psum = ctx.enter_context(nc.psum_tensor("banks", [P, 8, 512], F32))
        top = [0]

        def sb(*shape, dt=F32):
            n = int(np.prod(shape))
            words = n if dt == F32 else (n + 1) // 2
            a = arena[:, top[0]:top[0] + words]
            top[0] += words + words % 2
            assert top[0] <= ARENA, top[0]
            if dt != F32:
                a = a.bitcast(dt)
            if len(shape) > 1:
                names = "abcd"[:len(shape)]
                a = a.rearrange(f"p ({' '.join(names)}) -> p {' '.join(names)}", **dict(zip(names, shape)))
            return a

        def sem(name):
            return ctx.enter_context(nc.semaphore(name))

        ident = sb(P)
        noteye = sb(P)
        ones = sb(P)
        zrow = sb(W, dt=BF16)
        xnat = sb(T, D)
        dn = sb(T)
        rowsum = sb(T)
        mv = sb(T, 2)
        rstd = sb(T)
        bnst = sb(T, 6)
        mrow = sb(2)
        wcat0 = sb(KD, H0 * D + 2 * H0)
        wcat2 = sb(KD, D + 2 * H2)
        wcat3 = sb(KD, D + 2 * H3)
        w1T = sb(KD, D)
        b1_bc = sb(D)
        b3_bc = sb(D)
        xs = sb(2, D)
        xT = sb(2, KD, P)
        rows_s = sb(P)
        smalls = sb(8, T * H3)
        sum_bc = sb(D)
        part = sb(D)
        cpart = sb(H3)
        dflag = sb(T)
        cmax = sb(H3)
        has_neg = sb(1)
        has_neg_int = has_neg.bitcast(I32)
        stage_base = top[0]

        a0_bc = sb(H0, 2, D)
        a2_bc = sb(H2, 2, C2)
        a3_bc = sb(2, H3, C3)
        prod = sb(D * H0)
        w1n = sb(KD, D)
        top[0] = stage_base
        hW = sb(T, H0 * D + 2 * H0)
        ns = sb(T, D)
        ub_at = top[0]
        ub = sb(T, 3, 3 * H0 + 1, dt=BF16)
        E21 = sb(T, 3, 2 * H0 + 1)
        e6 = sb(2 * H0, T)
        e_step = sb(H0, T)
        d_s = sb(P)
        negm = sb(H0, T)
        den = sb(H0, T)
        ur = sb(T, 2 * H0)
        l0_base = top[0]
        wide = sb(2, RPC, 4 * P)
        AT = sb(4, W)
        Mp = sb(2, W, dt=BF16)
        Mm = sb(2, W, dt=BF16)
        top[0] = l0_base
        d_bc = arena[:, ub_at:ub_at + N // 4]
        assert ub_at + N // 4 <= ub_at + T * 3 * (3 * H0 + 1) // 2 + T * 3 * (2 * H0 + 1)
        strips = [xs.rearrange("p q d -> p (q d)"), xT.rearrange("p q k n -> p (q k n)")]
        support_s = wcat0.rearrange("p k n -> p (k n)")[:, 0:RPC * D]
        e_bc = sb(H0, N)
        arow = sb(2, N)
        mbias = sb(N, dt=BF16)
        strips += [sb(W), sb(W)]
        srow = ns.rearrange("p t d -> p (t d)")[:, 0:2 * N].rearrange("p (s n) -> p s n", s=2)
        top[0] = l0_base
        blk = sb(4, RPC, P)
        m_bc = sb(H0, W)
        E = sb(2, H0, W)
        PA = sb(2, H0, W)
        es = sb(T, D)
        top[0] = stage_base
        g_wT = sb(4, KD, 3 * D)
        g_bias = sb(4, 3 * D)
        g_wn = sb(4, 6, D)
        assert top[0] <= stage_base + T * (H0 * D + 2 * H0)
        top[0] = l0_base
        g_brz = sb(2, 2 * D)
        g_bnh = sb(2, 2 * D)
        st = sb(2, 3, D)
        sT = sb(2, 3, KD, P)
        g_rz = sb(2 * D)
        g_nh = sb(2 * D)
        g_th = sb(2 * D)
        g_q = sb(D)
        g_t = sb(D)
        g_n = sb(D)
        g_d = sb(D)
        g_e = sb(D)
        g_out = sb(2, D)
        assert top[0] <= l0_base + 4 * RPC * P + H0 * W + 4 * H0 * W, top[0]
        top[0] = stage_base
        xd = sb(T, D)
        raw1 = sb(T, D)
        proj = sb(T, D + 2 * H3)
        blk2 = sb(4, RPC, P)
        msk = sb(2, W, dt=BF16)
        stage_w = sb(2, H3 * (C3 + 1))
        S2 = sb(H2, W)
        den2 = sb(T, H2)
        free_from = top[0]
        r_bc = sb(H3, N)
        Y = sb(2, H3, W)
        PM = sb(2, H3, W)
        end_of_3 = top[0]
        top[0] = stage_base
        rawT2 = sb(H2, N)
        top[0] = stage_base
        rawT3 = sb(H3, N)
        assert top[0] <= stage_base + 2 * T * D
        top[0] = free_from
        tmp = sb(T, D)
        tmp2 = sb(T, D)
        assert top[0] <= end_of_3

        def bank(i, n=1):
            return psum[:, i:i + n, :].rearrange("p b n -> p (b n)")

        psT = [bank(6), bank(7)]

        waits_seen = sem("waits_seen")
        loaded, support_in, support_out = sem("loaded"), sem("support_in"), sem("support_out")
        const_ok = sem("const_ok")
        stage_done = sem("stage_done")
        dve_link, pool_link = sem("dve_link"), sem("pool_link")
        w1T_ok = sem("w1T_ok")
        projs = [[sem(f"l{l}_{s}") for s in ("staged", "xt_ps", "xt_ok", "proj_ps", "proj_ok")] for l in (0, 2, 3)]
        rows = {k: [None] + [sem(f"{k}_{s}") for s in ("ps", "sb", "dram", "bc")[0:3 if k in "dm" else 4]] for k in ("e", "d", "m", "r2", "r3")}
        steps = dict(A="transposed diag_ok at_ok mask_ok", C="y_ok p_ok", L1="",
                     B="", L2="diag_ok mask_ok y_ok p_ok", L3="mask_ok y_ok p_ok")
        rest_bc = {k: sem(f"{k}_rest_bc") for k in ("r2", "r3")}
        sw = {k: dict(blk_in=[sem(f"{k}_blk_in{i}") for i in range(2 if k == "A" else 4)],
                      **{s: sem(f"{k}_{s}") for s in (names + " mm_done acc_free").split()})
              for k, names in steps.items()}
        sw["A"]["wide_in"] = sw["A"].pop("blk_in")
        at_out = [sem(f"at_out{i}") for i in range(4)]
        st_ok = sem("st_ok")
        b_in = [sem(f"b_in{i}") for i in range(2)]
        b_diag, b_rowfree, b_s, b_negm, b_exp = (sem(f"b_{s}") for s in ("diag", "rowfree", "s", "negm", "exp"))
        b_sum = sem("b_sum")
        gen_arg, neg_in, neg_all, gen_in, gen_free, gen_link = (sem(s) for s in ("gen_arg", "neg_in", "neg_all", "gen_in", "gen_free", "gen_link"))
        mbc_in, c_arg = sem("mbc_in"), sem("c_arg")
        g_in, g_wps, g_wok = sem("g_in"), sem("g_wps"), sem("g_wok")
        g_staged, g_tps, g_tok, g_ready, g_pre, g_thok, g_tok2, g_nok = (
            sem(f"g_{s}") for s in ("staged", "tps", "tok", "ready", "pre", "thok", "tok2", "nok"))
        ln_var = sem("ln_var")
        ln_std = sem("ln_std")
        deg_in, deg_out = sem("deg_in"), sem("deg_out")
        h1_st, h1_ps, h1_ok, h1_mm, h1_done = (sem(f"h1_{s}") for s in ("st", "ps", "ok", "mm", "done"))
        cm_in = sem("cm_in")
        cm_ok = sem("cm_ok")
        fg_in = sem("fg_in")
        fg_ok = sem("fg_ok")
        neg_ok, den_zero = sem("neg_ok"), sem("den_zero")
        elu_in, elu_ok = sem("elu_in"), sem("elu_ok")
        sx_in = sem("sx_in")
        sx_ok = sem("sx_ok")
        stored = sem("stored")
        den_dve, den_pool, den_out, den_ps = (sem(f"den_{s}") for s in ("dve", "pool", "out", "ps"))
        back_ps = [sem(f"back_ps{i}") for i in range(2)]
        back_ok = [sem(f"back_ok{i}") for i in range(2)]
        h2_made, h2_out, h2_back = sem("h2_made"), sem("h2_out"), sem("h2_back")

        barriers = {}

        def stage_end(eng, name):
            barriers[name] = barriers.get(name, 0) + 1
            eng.drain().then_inc(stage_done, 1)
            eng.wait_ge(stage_done, 5 * barriers[name])

        def settle(eng):
            eng.sem_inc(waits_seen, 1)

        def load(eng, dst, src, s):
            eng.dma_start(dst, src).then_inc(s, 16)

        def load_nodes(eng, dst, src, s):
            load(eng, dst[:, 0:T - 1, :], src[0:(T - 1) * P, :].rearrange("(t p) d -> p t d", p=P), s)
            load(eng, dst[0:TAIL, T - 1, :], src[(T - 1) * P:N, :], s)

        def tl(a, t, nr):
            if isinstance(t, int):
                return a[0:nr, t, :]
            return a[0:nr, bass.ds(t, 1), :].rearrange("p a d -> p (a d)")

        def col(a, h, t, nr):
            return a[0:nr, h, bass.ds(t, 1)]

        def empty(c, last, acc, width, dst):
            if not last:
                return V.tensor_copy(dst[:, bass.ds(c * RPC, RPC), :], acc[:, 0:RPC * width].rearrange(
                    "p (r d) -> p r d", r=RPC))
            V.tensor_copy(dst[:, c * RPC, :], acc[:, 0:width])
            return V.tensor_copy(dst[0:TAIL, c * RPC + 1, :], acc[0:TAIL, width:2 * width])

        def wide_block(u, r, nr, w):
            return wide[0:nr, u.wide, r, u.slot * P:u.slot * P + w]

        def sp_blocks(sp):
            s = sw["A"]

            def chunk(c, last):
                def run(us):
                    for u in us:
                        if u.slot:
                            continue
                        sp.wait_ge(s["transposed"], u.n + 2 if isinstance(u.k, int) and u.k == 0 else u.n)
                        w = 4 * P if not (isinstance(u.k, int) and u.k == QUADS) else P + TAIL
                        col = bass.ds(u.tile * P, w)
                        if not last:
                            load(sp, wide[:, u.wide, :, 0:w], adj[bass.ds(c * W, W), col].rearrange("(r p) n -> p r n", p=P),
                                 s["wide_in"][u.wide])
                        else:
                            for r, nr in enumerate(u.rows):
                                load(sp, wide[0:nr, u.wide, r, 0:w], adj[c * W + r * P:c * W + r * P + nr, col],
                                     s["wide_in"][u.wide])
                sweep_wide(sp, c, last, run)
            sweep_chunks(sp, chunk)

        def strip_of(k, u):
            if k == "B":
                return strips[u.slot][0:u.kp, 0:u.w]
            return (blk if k == "C" else blk2)[0:u.kp, u.slot].rearrange("p r n -> p (r n)")[:, 0:u.w]

        def sp_strips(sp, k, matrix, used, per=1):
            s = sw[k]

            def chunk(c, last):
                def step(u):
                    sp.wait_ge(used, per * u.slot_free())
                    load(sp, strip_of(k, u), matrix[bass.ds(u.tile * P, u.kp), bass.ds(c * W, u.w)], s["blk_in"][u.slot])
                sweep_units(sp, c, last, step)
            sweep_chunks(sp, chunk)

        def sp_rows(sp, k, dram, heads, bc):
            sp.wait_ge(rows[k][2], 1)
            load(sp, dram.rearrange("h (t p) -> (h t) p", p=P), (d_s if k == "d" else rows_s)[0:heads * T, :], rows[k][3])
            sp.wait_ge(rows[k][3], 16)
            if k in ("r2", "r3"):
                load(sp, bc[:, :, 0:W], dram[:, 0:W].partition_broadcast(P), rows[k][4])
                load(sp, bc[:, :, W:N], dram[:, W:N].partition_broadcast(P), rest_bc[k])
            elif bc is not None:
                for h in range(heads):
                    load(sp, bc[:, h, :], dram[h:h + 1, 0:N].partition_broadcast(P).rearrange("p a n -> p (a n)"),
                         rows[k][4])

        block = ctx.enter_context(nc.Block())

        @block.sync
        def _(sp):
            load_nodes(sp, xnat, x, loaded)
            for kk in range(KD):
                f = slice(kk * P, (kk + 1) * P)
                load(sp, wcat0[:, kk, 0:H0 * D].rearrange("p (h f) -> p h f", h=H0),
                     gat_W[:, f, :].rearrange("h k f -> k h f"), loaded)
                load(sp, wcat2[:, kk, 0:D].rearrange("p (h f) -> p h f", h=H2), W2[:, f, :].rearrange("h k f -> k h f"),
                     loaded)
                load(sp, wcat3[:, kk, 0:D], W3[f, :], loaded)
                load(sp, w1n[:, kk, :], W1[f, :], loaded)
            flat = lambda a: a.partition_broadcast(P)
            load(sp, a0_bc.rearrange("p h s f -> p (h s f)"), flat(gat_a.rearrange("h f o -> (h f o)")), loaded)
            load(sp, a2_bc.rearrange("p h s f -> p (h s f)"), flat(a2.rearrange("h f o -> (h f o)")), loaded)
            load(sp, a3_bc[:, 0].rearrange("p h f -> p (h f)"), flat(a_src.rearrange("h f -> (h f)")), loaded)
            load(sp, a3_bc[:, 1].rearrange("p h f -> p (h f)"), flat(a_dst.rearrange("h f -> (h f)")), loaded)
            load(sp, b1_bc, flat(b1), loaded)
            load(sp, b3_bc, flat(b3), loaded)
            diag = bass.AP(adj.tensor, 0, [[N + 1, P], [P * (N + 1), T - 1], [1, 1]])
            sp.dma_start(dn[:, 0:T - 1].unsqueeze(2), diag, allow_slow_non_contiguous=True).then_inc(loaded, 16)
            diag_tail = bass.AP(adj.tensor, (T - 1) * P * (N + 1), [[N + 1, TAIL], [1, 1]])
            sp.dma_start(dn[0:TAIL, T - 1:T], diag_tail, allow_slow_non_contiguous=True).then_inc(loaded, 16)
            stage_end(sp, "sp")
            stage_end(sp, "sp")
            sp_blocks(sp)
            stage_end(sp, "sp")
            sp_rows(sp, "e", e_rows, H0, e_bc)
            sp_rows(sp, "d", d_rows, H0, None)
            sp_strips(sp, "B", adj_T, sw["B"]["mm_done"])
            sp_rows(sp, "m", m_rows, H0, None)
            stage_end(sp, "sp")
            load_nodes(sp, ns, support, support_in)
            s = sw["C"]

            def chunk(c, last):
                w = WL if last else W
                sp.wait_ge(c_arg, c * T + 1)
                for h in range(H0):
                    load(sp, m_bc[:, h, 0:w],
                         m_rows[h:h + 1, bass.ds(c * W, w)].partition_broadcast(P).rearrange("p a n -> p (a n)"), mbc_in)

                def step(u):
                    sp.wait_ge(s["p_ok"], H0 * u.slot_free())
                    load(sp, blk[0:u.kp, u.slot].rearrange("p r n -> p (r n)")[:, 0:w],
                         adj_T[bass.ds(u.tile * P, u.kp), bass.ds(c * W, w)], s["blk_in"][u.slot])
                sweep_units(sp, c, last, step)
            sweep_chunks(sp, chunk)
            sp.wait_ge(support_in, 32)
            stage_end(sp, "sp")
            for i, (w, b) in enumerate(((e_Wih, e_bih), (e_Whh, e_bhh), (n_Wih, n_bih), (n_Whh, n_bhh))):
                load(sp, g_wn[:, i], w.rearrange("(g p) k -> p g k", p=P), g_in)
                load(sp, g_bias[:, i], b.partition_broadcast(P), g_in)
            stage_end(sp, "sp")
            stage_end(sp, "sp")
            sp_strips(sp, "L1", adj_T, sw["L1"]["mm_done"])
            stage_end(sp, "sp")
            stage_end(sp, "sp")
            stage_end(sp, "sp")
            sp_rows(sp, "r2", r2_rows, H2, r_bc[:, 0:H2])
            sp_strips(sp, "L2", adj_T, sw["L2"]["mask_ok"])
            stage_end(sp, "sp")
            sp.wait_ge(h2_made, 1)
            for h in range(H2):
                f = slice(h * C2, (h + 1) * C2)
                load(sp, heads2[h * N:h * N + (T - 1) * P, :].rearrange("(t p) c -> p t c", p=P), tmp[:, 0:T - 1, f], h2_out)
                load(sp, heads2[h * N + (T - 1) * P:(h + 1) * N, :], tmp[0:TAIL, T - 1, f], h2_out)
            sp.wait_ge(h2_out, 16 * 2 * H2)
            load_nodes(sp, tmp, heads2.rearrange("(n g) c -> n (g c)", g=H2), h2_back)
            stage_end(sp, "sp")
            stage_end(sp, "sp")
            sp_rows(sp, "r3", r3_rows, H3, r_bc)
            sp_strips(sp, "L3", adj, sw["L3"]["mask_ok"])
            stage_end(sp, "sp")
            stage_end(sp, "sp")
            sp.dma_start(out[0:(T - 1) * P, :].rearrange("(t p) d -> p t d", p=P), xnat[:, 0:T - 1, :]).then_inc(stored, 16)
            sp.dma_start(out[(T - 1) * P:N, :], xnat[0:TAIL, T - 1, :]).then_inc(stored, 16)
            sp.wait_ge(stored, 32)

        def pool_diag(pool):
            s = sw["A"]

            def chunk(c, last):
                for u in load_units(c, last, QUADS, 1, LOADS - 1) if last else load_units(c, last, 0, 0, 0):
                    pool.wait_ge(s["wide_in"][u.wide], u.wide_loaded)
                    nr = u.rows[u.diag]
                    b = wide_block(u, u.diag, nr, nr)
                    G.tensor_tensor(b, b, noteye[0:nr, 0:nr], ALU.mult).then_inc(s["diag_ok"], 1)
            sweep_chunks(pool, chunk)

        @block.gpsimd
        def _(pool):
            link = Chain(pool, pool_link)
            G.memset(ones, 1.0)
            G.memset(zrow, 0.0)
            G.memset(ident, 0.0)
            link(G.memset(noteye, 1.0))
            G.affine_select(out=ident, in_=ident, compare_op=ALU.not_equal, fill=1.0, base=0, pattern=[[-1, P]],
                            channel_multiplier=1)
            G.affine_select(out=noteye, in_=noteye, compare_op=ALU.not_equal, fill=0.0, base=0, pattern=[[-1, P]],
                            channel_multiplier=1).then_inc(const_ok, 1)
            stage_end(pool, "pool")
            G.memset(e6, 0.0)
            G.memset(negm, 0.0)
            stage_end(pool, "pool")
            pool_diag(pool)
            pool.wait_ge(neg_in, 1)
            G.partition_all_reduce(cmax[:, 0:1], cpart[:, 0:1], P, RMAX).then_inc(neg_all, 1)
            stage_end(pool, "pool")

            def row_tile(t, q, nr):
                pool.wait_ge(b_in[q], 8 * (t - q) + 16)
                b = arow[0:nr, q, bass.ds(t * P, nr)]
                G.tensor_tensor(b, b, noteye[0:nr, 0:nr], ALU.mult).then_inc(b_diag, 1)
            tile_pairs(pool, row_tile)
            stage_end(pool, "pool")
            stage_end(pool, "pool")

            def gate_tile(t, q, nr):
                pool.wait_ge(g_tps, t + 1)
                G.tensor_copy(st[0:nr, q, 0], tl(ns, t, nr))
                G.tensor_copy(st[0:nr, q, 1], tl(es, t, nr))
                G.tensor_copy(st[0:nr, q, 2], tl(xnat, t, nr)).then_inc(g_staged, 1)
            tile_pairs(pool, gate_tile)
            stage_end(pool, "pool")
            stage_end(pool, "pool")
            stage_end(pool, "pool")
            stage_end(pool, "pool")

            def maxima(i, heads):
                pool.wait_ge(cm_in, i + 1)
                G.partition_all_reduce(cmax[:, 0:heads], cpart[:, 0:heads], P, RMAX).then_inc(cm_ok, 1)
            G.memset(smalls.rearrange("p a b -> p (a b)"), 0.0)
            stage_end(pool, "pool")
            maxima(0, H2)
            s = sw["L2"]
            pool.sem_inc(den_pool, 2)

            def chunk2(c, last):
                def step(u):
                    pool.wait_ge(den_pool, u.n + 2)
                    pool.wait_ge(s["p_ok"], 2 * H2 + u.n * H2 + 1)
                    G.tensor_tensor(S2[0:u.kp, 0, 0:u.w], S2[0:u.kp, 0, 0:u.w], PM[0:u.kp, u.q, 0, 0:u.w], ALU.add
                                    ).then_inc(den_pool, 1)
                pool.wait_ge(den_ps, c + 1)
                settle(pool)
                G.memset(S2[:, 0, :], 0.0).then_inc(pool_link, 1)
                pool.wait_ge(pool_link, c + 2)
                settle(pool)
                sweep_units(pool, c, last, step)
            sweep_chunks(pool, chunk2)
            stage_end(pool, "pool")
            stage_end(pool, "pool")
            stage_end(pool, "pool")
            maxima(1, H3)
            s = sw["L3"]
            pool.sem_inc(s["mask_ok"], 4)

            def chunk3(c, last):
                w = WL if last else W

                def step(u):
                    pool.wait_ge(s["blk_in"][u.slot], u.loaded)
                    pool.wait_ge(s["p_ok"], u.n * H3 + H3)
                    settle(pool)
                    G.tensor_scalar(msk[0:u.kp, u.q, 0:w], blk2[0:u.kp, u.slot].rearrange("p r n -> p (r n)")[:, 0:w],
                                    0.5, None, ALU.is_gt).then_inc(s["mask_ok"], 1)
                sweep_units(pool, c, last, step)
            sweep_chunks(pool, chunk3)
            stage_end(pool, "pool")
            stage_end(pool, "pool")

        def pe_project(pe, i, wcat, cols):
            staged, xt_ps, xt_ok, proj_ps, proj_ok = projs[i]
            pe.sem_inc(xt_ps, 2)

            def turn(t, q, nr):
                pe.wait_ge(staged, t + 1)
                for kk in range(KD):
                    last = PE.transpose(psT[q][:, kk * P:kk * P + nr], xs[0:nr, q, kk * P:(kk + 1) * P], ident[0:nr, 0:nr])
                last.then_inc(xt_ps, 1)

            def product(t, q, nr):
                pe.wait_ge(xt_ok, t + 1)
                pe.wait_ge(proj_ok, t + 1)
                for kk in range(KD):
                    for b, (lo, hi) in enumerate(splits(cols)):
                        last = PE.matmul(bank(2 * q + b)[0:nr, 0:hi - lo], xT[:, q, kk, 0:nr], wcat[:, kk, lo:hi],
                                         start=kk == 0, stop=kk == KD - 1)
                last.then_inc(proj_ps, 1)
            pairs_ahead(pe, turn, product)

        def pe_back(pe, i, src, heads, m):
            for t in range(T):
                nr = P if t < T - 1 else TAIL
                if t >= 4:
                    pe.wait_ge(back_ok[i], t - 3)
                for h in range(heads):
                    ins = PE.transpose(bank(t % 4)[0:nr, h * m:(h + 1) * m], src[0:m, h, t * P:t * P + nr],
                                       ident[0:m, 0:m])
                ins.then_inc(back_ps[i], 1)

        def pe_sums(pe, i):
            pe.wait_ge(sx_in, i + 1)
            PE.matmul(bank(4)[:, 0:D], ones, part, start=True, stop=True).then_inc(sx_ok, 1)

        def splits(cols):
            return [(0, cols)] if cols <= 512 else [(0, 512), (512, cols)]

        def pe_rows(k, src, heads, b=5):
            PE.transpose(bank(b)[0:heads * T, 0:P], src, ident[:, :]).then_inc(rows[k][1], 1)

        def pe_sweep(pe, k, banks, products, front=None, ahead=2):
            s = sw[k]
            pe.sem_inc(s["mm_done"], ahead)

            def chunk(c, last):
                pe.wait_ge(s["acc_free"], c + 1)
                for b in banks:
                    PE.matmul(bank(b), zrow[0:1, 0:P], zrow[0:1, :], start=True, stop=False)
                if front:
                    sweep_wide(pe, c, last, lambda us: run_ahead(us, front, products))
                else:
                    sweep_units(pe, c, last, products)
            sweep_chunks(pe, chunk)

        def accumulate(u, mms):
            for i, (o, b, l, r) in enumerate(mms):
                ins = PE.matmul(o, l, r, start=False, stop=False, skip_group_check=True)
            return ins

        def unit_done(u, ins, s, banks):
            if u.end:
                for b in banks:
                    ins = PE.matmul(bank(b), zrow[0:1, 0:P], zrow[0:1, :], start=False, stop=True)
            ins.then_inc(s["mm_done"], 1)

        @block.tensor
        def _(pe):
            pe.wait_ge(const_ok, 1)
            pe.wait_ge(loaded, 16 * (2 + 4 * KD + 8))
            for fo in range(KD):
                for kk in range(KD):
                    ins = PE.transpose(bank(4)[:, (kk * KD + fo) * P:(kk * KD + fo + 1) * P],
                                       w1n[:, fo, kk * P:(kk + 1) * P], ident)
            ins.then_inc(w1T_ok, 1)
            stage_end(pe, "pe")
            pe_project(pe, 0, wcat0, H0 * D + 2 * H0)
            stage_end(pe, "pe")
            s = sw["A"]

            def transposes_A(u):
                pe.wait_ge(s["at_ok"], u.n + 1)
                if u.diag is None:
                    pe.wait_ge(s["wide_in"][u.wide], u.wide_loaded)
                else:
                    pe.wait_ge(s["diag_ok"], u.c * 4 + u.diag + 1)
                for r, nr in enumerate(u.rows):
                    ins = PE.transpose(psT[u.q][0:u.kp, r * P:r * P + nr], wide_block(u, r, nr, u.kp), ident[0:nr, 0:nr])
                ins.then_inc(s["transposed"], 1)

            def products_A(u):
                pe.wait_ge(s["mask_ok"], u.n + 1)
                mms = []
                for m, lo, wide in ((Mp, 0, 2 * H0), (Mm, H0, 2 * H0 + 1)):
                    rhs_u = ub[0:u.kp, bass.ds(u.tile, 1), :, lo:lo + wide].rearrange("p a s h -> p (a s) h")
                    mms += [(bank(2)[0:nr, r * 21:(r + 1) * 21].rearrange("p (s h) -> p s h", s=3)[:, :, 0:wide], 2,
                             m[0:u.kp, u.q, r * P:r * P + nr], rhs_u) for r, nr in enumerate(u.rows)]
                unit_done(u, accumulate(u, mms), s, [2])
            pe.sem_inc(s["transposed"], 4)
            pe_sweep(pe, "A", [2], products_A, transposes_A)
            stage_end(pe, "pe")
            pe_rows("e", e6[:, 0:H0, :].rearrange("p h t -> p (h t)"), H0)
            pe_rows("d", e_step.rearrange("p h t -> p (h t)"), H0, 4)
            s = sw["B"]

            def products_B(u):
                pe.wait_ge(s["blk_in"][u.slot], u.loaded)
                rhs_x = xnat[0:u.kp, bass.ds(u.tile, 1), :].rearrange("p a d -> p (a d)")
                unit_done(u, accumulate(u, [(bank(0, 2)[0:nr, r * D:(r + 1) * D], r // 2,
                                             strips[u.slot][0:u.kp, r * P:r * P + nr], rhs_x)
                                            for r, nr in enumerate(u.rows)]), s, [0, 1])
            pe_sweep(pe, "B", [0, 1], products_B, ahead=4)
            pe.wait_ge(b_negm, T * H0)
            pe_rows("m", negm.rearrange("p h t -> p (h t)"), H0)
            stage_end(pe, "pe")
            s = sw["C"]

            def products_C(u):
                for h in range(H0):
                    pe.wait_ge(s["p_ok"], 4 * H0 + u.n * H0 + h + 1)
                    rhs_h = hW[0:u.kp, bass.ds(u.tile, 1), h * D:(h + 1) * D].rearrange("p a d -> p (a d)")
                    mms = [(bank(0, 6)[0:nr, (r * H0 + h) * D:(r * H0 + h + 1) * D], (r * H0 + h) // 2,
                            PA[0:u.kp, u.q, h, r * P:r * P + nr], rhs_h) for r, nr in enumerate(u.rows)]
                    for o, b, l, rr in mms:
                        ins = PE.matmul(o, l, rr, start=False, stop=False, skip_group_check=True)
                unit_done(u, ins, s, range(6))
            pe_sweep(pe, "C", range(6), products_C)
            stage_end(pe, "pe")
            pe.wait_ge(g_in, 128)
            n = 0
            for i in range(4):
                for kk in range(KD):
                    for g0 in (0, 3):
                        if n >= 4:
                            pe.wait_ge(g_wok, n - 3)
                        for g in range(g0, g0 + 3):
                            ins = PE.transpose(bank(n % 4)[:, (g - g0) * P:(g - g0 + 1) * P],
                                               g_wn[:, i, g, kk * P:(kk + 1) * P], ident)
                        ins.then_inc(g_wps, 1)
                        n += 1
            pe.wait_ge(g_wok, n)
            pe.sem_inc(g_tps, 2)

            def gate_transposes(t, q, nr):
                pe.wait_ge(g_staged, t + 1)
                pe.wait_ge(g_tok, t + 1)
                for j in range(3):
                    for kk in range(KD):
                        i = j * KD + kk
                        ins = PE.transpose(bank(4 + 2 * q, 2)[:, i * P:i * P + nr], st[0:nr, q, j, kk * P:(kk + 1) * P],
                                           ident[0:nr, 0:nr])
                ins.then_inc(g_tps, 1)

            def gate_tile(t, q, nr):
                if not isinstance(t, int) or t < T - 1:
                    gate_transposes(t + 1, 1 - q, TAIL if isinstance(t, int) else P)
                pe.wait_ge(g_tok, t + 3)
                for g in range(2):
                    pe.wait_ge(g_pre, 2 * t + g + 1)
                    wi, wh = g_wT[:, 2 * g], g_wT[:, 2 * g + 1]
                    rz, nh = bank(2 * g)[0:nr], bank(2 * g + 1)[0:nr]
                    for kk in range(KD):
                        X, Hh = sT[:, q, g, kk, 0:nr], sT[:, q, 2, kk, 0:nr]
                        PE.matmul(rz, X, wi[:, kk, 0:2 * D], start=kk == 0, stop=False)
                        PE.matmul(rz, Hh, wh[:, kk, 0:2 * D], start=False, stop=kk == 1)
                        PE.matmul(nh[:, 0:D], X, wi[:, kk, 2 * D:3 * D], start=kk == 0, stop=False, skip_group_check=True)
                        ins = PE.matmul(nh[:, D:2 * D], Hh, wh[:, kk, 2 * D:3 * D], start=False, stop=kk == 1,
                                        skip_group_check=True)
                    ins.then_inc(g_ready, 1)
            gate_transposes(0, 0, P)
            tile_pairs(pe, gate_tile)
            stage_end(pe, "pe")
            stage_end(pe, "pe")
            s = sw["L1"]

            def products_1(u):
                pe.wait_ge(s["blk_in"][u.slot], u.loaded)
                r1 = xd[0:u.kp, bass.ds(u.tile, 1), :].rearrange("p a d -> p (a d)")
                unit_done(u, accumulate(u, [(bank(0, 2)[0:nr, r * D:(r + 1) * D], r // 2,
                                             blk2[0:u.kp, u.slot, r, 0:nr], r1) for r, nr in enumerate(u.rows)]), s, [0, 1])
            pe_sweep(pe, "L1", [0, 1], products_1, ahead=4)
            stage_end(pe, "pe")
            pe.sem_inc(h1_ps, 2)

            def turn1(t, q, nr):
                pe.wait_ge(h1_st, t + 1)
                for kk in range(KD):
                    ins = PE.transpose(psT[q][:, kk * P:kk * P + nr], xs[0:nr, q, kk * P:(kk + 1) * P], ident[0:nr, 0:nr])
                ins.then_inc(h1_ps, 1)

            def product1(t, q, nr):
                pe.wait_ge(h1_ok, t + 1)
                pe.wait_ge(h1_done, t + 1)
                for kk in range(KD):
                    ins = PE.matmul(bank(q)[0:nr, 0:D], xT[:, q, kk, 0:nr], w1T[:, kk, :], start=kk == 0, stop=kk == KD - 1)
                ins.then_inc(h1_mm, 1)
            pairs_ahead(pe, turn1, product1)
            stage_end(pe, "pe")
            pe_project(pe, 1, wcat2, D + 2 * H2)
            stage_end(pe, "pe")
            pe.wait_ge(fg_ok, 1)
            pe_rows("r2", smalls[:, 6, 0:H2 * T], H2)
            pe_sums(pe, 0)
            s2 = sw["L2"]

            def products_2(u):
                pe.wait_ge(st_ok, u.n + 1)
                for h in range(H2):
                    pe.wait_ge(s2["p_ok"], 2 * H2 + u.n * H2 + h + 1)
                    ins = PE.matmul(bank(h)[:, 0:u.w], stage_w[0:u.kp, u.q, h * C2:(h + 1) * C2],
                                    PM[0:u.kp, u.q, h, 0:u.w], start=False, stop=False)
                unit_done(u, ins, s2, range(H2))
                if u.end:
                    pe.wait_ge(den_dve, (u.c + 1) * T + 1)
                    pe.wait_ge(den_pool, (u.c + 1) * T + 2)
                    pe.wait_ge(den_out, u.c + 1)
                    for h in range(H2):
                        for r, nr in enumerate(u.rows):
                            i = r * H2 + h
                            ins = PE.matmul(bank(4)[0:nr, i:i + 1], S2[:, h, r * P:r * P + nr], ones[:, 0:1], start=True,
                                            stop=True)
                    ins.then_inc(den_ps, 1)
            pe_sweep(pe, "L2", range(H2), products_2)
            stage_end(pe, "pe")
            pe_back(pe, 0, rawT2, H2, C2)
            stage_end(pe, "pe")
            pe_project(pe, 2, wcat3, D + 2 * H3)
            stage_end(pe, "pe")
            pe.wait_ge(fg_ok, 2)
            pe_rows("r3", smalls[:, 6, 0:H3 * T], H3)
            pe_sums(pe, 1)
            s3 = sw["L3"]

            def products_3(u):
                for h in range(H3):
                    pe.wait_ge(s3["p_ok"], 2 * H3 + u.n * H3 + h + 1)
                    ins = PE.matmul(bank(h)[0:C3 + 1, 0:u.w], stage_w[0:u.kp, u.q, h * (C3 + 1):(h + 1) * (C3 + 1)],
                                    PM[0:u.kp, u.q, h, 0:u.w], start=False, stop=False)
                unit_done(u, ins, s3, range(H3))
            pe_sweep(pe, "L3", range(H3), products_3)
            stage_end(pe, "pe")
            pe_back(pe, 1, rawT3, H3, C3 + 1)
            stage_end(pe, "pe")

        def act_project(act, i):
            staged, xt_ps, xt_ok, proj_ps, proj_ok = projs[i]

            def stage(t, q, nr):
                act.wait_ge(xt_ps, t + 1)
                settle(act)
                S.copy(xs[0:nr, q, :], tl(xnat, t, nr)).then_inc(staged, 1)

            def turned(t, q, nr):
                act.wait_ge(xt_ps, t + 3)
                act.wait_ge(proj_ps, t + 1)
                S.copy(xT[:, q, :, 0:nr], psT[q][:, 0:D].rearrange("p (k n) -> p k n", k=KD)[:, :, 0:nr]).then_inc(xt_ok, 1)
            act.sem_inc(proj_ps, 2)
            pairs_ahead(act, stage, turned)

        def act_rows(act, k, heads):
            act.wait_ge(rows[k][1], 1)
            dst, b = (d_s, 4) if k == "d" else (rows_s, 5)
            S.copy(dst[0:heads * T, :], bank(b)[0:heads * T, 0:P]).then_inc(rows[k][2], 1)

        def act_std(act, i):
            act.wait_ge(ln_var, i + 1)
            S.activation(rstd, rstd, ACT.Sqrt).then_inc(ln_std, 1)

        def act_copy_sweep(act):
            s = sw["A"]
            act.sem_inc(s["at_ok"], 2)
            for i in range(4):
                act.sem_inc(at_out[i], 16)

            def chunk(c, last):
                def step(u):
                    act.wait_ge(s["transposed"], u.n + 5)
                    act.wait_ge(s["mm_done"], u.n + 1)
                    act.wait_ge(at_out[u.slot], u.loaded)
                    S.copy(AT[0:u.kp, u.slot, 0:u.w], psT[u.q][0:u.kp, 0:u.w]).then_inc(s["at_ok"], 1)
                    act.wait_ge(s["at_ok"], u.n + 3)
                    act.dma_start(adj_T[bass.ds(u.tile * P, u.kp), bass.ds(c * W, u.w)], AT[0:u.kp, u.slot, 0:u.w]
                                  ).then_inc(at_out[u.slot], 16)
                sweep_units(act, c, last, step)
            sweep_chunks(act, chunk)
            for i in range(4):
                act.wait_ge(at_out[i], 16 * (1 + (6 if i < 2 else 5) * CH))

        def act_ratio_sweep(act, k, heads, sm):
            s = sw[k]
            act.wait_ge(neg_ok, 1 if k == "L2" else 2)

            def chunk(c, last):
                def step(u):
                    if k == "L2":
                        act.wait_ge(s["mm_done"], u.n + 1)
                        settle(act)
                        S.copy(stage_w[0:u.kp, u.q, 0:D], proj[0:u.kp, bass.ds(u.tile, 1), 0:D].rearrange(
                            "p a d -> p (a d)")).then_inc(st_ok, 1)
                    for h in range(heads):
                        act.wait_ge(s["p_ok"], u.n * heads + h + 1)
                        settle(act)
                        S.activation(Y[0:u.kp, u.q, h, 0:u.w], r_bc[0:u.kp, h, bass.ds(c * W, u.w)], ACT.Relu,
                                     bias=sm[0:u.kp, 3, bass.ds(u.tile + h * T, 1)],
                                     scale=sm[0:u.kp, 5, bass.ds(u.tile + h * T, 1)]
                                     ).then_inc(s["y_ok"], 1)
                sweep_units(act, c, last, step)
            name = "r2" if k == "L2" else "r3"
            act.wait_ge(rows[name][4], 16)
            chunk(0, False)
            act.wait_ge(rest_bc[name], 16)
            settle(act)
            with act.Fori(1, CH - 1) as c:
                chunk(c, False)
            chunk(CH - 1, True)

        @block.scalar
        def _(act):
            act.wait_ge(w1T_ok, 1)
            S.copy(w1T.rearrange("p k f -> p (k f)"), bank(4)[:, 0:KD * D])
            stage_end(act, "act")
            act_project(act, 0)
            stage_end(act, "act")
            act_copy_sweep(act)
            stage_end(act, "act")
            s = sw["B"]
            act_rows(act, "e", H0)
            act_rows(act, "d", H0)

            act.sem_inc(s["acc_free"], 1)
            act.sem_inc(support_out, 16)
            negative = act.value_load(has_neg_int[0:1, 0:1])

            def row_load(t, q, nr):
                load(act, arow[0:nr, q, :], adj[bass.ds(t * P, nr), :], b_in[q])

            def row_sum(t, q, nr):
                act.wait_ge(b_diag, t + 1)
                settle(act)
                S.activation(arow[0:nr, q, :], arow[0:nr, q, :], ACT.Copy, accum_out=rowsum[0:nr, bass.ds(t, 1)]
                             ).then_inc(b_sum, 1)

            def row_tile(t, q, nr, general):
                static = isinstance(t, int)
                if not (static and t == T - 1):
                    row_sum(t + 1, 1 - q, TAIL if static and t == T - 2 else P)

                def load_ahead():
                    if not (static and t >= T - 2):
                        act.wait_ge(b_rowfree, t + 1)
                        row_load(t + 2, q, TAIL if static and t == T - 3 else P)
                if not general:
                    load_ahead()
                for h in range(H0):
                    if general:
                        for i in range(4):
                            act.wait_ge(gen_free, (t * H0 + h) * 4 + i + 1)
                            cols = slice(i * (N // 4), (i + 1) * (N // 4))
                            load(act, d_bc, d_rows[h:h + 1, cols].partition_broadcast(P).rearrange("p a n -> p (a n)"), gen_in)
                    sl = (q * H0 + h) % 2
                    act.wait_ge(b_negm, H0 * t + h + 1)
                    settle(act)
                    S.activation(srow[0:nr, sl, :], srow[0:nr, sl, :], ACT.Exp, bias=col(negm, h, t, nr),
                                 accum_out=col(den, h, t, nr)).then_inc(b_exp, 1)
                if general:
                    load_ahead()

            def chunk(c, last, general):
                sizes = [P, TAIL] if last else [P] * RPC
                for v, nr in enumerate(sizes):
                    row_tile(c * RPC + v, v % 2, nr, general)
                act.wait_ge(s["mm_done"], (c + 1) * T + 4)
                act.wait_ge(support_out, 16 * (c + 1))
                if not last:
                    S.copy(support_s, bank(0, 2)).then_inc(s["acc_free"], 1)
                else:
                    for v, nr in enumerate(sizes):
                        ins = S.copy(support_s[0:nr, v * D:(v + 1) * D], bank(0, 2)[0:nr, v * D:(v + 1) * D])
                    ins.then_inc(s["acc_free"], 1)
                act.wait_ge(s["acc_free"], c + 2)
                if not last:
                    act.dma_start(support[bass.ds(c * W, W), :].rearrange("(r p) d -> p r d", p=P),
                                  support_s.rearrange("p (r d) -> p r d", r=RPC)).then_inc(support_out, 16)
                else:
                    for v, nr in enumerate(sizes):
                        act.dma_start(support[c * W + v * P:c * W + v * P + nr, :], support_s[0:nr, v * D:(v + 1) * D]
                                      ).then_inc(support_out, 16)

            def all_rows(general):
                with act.Fori(0, CH - 2) as c:
                    chunk(c, False, general)
                chunk(CH - 2, False, general)
                chunk(CH - 1, True, general)
            for q in range(2):
                row_load(q, q, P)
            row_sum(0, 0, P)
            with act.If(negative != 0):
                act.wait_ge(rows["d"][3], 16)
                all_rows(True)
            with act.Else():
                all_rows(False)
            act.wait_ge(support_out, 16 * (CH + 2))
            act_rows(act, "m", H0)
            stage_end(act, "act")
            s = sw["C"]

            def chunk(c, last):
                def step(u):
                    act.wait_ge(c_arg, u.n + 2)
                    S.activation(E[0:u.kp, u.q, :, 0:u.w], E[0:u.kp, u.q, :, 0:u.w], ACT.Exp).then_inc(s["y_ok"], 1)
                sweep_units(act, c, last, step)
            sweep_chunks(act, chunk)
            stage_end(act, "act")
            n = 0
            for i in range(4):
                for kk in range(KD):
                    for g0 in (0, 3):
                        act.wait_ge(g_wps, n + 1)
                        S.copy(g_wT[:, i, kk, g0 * P:(g0 + 3) * P], bank(n % 4)[:, 0:3 * P]).then_inc(g_wok, 1)
                        n += 1
            act.sem_inc(g_tok, 2)

            def gate_copy(t, q, nr):
                act.wait_ge(g_tps, t + 3)
                act.wait_ge(g_ready, 2 * t + 1)
                S.copy(sT[:, q].rearrange("p j k n -> p (j k) n")[:, :, 0:nr],
                       bank(4 + 2 * q, 2)[:, 0:3 * D].rearrange("p (i n) -> p i n", n=P)[:, :, 0:nr]).then_inc(g_tok, 1)

            def gate_tile(t, q, nr):
                for g in range(2):
                    if g and (not isinstance(t, int) or t < T - 1):
                        gate_copy(t + 1, 1 - q, TAIL if isinstance(t, int) else P)
                    act.wait_ge(g_pre, 2 * t + g + 3)
                    S.activation(g_th[0:nr], g_rz[0:nr], ACT.Tanh, scale=0.5).then_inc(g_thok, 1)
                    act.wait_ge(g_tok2, 2 * t + g + 1)
                    S.activation(g_n[0:nr], g_t[0:nr], ACT.Tanh).then_inc(g_nok, 1)
            act.sem_inc(g_ready, 3)
            gate_copy(0, 0, P)
            tile_pairs(act, gate_tile)
            stage_end(act, "act")
            act_std(act, 0)
            act.wait_ge(deg_in, 1)
            S.activation(rowsum, rowsum, ACT.Sqrt).then_inc(deg_out, 1)
            stage_end(act, "act")
            stage_end(act, "act")

            def stage1(t, q, nr):
                act.wait_ge(h1_ps, t + 1)
                settle(act)
                S.copy(xs[0:nr, q, :], tl(raw1, t, nr)).then_inc(h1_st, 1)

            def turned1(t, q, nr):
                act.wait_ge(h1_ps, t + 3)
                act.wait_ge(h1_mm, t + 1)
                S.copy(xT[:, q, :, 0:nr], psT[q][:, 0:D].rearrange("p (k n) -> p k n", k=KD)[:, :, 0:nr]).then_inc(h1_ok, 1)
            act.sem_inc(h1_mm, 2)
            pairs_ahead(act, stage1, turned1)
            act_std(act, 1)
            stage_end(act, "act")
            act_project(act, 1)
            stage_end(act, "act")

            def factors(i, heads):
                act.wait_ge(fg_in, i + 1)
                S.activation(smalls[:, 4:7, 0:heads * T], smalls[:, 0:3, 0:heads * T], ACT.Exp).then_inc(fg_ok, 1)
            factors(0, H2)
            act_rows(act, "r2", H2)
            act_ratio_sweep(act, "L2", H2, smalls)
            stage_end(act, "act")
            act.wait_ge(elu_in, 1)
            for nr, ts in FULL:
                ins = S.activation(tmp2[0:nr, ts], tmp2[0:nr, ts], ACT.Exp)
            ins.then_inc(elu_ok, 1)
            act_std(act, 2)
            stage_end(act, "act")
            act_project(act, 2)
            stage_end(act, "act")
            factors(1, H3)
            act_rows(act, "r3", H3)
            act_ratio_sweep(act, "L3", H3, smalls)
            stage_end(act, "act")
            act_std(act, 3)
            stage_end(act, "act")

        def dve_project(dve, i, dst, cols):
            staged, xt_ps, xt_ok, proj_ps, proj_ok = projs[i]
            dve.sem_inc(proj_ok, 2)

            def tile(t, q, nr):
                dve.wait_ge(proj_ps, t + 3)
                for b, (lo, hi) in enumerate(splits(cols)):
                    ins = V.tensor_copy(dst[0:nr, bass.ds(t, 1), lo:hi].rearrange("p a d -> p (a d)"),
                                        bank(2 * q + b)[0:nr, 0:hi - lo])
                ins.then_inc(proj_ok, 1)
            tile_pairs(dve, tile)
            dve.wait_ge(proj_ok, T + 2)

        def stats(t, q, nr):
            return V.bn_stats(bnst[0:nr, bass.ds(t, 1), :].rearrange("p a m -> p (a m)"), tl(xnat, t, nr))

        def dve_norm(dve, link, i, with_stats=True):
            if with_stats:
                link(tile_pairs(dve, stats))
            for t in range(T):
                nr = P if t < T - 1 else TAIL
                ins = V.bn_aggr(mv[0:nr, t, :], bnst[0:nr, t, :])
            link(ins)
            V.tensor_scalar(rstd[:, 0:T - 1], mv[:, 0:T - 1, 1], EPS, None, ALU.add)
            V.tensor_scalar(rstd[0:TAIL, T - 1:T], mv[0:TAIL, T - 1:T, 1], EPS, None, ALU.add).then_inc(ln_var, 1)
            dve.wait_ge(ln_std, i + 1)
            link(V.reciprocal(rstd, rstd))

            def scale(t, q, nr):
                return V.tensor_scalar(tl(xnat, t, nr), tl(xnat, t, nr), mv[0:nr, bass.ds(t, 1), 0], rstd[0:nr, bass.ds(t, 1)],
                                ALU.subtract, ALU.mult)
            link(tile_pairs(dve, scale))

        def head_vector(link, wv, av, dst):
            _, hh, ff = wv.shape
            pv = prod[:, 0:hh * ff].rearrange("p (h f) -> p h f", h=hh)
            link(V.tensor_tensor(pv, wv, av, ALU.mult))
            link(V.tensor_reduce(dst, pv, AX_X, ALU.add))

        def node_sum(dve, link, i):
            link(V.tensor_reduce(part, proj[:, 0:T - 1, 0:D].rearrange("p t d -> p d t"), AX_X, ALU.add))
            V.tensor_tensor(part[0:TAIL], part[0:TAIL], proj[0:TAIL, T - 1, 0:D], ALU.add).then_inc(sx_in, 1)
            dve.wait_ge(sx_ok, i + 1)
            V.tensor_copy(sum_bc, bank(4)[:, 0:D])

        @block.vector
        def _(dve):
            link = Chain(dve, dve_link)
            V.memset(rstd, 1.0)
            V.memset(rowsum, 1.0)
            dve.wait_ge(const_ok, 1)
            dve.wait_ge(loaded, 16 * (2 + 4 * KD + 8))
            for kk in range(KD):
                w0 = wcat0[:, kk, 0:H0 * D].rearrange("p (h f) -> p h f", h=H0)
                w2 = wcat2[:, kk, 0:D].rearrange("p (h f) -> p h f", h=H2)
                w3 = wcat3[:, kk, 0:D].rearrange("p (h f) -> p h f", h=H3)
                for j in range(2):
                    head_vector(link, w0, a0_bc[:, :, j, :], wcat0[:, kk, H0 * D + j * H0:H0 * D + (j + 1) * H0])
                    head_vector(link, w2, a2_bc[:, :, j, :], wcat2[:, kk, D + j * H2:D + (j + 1) * H2])
                    head_vector(link, w3, a3_bc[:, j], wcat3[:, kk, D + j * H3:D + (j + 1) * H3])
            stage_end(dve, "dve")
            dve_project(dve, 0, hW, H0 * D + 2 * H0)
            for nr, ts in FULL:
                ins = V.tensor_copy(ur[0:nr, ts], hW[0:nr, ts, H0 * D:])
            link(ins)
            for part in range(3):
                for nr, ts in FULL:
                    ins = V.tensor_copy(ub[0:nr, ts, part, 0:2 * H0], ur[0:nr, ts])
                link(ins)
                for nr, ts in FULL:
                    V.tensor_copy(ub[0:nr, ts, part, 2 * H0:3 * H0], ub[0:nr, ts, part, 0:H0])
                    V.memset(ub[0:nr, ts, part, 3 * H0:], 1.0)
                    ins = V.tensor_tensor(ur[0:nr, ts], ur[0:nr, ts], ub[0:nr, ts, part, 0:2 * H0], ALU.subtract)
                link(ins)
            stage_end(dve, "dve")
            s = sw["A"]
            dve.sem_inc(s["acc_free"], 1)

            def chunkA(c, last):
                def step(u):
                    dve.wait_ge(s["at_ok"], u.n + 3)
                    dve.wait_ge(s["mm_done"], u.n + 1)
                    V.tensor_scalar(Mp[0:u.kp, u.q, 0:u.w], AT[0:u.kp, u.slot, 0:u.w], 0.0, None, ALU.is_gt)
                    V.tensor_scalar(Mm[0:u.kp, u.q, 0:u.w], AT[0:u.kp, u.slot, 0:u.w], 0.0, None, ALU.is_lt
                                    ).then_inc(s["mask_ok"], 1)
                sweep_units(dve, c, last, step)
                dve.wait_ge(s["mm_done"], (c + 1) * T + 2)
                empty(c, last, bank(2), 21, E21.rearrange("p t s h -> p t (s h)")).then_inc(s["acc_free"], 1)
            sweep_chunks(dve, chunkA)
            dve.wait_ge(s["acc_free"], CH + 1)
            for nr, ts in FULL:
                ev = e6[0:nr, :, ts].rearrange("p h t -> p t h")
                link(V.tensor_tensor(ur[0:nr, ts], E21[0:nr, ts, 2, 0:2 * H0], E21[0:nr, ts, 1, 0:2 * H0], ALU.add))
                link(V.tensor_tensor(ur[0:nr, ts], ur[0:nr, ts], E21[0:nr, ts, 0, 0:2 * H0], ALU.add))
                link(V.scalar_tensor_tensor(ev, ur[0:nr, ts], SLOPE, ur[0:nr, ts], ALU.mult, ALU.max))
            V.tensor_tensor(e_step, e6[:, H0:2 * H0, :], e6[:, 0:H0, :], ALU.subtract)
            link(V.tensor_reduce(cpart[:, 0:1], E21[:, 0:T - 1, 0, 2 * H0], AX_X, ALU.max))
            V.tensor_tensor(cpart[0:TAIL, 0:1], cpart[0:TAIL, 0:1], E21[0:TAIL, T - 1, 0, 2 * H0:], ALU.max
                            ).then_inc(neg_in, 1)
            dve.wait_ge(neg_all, 1)
            link(V.tensor_scalar(cpart[:, 0:1], cmax[:, 0:1], 0.0, None, ALU.is_gt))
            V.tensor_copy(has_neg_int, cpart[:, 0:1])
            stage_end(dve, "dve")
            V.memset(den.rearrange("p h t -> p (h t)"), 1.0)
            dve.wait_ge(rows["e"][4], 16 * H0)
            dve.sem_inc(b_exp, 2)

            negative = dve.value_load(has_neg_int[0:1, 0:1])
            glink = Chain(dve, gen_link)

            def row_tile(t, q, nr, general=False):
                dve.wait_ge(b_diag, t + 1)
                dve.wait_ge(b_sum, t + 1)
                link(V.tensor_scalar(mbias[0:nr, :], arow[0:nr, q, :], 0.0, NEG, ALU.is_equal, ALU.mult))
                if not general:
                    dve.sem_inc(b_rowfree, 1)
                for h in range(H0):
                    sl = (q * H0 + h) % 2
                    dve.wait_ge(b_exp, H0 * t + h + 1)
                    settle(dve)
                    link(V.tensor_tensor_reduce(out=srow[0:nr, sl, :], in0=mbias[0:nr, :], in1=e_bc[0:nr, h, :], scale=1.0,
                                                scalar=3 * NEG, op0=ALU.add, op1=ALU.max, accum_out=mrow[0:nr, sl:sl + 1]))
                    if general:
                        for i in range(4):
                            cols = slice(i * (N // 4), (i + 1) * (N // 4))
                            dve.wait_ge(gen_in, 16 * ((t * H0 + h) * 4 + i + 1))
                            glink(V.scalar_tensor_tensor(d_bc[0:nr], arow[0:nr, q, cols], 0.0, d_bc[0:nr], ALU.is_lt,
                                                         ALU.mult))
                            glink(V.tensor_tensor(srow[0:nr, sl, cols], srow[0:nr, sl, cols], d_bc[0:nr], ALU.add))
                            dve.sem_inc(gen_free, 1)
                        glink(V.tensor_reduce(mrow[0:nr, sl:sl + 1], srow[0:nr, sl, :], AX_X, ALU.max))
                    V.tensor_scalar(col(negm, h, t, nr), mrow[0:nr, sl:sl + 1], -1.0, None, ALU.mult).then_inc(b_negm, 1)
                if general:
                    dve.sem_inc(b_rowfree, 1)
            def all_rows(general):
                with dve.Fori(0, CH - 1) as c:
                    with link.loop(c, CH - 1, RPC * (1 + H0)), glink.loop(c, CH - 1, RPC * 9 * H0 if general else 0):
                        for v in range(RPC):
                            row_tile(c * RPC + v, v % 2, P, general)
                for v, nr in enumerate((P, TAIL)):
                    row_tile((CH - 1) * RPC + v, v, nr, general)
            with link.either():
                with dve.If(negative != 0):
                    dve.sem_inc(gen_free, 1)
                    all_rows(True)
            with dve.Else():
                all_rows(False)
            dve.wait_ge(b_exp, T * H0 + 2)
            link(V.reciprocal(den.rearrange("p h t -> p (h t)"), den.rearrange("p h t -> p (h t)")))
            link(V.tensor_scalar(den.rearrange("p h t -> p (h t)"), den.rearrange("p h t -> p (h t)"), 1.0 / H0, None,
                                 ALU.mult))
            stage_end(dve, "dve")
            s = sw["C"]
            dve.sem_inc(s["acc_free"], 1)
            dve.sem_inc(s["p_ok"], 4 * H0)

            dve.sem_inc(c_arg, 1)

            def chunkC(c, last, general):
                dve.wait_ge(mbc_in, 16 * H0 * (c + 1))

                def strip(u):
                    return blk[0:u.kp, u.slot].rearrange("p r n -> p (r n)")[:, 0:u.w]

                def exponents(u):
                    dve.wait_ge(s["p_ok"], u.n * H0 + 3 * H0)
                    if general:
                        dve.wait_ge(s["blk_in"][u.slot], u.loaded)
                        for h in range(H0):
                            ins = V.tensor_scalar(E[0:u.kp, u.q, h, 0:u.w], strip(u), 0.0,
                                                  e_step[0:u.kp, h, bass.ds(u.tile, 1)], ALU.is_lt, ALU.mult)
                        ins.then_inc(gen_arg, 1)
                        dve.wait_ge(gen_arg, 2 * u.n + 1)
                        V.tensor_tensor(E[0:u.kp, u.q, :, 0:u.w], E[0:u.kp, u.q, :, 0:u.w], m_bc[0:u.kp, :, 0:u.w], ALU.add
                                        ).then_inc(gen_arg, 1)
                        dve.wait_ge(gen_arg, 2 * u.n + 2)
                    arg = E[:, u.q] if general else m_bc
                    for h in range(H0):
                        ins = V.tensor_scalar(E[0:u.kp, u.q, h, 0:u.w], arg[0:u.kp, h, 0:u.w],
                                              e6[0:u.kp, h, bass.ds(u.tile, 1)], 0.0, ALU.add, ALU.min)
                    ins.then_inc(c_arg, 1)

                def step(u):
                    dve.wait_ge(s["blk_in"][u.slot], u.loaded)
                    dve.wait_ge(s["mm_done"], u.n + 1)
                    dve.wait_ge(s["y_ok"], u.n + 1)
                    for h in range(H0):
                        V.tensor_tensor(PA[0:u.kp, u.q, h, 0:u.w], E[0:u.kp, u.q, h, 0:u.w], strip(u), ALU.mult
                                        ).then_inc(s["p_ok"], 1)
                sweep_ahead(dve, c, last, exponents, step)
                dve.wait_ge(s["mm_done"], (c + 1) * T + 2)
                sizes = [P] * RPC if not last else [P, TAIL]
                for h in range(H0):
                    for r, nr in enumerate(sizes):
                        t = c * RPC + r
                        acc = bank(0, 6)[0:nr, (r * H0 + h) * D:(r * H0 + h + 1) * D]
                        if h == 0:
                            ins = V.tensor_scalar(tl(es, t, nr), acc, col(den, h, t, nr), None, ALU.mult)
                        else:
                            ins = V.scalar_tensor_tensor(tl(es, t, nr), acc, col(den, h, t, nr), tl(es, t, nr), ALU.mult,
                                                         ALU.add)
                    if h < H0 - 1:
                        link(ins)
                ins.then_inc(s["acc_free"], 1)
            def all_chunks(general):
                with dve.Fori(0, CH - 1) as c:
                    with link.loop(c, CH - 1, H0 - 1):
                        chunkC(c, False, general)
                chunkC(CH - 1, True, general)
            with link.either():
                with dve.If(negative != 0):
                    all_chunks(True)
            with dve.Else():
                all_chunks(False)
            stage_end(dve, "dve")
            dve.sem_inc(g_pre, 2)
            dve.wait_ge(g_in, 128)
            for g in range(2):
                V.tensor_tensor(g_brz[:, g], g_bias[:, 2 * g, 0:2 * D], g_bias[:, 2 * g + 1, 0:2 * D], ALU.add)
                V.tensor_copy(g_bnh[:, g, 0:D], g_bias[:, 2 * g, 2 * D:])
                ins = V.tensor_copy(g_bnh[:, g, D:], g_bias[:, 2 * g + 1, 2 * D:])
            link(ins)

            def gate_tile(t, q, nr):
                X = tl(xnat, t, nr)
                for g in range(2):
                    dve.wait_ge(g_ready, 2 * t + g + 4)
                    V.tensor_tensor(g_rz[0:nr], bank(2 * g)[0:nr], g_brz[0:nr, g], ALU.add)
                    V.tensor_tensor(g_nh[0:nr], bank(2 * g + 1)[0:nr], g_bnh[0:nr, g], ALU.add).then_inc(g_pre, 1)
                    dve.wait_ge(g_pre, 2 * t + g + 3)
                    dve.wait_ge(g_thok, 2 * t + g + 1)
                    link(V.scalar_tensor_tensor(g_q[0:nr], g_th[0:nr, 0:D], 1.0, g_nh[0:nr, D:2 * D], ALU.add, ALU.mult))
                    V.scalar_tensor_tensor(g_t[0:nr], g_q[0:nr], 0.5, g_nh[0:nr, 0:D], ALU.mult, ALU.add
                                           ).then_inc(g_tok2, 1)
                    dve.wait_ge(g_nok, 2 * t + g + 1)
                    link(V.tensor_tensor(g_d[0:nr], X, g_n[0:nr], ALU.subtract))
                    link(V.scalar_tensor_tensor(g_e[0:nr], g_th[0:nr, D:2 * D], 1.0, g_d[0:nr], ALU.add, ALU.mult))
                    link(V.scalar_tensor_tensor(g_out[0:nr, g], g_e[0:nr], 0.5, g_n[0:nr], ALU.mult, ALU.add))
                link(V.tensor_tensor(g_d[0:nr], g_out[0:nr, 0], g_out[0:nr, 1], ALU.add))
                dve.wait_ge(g_staged, t + 1)
                link(V.scalar_tensor_tensor(X, g_d[0:nr], dn[0:nr, bass.ds(t, 1)], X, ALU.mult, ALU.add))
            tile_pairs(dve, gate_tile, (link, 10))
            stage_end(dve, "dve")
            dve_norm(dve, link, 0)
            zero = smalls[:, 7, 0:T]
            for nr, ts in FULL:
                ins = V.tensor_tensor(rowsum[0:nr, ts], rowsum[0:nr, ts], dn[0:nr, ts], ALU.add)
            link(ins)
            link(V.tensor_scalar(zero, rowsum, 0.0, None, ALU.is_equal))
            dve.sem_inc(deg_in, 1)
            dve.wait_ge(deg_out, 1)
            link(V.tensor_tensor(rowsum, rowsum, zero, ALU.add))
            link(V.reciprocal(rowsum, rowsum))
            link(V.tensor_scalar(zero, zero, -1.0, 1.0, ALU.mult, ALU.add))
            link(V.tensor_tensor(rowsum, rowsum, zero, ALU.mult))
            r1v = xd

            def by_degree(t, q, nr):
                V.tensor_scalar(tl(r1v, t, nr), tl(xnat, t, nr), rowsum[0:nr, bass.ds(t, 1)], None, ALU.mult)
            tile_pairs(dve, by_degree)
            stage_end(dve, "dve")
            s1 = sw["L1"]
            dve.sem_inc(s1["acc_free"], 1)
            for nr, ts in FULL:
                V.tensor_tensor(xnat[0:nr, ts], xnat[0:nr, ts], b1_bc[0:nr].unsqueeze(1).to_broadcast(
                    [nr, ts.stop - ts.start, D]), ALU.add)

            def chunk1(c, last):
                dve.wait_ge(s1["mm_done"], (c + 1) * T + 4)
                for r, nr in enumerate([P] * RPC if not last else [P, TAIL]):
                    t = c * RPC + r
                    ins = V.scalar_tensor_tensor(tl(raw1, t, nr), tl(xd, t, nr), dn[0:nr, bass.ds(t, 1)],
                                                 bank(0, 2)[0:nr, r * D:(r + 1) * D], ALU.mult, ALU.add)
                ins.then_inc(s1["acc_free"], 1)
            sweep_chunks(dve, chunk1)
            stage_end(dve, "dve")
            dve.sem_inc(h1_done, 2)

            def tile1(t, q, nr):
                dve.wait_ge(h1_mm, t + 3)
                link(V.scalar_tensor_tensor(tl(xnat, t, nr), bank(q)[0:nr, 0:D], rowsum[0:nr, bass.ds(t, 1)],
                                            tl(xnat, t, nr), ALU.mult, ALU.add))
                dve.sem_inc(h1_done, 1)
                link(stats(t, q, nr))
            tile_pairs(dve, tile1, (link, 2))
            dve_norm(dve, link, 1, False)
            stage_end(dve, "dve")
            for i, (heads, cf) in enumerate(((H2, C2), (H3, C3))):
                k = "L2" if i == 0 else "L3"
                s = sw[k]
                dve_project(dve, i + 1, proj, D + 2 * heads)
                stage_end(dve, "dve")
                own, oth = (0, heads) if i == 0 else (heads, 0)
                sm = lambda j: smalls[:, j, 0:heads * T].rearrange("p (h t) -> p h t", h=heads)
                for nr, ts in FULL:
                    V.tensor_copy(sm(0)[0:nr, :, ts], proj[0:nr, ts, D + oth:D + oth + heads].rearrange("p t h -> p h t"))
                    ins = V.tensor_copy(sm(2)[0:nr, :, ts],
                                        proj[0:nr, ts, D + own:D + own + heads].rearrange("p t h -> p h t"))
                link(ins)
                link(V.tensor_reduce(cpart[:, 0:heads], sm(0)[:, :, 0:T - 1], AX_X, ALU.max))
                V.tensor_tensor(cpart[0:TAIL, 0:heads], cpart[0:TAIL, 0:heads], sm(0)[0:TAIL, :, T - 1], ALU.max
                                ).then_inc(cm_in, 1)
                dve.wait_ge(cm_ok, i + 1)
                cb = cmax[:, 0:heads].unsqueeze(2).to_broadcast([P, heads, T])
                link(V.tensor_tensor(sm(0), sm(0), cb, ALU.subtract))
                V.tensor_scalar(sm(1), sm(0), SLOPE, None, ALU.mult)
                link(V.tensor_tensor(sm(2), sm(2), cb, ALU.add))
                V.tensor_scalar(sm(2), sm(2), -(1.0 - SLOPE), None, ALU.mult).then_inc(fg_in, 1)
                dve.wait_ge(fg_ok, i + 1)
                V.tensor_scalar(sm(3), sm(4), -1.0, None, ALU.mult).then_inc(neg_ok, 1)
                dve.wait_ge(neg_ok, i + 1)
                node_sum(dve, link, i)
                if i == 1:
                    for nr, ts in FULL:
                        V.tensor_tensor(xnat[0:nr, ts], xnat[0:nr, ts], b3_bc[0:nr].unsqueeze(1).to_broadcast(
                            [nr, ts.stop - ts.start, D]), ALU.add)
                if i == 1:
                    V.memset(stage_w.rearrange("p q m -> p (q m)"), 1.0)
                else:
                    for nr, ts in FULL:
                        V.tensor_scalar(dflag[0:nr, ts], dn[0:nr, ts], 1.0, 0.0, ALU.add, ALU.is_gt)
                    dve.sem_inc(s["mask_ok"], 4)
                    dve.sem_inc(den_out, 1)
                    dve.sem_inc(den_ps, 1)
                    dve.sem_inc(den_dve, 1)
                link(V.memset(cpart, 0.0))
                dve.sem_inc(s["acc_free"], 1)
                dve.sem_inc(s["p_ok"], 2 * heads)
                width = cf if i == 0 else cf + 1
                rawT = rawT2 if i == 0 else rawT3
                sv = stage_w.rearrange("p q (h m) -> p q h m", h=H3) if i == 1 else \
                    stage_w[:, :, 0:D].rearrange("p q (h m) -> p q h m", h=H2)

                def chunk(c, last):
                    def front(u):
                        if i == 0:
                            dve.wait_ge(s["blk_in"][u.slot], u.loaded)
                            m = msk[0:u.kp, u.q, 0:u.w]
                            ins = V.tensor_scalar(m, blk2[0:u.kp, u.slot].rearrange("p r n -> p (r n)")[:, 0:u.w], 0.0,
                                                  None, ALU.is_gt)
                            if u.diag is not None:
                                ins.then_inc(s["diag_ok"], 1)
                                dve.wait_ge(s["diag_ok"], c * 4 + u.diag + 1)
                                nr = u.rows[u.diag]
                                mb = m[:, u.diag * P:u.diag * P + nr]
                                ins = V.scalar_tensor_tensor(mb, ident[0:nr, 0:nr], dflag[0:nr, bass.ds(u.tile, 1)], mb,
                                                             ALU.mult, ALU.add)
                            ins.then_inc(s["mask_ok"], 1)

                    def step(u):
                        if i == 0:
                            dve.wait_ge(s["mask_ok"], u.n + 5)
                            dve.wait_ge(s["mm_done"], u.n + 1)
                            dve.wait_ge(den_pool, u.n + 1)
                        else:
                            dve.wait_ge(s["mask_ok"], u.n + 5)
                            dve.wait_ge(s["mm_done"], u.n + 1)
                            V.tensor_copy(sv[0:u.kp, u.q, :, 0:cf], proj[0:u.kp, bass.ds(u.tile, 1), 0:D].rearrange(
                                "p a (h c) -> p (a h) c", h=heads))
                        for h in range(heads):
                            dve.wait_ge(s["y_ok"], u.n * heads + h + 1)
                            V.scalar_tensor_tensor(PM[0:u.kp, u.q, h, 0:u.w], Y[0:u.kp, u.q, h, 0:u.w],
                                                   smalls[0:u.kp, 4, bass.ds(u.tile + h * T, 1)],
                                                   msk[0:u.kp, u.q, 0:u.w], ALU.add, ALU.mult).then_inc(s["p_ok"], 1)

                    def tail(u):
                        if i == 0:
                            dve.wait_ge(den_dve, u.n + 1)
                            dve.wait_ge(s["p_ok"], 2 * H2 + u.n * H2 + H2)
                            V.tensor_tensor(S2[0:u.kp, 1, 0:u.w], S2[0:u.kp, 1, 0:u.w], PM[0:u.kp, u.q, 1, 0:u.w],
                                            ALU.add).then_inc(den_dve, 1)
                    if i == 0:
                        dve.wait_ge(den_ps, c + 1)
                        V.memset(S2[:, 1, :], 0.0).then_inc(den_zero, 1)
                        dve.wait_ge(den_zero, c + 1)
                        settle(dve)
                    sweep_ahead(dve, c, last, front, step, tail)
                    dve.wait_ge(s["mm_done"], (c + 1) * T + 2)
                    w = WL if last else W
                    for h in range(heads):
                        ins = V.tensor_copy(rawT[0:width, h, bass.ds(c * W, w)], bank(h)[0:width, 0:w])
                    ins.then_inc(s["acc_free"], 1)
                    if i == 0:
                        dve.wait_ge(den_ps, c + 2)
                        empty(c, last, bank(4), H2, den2).then_inc(den_out, 1)
                sweep_chunks(dve, chunk)
                stage_end(dve, "dve")
                zz = smalls[:, 7, 0:heads * T].rearrange("p (t h) -> p t h", h=heads)
                dd = smalls[:, 3, 0:heads * T].rearrange("p (t h) -> p t h", h=heads)
                t4 = tmp.rearrange("p t (h c) -> p t h c", h=heads)
                u4 = tmp2.rearrange("p t (h c) -> p t h c", h=heads)
                if i == 0:
                    for nr, ts in FULL:
                        V.tensor_copy(dd[0:nr, ts], den2[0:nr, ts])
                        ins = V.tensor_scalar(zz[0:nr, ts], den2[0:nr, ts], 0.0, None, ALU.is_equal)
                    link(ins)
                for t in range(T):
                    nr = P if t < T - 1 else TAIL
                    b4 = bank(t % 4)[0:nr, 0:heads * width].rearrange("p (h c) -> p h c", h=heads)
                    dve.wait_ge(back_ps[i], t + 1)
                    if i == 1:
                        V.tensor_copy(dd[0:nr, t, :].unsqueeze(2), b4[:, :, cf:cf + 1])
                        ins = V.tensor_copy(t4[0:nr, t], b4[:, :, 0:cf])
                    else:
                        for h in range(heads):
                            ins = V.scalar_tensor_tensor(t4[0:nr, t, h], sum_bc[0:nr, h * cf:(h + 1) * cf],
                                                         zz[0:nr, t, h:h + 1], b4[:, h, 0:cf], ALU.mult, ALU.add)
                    ins.then_inc(back_ok[i], 1)
                dve.wait_ge(back_ok[i], T)
                for nr, ts in FULL:
                    nt = ts.stop - ts.start
                    if i == 1:
                        link(V.tensor_scalar(zz[0:nr, ts], dd[0:nr, ts], 0.0, None, ALU.is_equal))
                    link(V.scalar_tensor_tensor(dd[0:nr, ts], zz[0:nr, ts], float(N), dd[0:nr, ts], ALU.mult, ALU.add))
                    link(V.reciprocal(dd[0:nr, ts], dd[0:nr, ts]))
                    if i == 1:
                        for h in range(heads):
                            mb = sum_bc[0:nr, h * cf:(h + 1) * cf].unsqueeze(1).to_broadcast([nr, nt, cf])
                            ins = V.tensor_tensor(u4[0:nr, ts, h], zz[0:nr, ts, h].unsqueeze(2).to_broadcast([nr, nt, cf]),
                                                  mb, ALU.mult)
                        link(ins)
                        link(V.tensor_tensor(tmp[0:nr, ts], tmp[0:nr, ts], tmp2[0:nr, ts], ALU.add))
                    for h in range(heads):
                        ins = V.tensor_tensor(t4[0:nr, ts, h], t4[0:nr, ts, h],
                                              dd[0:nr, ts, h].unsqueeze(2).to_broadcast([nr, nt, cf]), ALU.mult)
                    link(ins)
                if i == 0:
                    dve.sem_inc(h2_made, 1)
                    dve.wait_ge(h2_back, 32)
                    for nr, ts in FULL:
                        ins = V.tensor_scalar(tmp2[0:nr, ts], tmp[0:nr, ts], 0.0, None, ALU.min)
                    ins.then_inc(elu_in, 1)
                    for nr, ts in FULL:
                        ins = V.scalar_tensor_tensor(xnat[0:nr, ts], tmp[0:nr, ts], 0.0, xnat[0:nr, ts], ALU.max, ALU.add)
                    link(ins)
                    dve.wait_ge(elu_ok, 1)
                    for nr, ts in FULL:
                        ins = V.scalar_tensor_tensor(xnat[0:nr, ts], tmp2[0:nr, ts], -1.0, xnat[0:nr, ts], ALU.add, ALU.add)
                else:
                    for nr, ts in FULL:
                        ins = V.tensor_tensor(xnat[0:nr, ts], xnat[0:nr, ts], tmp[0:nr, ts], ALU.add)
                link(ins)
                dve_norm(dve, link, 2 + i)
                stage_end(dve, "dve")


_OUT = (N, D)
_NAMES = ["x", "adj", "L0_gnn_gat_W", "L0_gnn_gat_a", "L0_gnn_edge_Wih", "L0_gnn_edge_Whh", "L0_gnn_edge_bih",
          "L0_gnn_edge_bhh", "L0_gnn_node_Wih", "L0_gnn_node_Whh", "L0_gnn_node_bih", "L0_gnn_node_bhh", "L1_gnn_W",
          "L1_gnn_b", "L2_gnn_W", "L2_gnn_a", "L3_gnn_W", "L3_gnn_a_src", "L3_gnn_a_dst", "L3_gnn_bias"]


def kernel(**inputs):
    import concourse.bacc as bacc
    from concourse.bass_utils import run_bass_kernel_spmd

    nc = bacc.Bacc("TRN2", target_bir_lowering=False, num_devices=1)
    arrays, args = {}, []
    for name in _NAMES:
        a = np.ascontiguousarray(inputs[name])
        arrays[f"in_{name}"] = a
        args.append(nc.dram_tensor(f"in_{name}", a.shape, mybir.dt.from_np(a.dtype), kind="ExternalInput").ap())
    args.append(nc.dram_tensor("out_x", _OUT, F32, kind="ExternalOutput").ap())
    build(nc, *args)
    r = run_bass_kernel_spmd(nc, [arrays], core_ids=[0])
    return r.results[0]["out_x"]
```
